# Optimizing a Trainium2 kernel written in Bass

```python
import numpy as np
import jax
import jax.numpy as jnp

def _softmax(x, axis=-1):
    return jax.nn.softmax(x, axis=axis)

def _gelu(x):
    return jax.nn.gelu(x, approximate=True)

def _silu(x):
    return jax.nn.silu(x)

def _sigmoid(x):
    return jax.nn.sigmoid(x)

def _layernorm(x, axis=-1, eps=1e-05):
    m = jnp.mean(x, axis=axis, keepdims=True)
    v = jnp.var(x, axis=axis, keepdims=True)
    return (x - m) / jnp.sqrt(v + eps)

def _scatter_add(tgt, idx, src, axis=0):
    return tgt.at[idx].add(src)

def _segment_sum(src, seg, n):
    return jax.ops.segment_sum(src, seg, n)
kernel_name = 'mk_gps_d2_gnn_r8_4cd360'

def setup_inputs(seed: int=0):
    np.random.seed(seed)
    _w = jnp.asarray

    def _rec_inputs():
        import jax
        import jax.numpy as jnp
        _gk = jax.random.key(seed)
        x = -8.776e-05 + 1 * jax.random.normal(jax.random.fold_in(_gk, 1), (1250, 512), jnp.float32)
        _s = jax.random.randint(jax.random.fold_in(_gk, 2), (20000,), 0, 1250, jnp.int32)
        _d = jax.random.randint(jax.random.fold_in(_gk, 3), (20000,), 0, 1250, jnp.int32)
        _loop = jnp.arange(1250, dtype=jnp.int32)
        src = jnp.concatenate([_s, _d, _loop])
        dst = jnp.concatenate([_d, _s, _loop])
        _o = jnp.argsort(dst, stable=True)
        src = src[_o]
        dst = dst[_o]
        return (x, src, dst)
    x, src, dst = _rec_inputs()

    def _L0_gnn_setup():
        import jax, jax.numpy as jnp
        import numpy as np
        N_NODES = 1250
        N_EDGES = 20000
        IN_DIM = 512
        OUT_DIM = 512
        LN_EPS = 1e-05
        key = jax.random.key(seed)
        k_x, k_src, k_ws, k_wn = jax.random.split(key, 4)
        x = jax.random.normal(k_x, (N_NODES, IN_DIM), dtype=jnp.float32)
        edge_src = jax.random.randint(k_src, (N_EDGES,), 0, N_NODES, dtype=jnp.int32)
        edge_dst = jnp.repeat(jnp.arange(N_NODES, dtype=jnp.int32), N_EDGES // N_NODES)
        deg = jnp.full((N_NODES,), float(N_EDGES // N_NODES), dtype=jnp.float32)
        scale = 1.0 / np.sqrt(IN_DIM)
        W_self = jax.random.normal(k_ws, (OUT_DIM, IN_DIM), dtype=jnp.float32) * scale
        W_neigh = jax.random.normal(k_wn, (OUT_DIM, IN_DIM), dtype=jnp.float32) * scale
        bias = jnp.zeros((OUT_DIM,), dtype=jnp.float32)
        gamma = jnp.ones((OUT_DIM,), dtype=jnp.float32)
        beta = jnp.zeros((OUT_DIM,), dtype=jnp.float32)
        return {'x': x, 'edge_src': edge_src, 'edge_dst': edge_dst, 'deg': deg, 'W_self': W_self, 'W_neigh': W_neigh, 'bias': bias, 'gamma': gamma, 'beta': beta}
    _L0_gnn_all = _L0_gnn_setup()
    _L0_gnn_in = {k: v for k, v in _L0_gnn_all.items() if k in ('W_self', 'W_neigh', 'bias', 'gamma', 'beta')}
    del _L0_gnn_all

    def _L0_mix_setup():
        import jax, jax.numpy as jnp
        import numpy as np
        NUM_HEADS = 8

        def _reference_tuple_inner(x, Wq, bq, Wk, bk, Wv, bv):
            R, C, E = x.shape
            H = NUM_HEADS
            D = E // H
            q = (x @ Wq.T + bq).reshape(R, C, H, D).transpose(0, 2, 1, 3)
            k = (x @ Wk.T + bk).reshape(R, C, H, D).transpose(0, 2, 1, 3)
            v = (x @ Wv.T + bv).reshape(R, C, H, D).transpose(0, 2, 1, 3)
            q = q.mean(axis=0)
            k = k.mean(axis=0)
            q = jax.nn.softmax(q, axis=-1) * D ** (-0.5)
            k = jax.nn.softmax(k, axis=-2)
            attn_weights = jnp.einsum('hnd,hmd->hnm', q, k)
            context = jnp.einsum('hnd,bhne->bhde', k, v)
            out = jnp.einsum('hnd,bhde->bhne', q, context)
            out = out.transpose(0, 2, 1, 3).reshape(R, C, E)
            return (out, attn_weights)
        key = jax.random.key(seed)
        ks = jax.random.split(key, 7)
        R, C, E = (64, 256, 512)
        x = jax.random.normal(ks[0], (R, C, E), dtype=jnp.float32)
        s = 0.02
        Wq = jax.random.normal(ks[1], (E, E), dtype=jnp.float32) * s
        bq = jax.random.normal(ks[2], (E,), dtype=jnp.float32) * s
        Wk = jax.random.normal(ks[3], (E, E), dtype=jnp.float32) * s
        bk = jax.random.normal(ks[4], (E,), dtype=jnp.float32) * s
        Wv = jax.random.normal(ks[5], (E, E), dtype=jnp.float32) * s
        bv = jax.random.normal(ks[6], (E,), dtype=jnp.float32) * s
        return {'x': x, 'Wq': Wq, 'bq': bq, 'Wk': Wk, 'bk': bk, 'Wv': Wv, 'bv': bv}
    _L0_mix_all = _L0_mix_setup()
    _L0_mix_in = {k: v for k, v in _L0_mix_all.items() if k in ('Wq', 'bq', 'Wk', 'bk', 'Wv', 'bv')}
    del _L0_mix_all

    def _L0_ffn_setup():
        import jax, jax.numpy as jnp
        import numpy as np
        DIM = 512
        FFN_DIM = 1408
        GROUP = 128
        EPS = 1e-05

        def _quantize_weight(w, group_size):
            o, i = w.shape
            wg = w.reshape(o, i // group_size, group_size)
            scale = jnp.mean(jnp.abs(wg), axis=-1, keepdims=True) + EPS
            wq = jnp.clip(jnp.round(wg / scale), -1.0, 1.0) * scale
            return wq.reshape(o, i)

        def _bitlinear(x, w, group_size=GROUP):
            wq = w + jax.lax.stop_gradient(_quantize_weight(w, group_size) - w)
            return jnp.einsum('bsd,fd->bsf', x, wq)
        key = jax.random.key(seed)
        k_x, k_g, k_u, k_d = jax.random.split(key, 4)
        x = jax.random.normal(k_x, (8, 512, DIM), dtype=jnp.float32)
        sd_in = 1.0 / np.sqrt(DIM)
        sd_ffn = 1.0 / np.sqrt(FFN_DIM)
        w_gate = jax.random.normal(k_g, (FFN_DIM, DIM), dtype=jnp.float32) * sd_in
        w_up = jax.random.normal(k_u, (FFN_DIM, DIM), dtype=jnp.float32) * sd_in
        w_down = jax.random.normal(k_d, (DIM, FFN_DIM), dtype=jnp.float32) * sd_ffn
        return {'x': x, 'w_gate': w_gate, 'w_up': w_up, 'w_down': w_down}
    _L0_ffn_all = _L0_ffn_setup()
    _L0_ffn_in = {k: v for k, v in _L0_ffn_all.items() if k in ('w_gate', 'w_up', 'w_down')}
    del _L0_ffn_all

    def _L1_gnn_setup():
        import jax, jax.numpy as jnp
        import numpy as np
        N_NODES = 6250
        N_EDGES = 100000
        D_IN = 512
        D_OUT = 512
        EPS = 1e-05
        key = jax.random.key(seed)
        k1, k2, k3, k4, k5 = jax.random.split(key, 5)
        x = jax.random.normal(k1, (N_NODES, D_IN), dtype=jnp.float32)
        edge_index = jax.random.randint(k2, (2, N_EDGES), 0, N_NODES, dtype=jnp.int64)
        s = 1.0 / np.sqrt(D_IN)
        W_l = jax.random.uniform(k3, (D_OUT, D_IN), jnp.float32, -s, s)
        b_l = jnp.zeros((D_OUT,), jnp.float32)
        W_r = jax.random.uniform(k4, (D_OUT, D_IN), jnp.float32, -s, s)
        gamma = jnp.ones((D_OUT,), jnp.float32)
        beta = jnp.zeros((D_OUT,), jnp.float32)
        return {'x': x, 'edge_index': edge_index, 'W_l': W_l, 'b_l': b_l, 'W_r': W_r, 'gamma': gamma, 'beta': beta}
    _L1_gnn_all = _L1_gnn_setup()
    _L1_gnn_in = {k: v for k, v in _L1_gnn_all.items() if k in ('W_l', 'b_l', 'W_r', 'gamma', 'beta')}
    del _L1_gnn_all

    def _L1_mix_setup():
        import jax, jax.numpy as jnp
        import numpy as np
        DIM, HEADS, NB_FEATURES = (512, 8, 64)
        HEAD_DIM = DIM // HEADS

        def _phi(t, proj_mat):
            return jax.nn.elu(jnp.einsum('bnhd,hdf->bnhf', t, proj_mat)) + 1.0
        key = jax.random.key(seed)
        k_x, k_qkv, k_pm, k_wp, k_bp = jax.random.split(key, 5)
        B, N = (8, 512)
        x = jax.random.normal(k_x, (B, N, DIM), dtype=jnp.float32)
        w_qkv = jax.random.normal(k_qkv, (DIM, 3 * DIM), dtype=jnp.float32) * (1.0 / np.sqrt(DIM))
        proj_mat = jax.random.normal(k_pm, (HEADS, HEAD_DIM, NB_FEATURES), dtype=jnp.float32)
        w_proj = jax.random.normal(k_wp, (DIM, DIM), dtype=jnp.float32) * (1.0 / np.sqrt(DIM))
        b_proj = jax.random.normal(k_bp, (DIM,), dtype=jnp.float32) * 0.01
        return {'x': x, 'w_qkv': w_qkv, 'proj_mat': proj_mat, 'w_proj': w_proj, 'b_proj': b_proj}
    _L1_mix_all = _L1_mix_setup()
    _L1_mix_in = {k: v for k, v in _L1_mix_all.items() if k in ('w_qkv', 'proj_mat', 'w_proj', 'b_proj')}
    del _L1_mix_all

    def _L1_ffn_setup():
        import jax, jax.numpy as jnp
        import numpy as np
        MIN_EXPERT_CAPACITY = 4
        EPS = 1e-09
        CAPACITY_FACTOR = 2.0

        def cumsum_exclusive(t, axis):
            return jnp.cumsum(t, axis=axis) - t

        def safe_one_hot(idx, depth):
            return jax.nn.one_hot(idx, depth + 1)[..., :depth]

        def top2_gating(x, w_gating):
            b, n, d = x.shape
            e = w_gating.shape[-1]
            raw_gates = jax.nn.softmax(jnp.einsum('bnd,de->bne', x, w_gating), axis=-1)
            gate_1 = jnp.max(raw_gates, axis=-1)
            index_1 = jnp.argmax(raw_gates, axis=-1)
            mask_1 = jax.nn.one_hot(index_1, e, dtype=raw_gates.dtype)
            gates_without_top1 = raw_gates * (1.0 - mask_1)
            gate_2 = jnp.max(gates_without_top1, axis=-1)
            index_2 = jnp.argmax(gates_without_top1, axis=-1)
            mask_2 = jax.nn.one_hot(index_2, e, dtype=raw_gates.dtype)
            denom = gate_1 + gate_2 + EPS
            gate_1 = gate_1 / denom
            gate_2 = gate_2 / denom
            density_1 = jnp.mean(mask_1, axis=-2)
            density_1_proxy = jnp.mean(raw_gates, axis=-2)
            loss = jnp.mean(density_1_proxy * density_1) * float(e * e)
            capacity = max(min(n, int(n * 2 * CAPACITY_FACTOR / e)), MIN_EXPERT_CAPACITY)
            cap_f = float(capacity)
            pos1 = cumsum_exclusive(mask_1, axis=-2) * mask_1
            mask_1 = mask_1 * (pos1 < cap_f).astype(mask_1.dtype)
            mask_1_count = jnp.sum(mask_1, axis=-2, keepdims=True)
            mask_1_flat = jnp.sum(mask_1, axis=-1)
            pos1 = jnp.sum(pos1, axis=-1)
            gate_1 = gate_1 * mask_1_flat
            pos2 = (cumsum_exclusive(mask_2, axis=-2) + mask_1_count) * mask_2
            mask_2 = mask_2 * (pos2 < cap_f).astype(mask_2.dtype)
            mask_2_flat = jnp.sum(mask_2, axis=-1)
            pos2 = jnp.sum(pos2, axis=-1)
            gate_2 = gate_2 * mask_2_flat
            combine = gate_1[..., None, None] * mask_1_flat[..., None, None] * jax.nn.one_hot(index_1, e, dtype=x.dtype)[..., None] * safe_one_hot(pos1.astype(jnp.int32), capacity)[..., None, :] + gate_2[..., None, None] * mask_2_flat[..., None, None] * jax.nn.one_hot(index_2, e, dtype=x.dtype)[..., None] * safe_one_hot(pos2.astype(jnp.int32), capacity)[..., None, :]
            dispatch = (combine > 0).astype(combine.dtype)
            return (dispatch, combine, loss)
        key = jax.random.key(seed)
        k_x, k_g, k_w1, k_w2 = jax.random.split(key, 4)
        b, n, d, e, h = (2, 512, 512, 16, 256)
        x = jax.random.normal(k_x, (b, n, d), dtype=jnp.float32)
        w_gating = jax.random.normal(k_g, (d, e), dtype=jnp.float32) / np.sqrt(d)
        w1 = jax.random.normal(k_w1, (e, d, h), dtype=jnp.float32) / np.sqrt(d)
        w2 = jax.random.normal(k_w2, (e, h, d), dtype=jnp.float32) / np.sqrt(h)
        return {'x': x, 'w_gating': w_gating, 'w1': w1, 'w2': w2}
    _L1_ffn_all = _L1_ffn_setup()
    _L1_ffn_in = {k: v for k, v in _L1_ffn_all.items() if k in ('w_gating', 'w1', 'w2')}
    del _L1_ffn_all
    return {'x': x, 'src': src, 'dst': dst, 'L0_gnn_W_self': _L0_gnn_in['W_self'], 'L0_gnn_W_neigh': _L0_gnn_in['W_neigh'], 'L0_gnn_bias': _L0_gnn_in['bias'], 'L0_gnn_gamma': _L0_gnn_in['gamma'], 'L0_gnn_beta': _L0_gnn_in['beta'], 'L0_mix_Wq': _L0_mix_in['Wq'], 'L0_mix_bq': _L0_mix_in['bq'], 'L0_mix_Wk': _L0_mix_in['Wk'], 'L0_mix_bk': _L0_mix_in['bk'], 'L0_mix_Wv': _L0_mix_in['Wv'], 'L0_mix_bv': _L0_mix_in['bv'], 'L0_ffn_w_gate': _L0_ffn_in['w_gate'], 'L0_ffn_w_up': _L0_ffn_in['w_up'], 'L0_ffn_w_down': _L0_ffn_in['w_down'], 'L1_gnn_W_l': _L1_gnn_in['W_l'], 'L1_gnn_b_l': _L1_gnn_in['b_l'], 'L1_gnn_W_r': _L1_gnn_in['W_r'], 'L1_gnn_gamma': _L1_gnn_in['gamma'], 'L1_gnn_beta': _L1_gnn_in['beta'], 'L1_mix_w_qkv': _L1_mix_in['w_qkv'], 'L1_mix_proj_mat': _L1_mix_in['proj_mat'], 'L1_mix_w_proj': _L1_mix_in['w_proj'], 'L1_mix_b_proj': _L1_mix_in['b_proj'], 'L1_ffn_w_gating': _L1_ffn_in['w_gating'], 'L1_ffn_w1': _L1_ffn_in['w1'], 'L1_ffn_w2': _L1_ffn_in['w2']}

def reference(x, src, dst, L0_gnn_W_self, L0_gnn_W_neigh, L0_gnn_bias, L0_gnn_gamma, L0_gnn_beta, L0_mix_Wq, L0_mix_bq, L0_mix_Wk, L0_mix_bk, L0_mix_Wv, L0_mix_bv, L0_ffn_w_gate, L0_ffn_w_up, L0_ffn_w_down, L1_gnn_W_l, L1_gnn_b_l, L1_gnn_W_r, L1_gnn_gamma, L1_gnn_beta, L1_mix_w_qkv, L1_mix_proj_mat, L1_mix_w_proj, L1_mix_b_proj, L1_ffn_w_gating, L1_ffn_w1, L1_ffn_w2):
    import jax
    import jax.numpy as jnp

    def _L0_gnn_ref(x, edge_src, edge_dst, deg, W_self, W_neigh, bias, gamma, beta):
        import jax, jax.numpy as jnp
        import numpy as np
        N_NODES = 1250
        N_EDGES = 20000
        IN_DIM = 512
        OUT_DIM = 512
        LN_EPS = 1e-05
        n = x.shape[0]
        h_self = jnp.einsum('nd,od->no', x, W_self)
        neigh_sum = jax.ops.segment_sum(x[edge_src], edge_dst, num_segments=n)
        neigh_mean = neigh_sum / jnp.maximum(deg, 1.0)[:, None]
        h_neigh = jnp.einsum('nd,od->no', neigh_mean, W_neigh)
        h = h_self + h_neigh + bias
        mu = jnp.mean(h, axis=-1, keepdims=True)
        var = jnp.mean(jnp.square(h - mu), axis=-1, keepdims=True)
        h = (h - mu) * jax.lax.rsqrt(var + LN_EPS)
        return h * gamma + beta

    def _L0_mix_ref(x, Wq, bq, Wk, bk, Wv, bv):
        import jax, jax.numpy as jnp
        import numpy as np
        NUM_HEADS = 8

        def _reference_tuple_inner(x, Wq, bq, Wk, bk, Wv, bv):
            R, C, E = x.shape
            H = NUM_HEADS
            D = E // H
            q = (x @ Wq.T + bq).reshape(R, C, H, D).transpose(0, 2, 1, 3)
            k = (x @ Wk.T + bk).reshape(R, C, H, D).transpose(0, 2, 1, 3)
            v = (x @ Wv.T + bv).reshape(R, C, H, D).transpose(0, 2, 1, 3)
            q = q.mean(axis=0)
            k = k.mean(axis=0)
            q = jax.nn.softmax(q, axis=-1) * D ** (-0.5)
            k = jax.nn.softmax(k, axis=-2)
            attn_weights = jnp.einsum('hnd,hmd->hnm', q, k)
            context = jnp.einsum('hnd,bhne->bhde', k, v)
            out = jnp.einsum('hnd,bhde->bhne', q, context)
            out = out.transpose(0, 2, 1, 3).reshape(R, C, E)
            return (out, attn_weights)
        return _reference_tuple_inner(x, Wq, bq, Wk, bk, Wv, bv)[0]

    def _L0_ffn_ref(x, w_gate, w_up, w_down):
        import jax, jax.numpy as jnp
        import numpy as np
        DIM = 512
        FFN_DIM = 1408
        GROUP = 128
        EPS = 1e-05

        def _quantize_weight(w, group_size):
            o, i = w.shape
            wg = w.reshape(o, i // group_size, group_size)
            scale = jnp.mean(jnp.abs(wg), axis=-1, keepdims=True) + EPS
            wq = jnp.clip(jnp.round(wg / scale), -1.0, 1.0) * scale
            return wq.reshape(o, i)

        def _bitlinear(x, w, group_size=GROUP):
            wq = w + jax.lax.stop_gradient(_quantize_weight(w, group_size) - w)
            return jnp.einsum('bsd,fd->bsf', x, wq)
        gate = _bitlinear(x, w_gate)
        up = _bitlinear(x, w_up)
        h = jax.nn.silu(gate) * up
        return _bitlinear(h, w_down)

    def _L1_gnn_ref(x, edge_index, W_l, b_l, W_r, gamma, beta):
        import jax, jax.numpy as jnp
        import numpy as np
        N_NODES = 6250
        N_EDGES = 100000
        D_IN = 512
        D_OUT = 512
        EPS = 1e-05
        N = x.shape[0]
        src = edge_index[0]
        dst = edge_index[1]
        agg = jax.ops.segment_sum(x[src], dst, num_segments=N)
        deg = jax.ops.segment_sum(jnp.ones_like(dst, jnp.float32), dst, num_segments=N)
        mean_nb = agg / jnp.maximum(deg, 1.0)[:, None]
        h = mean_nb @ W_l.T + b_l + x @ W_r.T
        h = jax.nn.relu(h)
        mu = jnp.mean(h, axis=0)
        var = jnp.mean((h - mu) ** 2, axis=0)
        out = (h - mu) * jax.lax.rsqrt(var + EPS) * gamma + beta
        return out

    def _L1_mix_ref(x, w_qkv, proj_mat, w_proj, b_proj):
        import jax, jax.numpy as jnp
        import numpy as np
        DIM, HEADS, NB_FEATURES = (512, 8, 64)
        HEAD_DIM = DIM // HEADS

        def _phi(t, proj_mat):
            return jax.nn.elu(jnp.einsum('bnhd,hdf->bnhf', t, proj_mat)) + 1.0
        B, N, dim = x.shape
        H, D = (HEADS, dim // HEADS)
        qkv = x @ w_qkv
        q, k, v = jnp.split(qkv, 3, axis=-1)
        q = q.reshape(B, N, H, D)
        k = k.reshape(B, N, H, D)
        v = v.reshape(B, N, H, D)
        q_phi = _phi(q, proj_mat)
        k_phi = _phi(k, proj_mat)
        kv = jnp.einsum('bnhf,bnhd->bhfd', k_phi, v)
        z = 1.0 / jnp.einsum('bnhf,bhf->bnh', q_phi, k_phi.sum(axis=1))
        out = jnp.einsum('bnhf,bhfd,bnh->bnhd', q_phi, kv, z)
        out = out.reshape(B, N, H * D)
        return out @ w_proj + b_proj

    def _L1_ffn_ref(x, w_gating, w1, w2):
        import jax, jax.numpy as jnp
        import numpy as np
        MIN_EXPERT_CAPACITY = 4
        EPS = 1e-09
        CAPACITY_FACTOR = 2.0

        def cumsum_exclusive(t, axis):
            return jnp.cumsum(t, axis=axis) - t

        def safe_one_hot(idx, depth):
            return jax.nn.one_hot(idx, depth + 1)[..., :depth]

        def top2_gating(x, w_gating):
            b, n, d = x.shape
            e = w_gating.shape[-1]
            raw_gates = jax.nn.softmax(jnp.einsum('bnd,de->bne', x, w_gating), axis=-1)
            gate_1 = jnp.max(raw_gates, axis=-1)
            index_1 = jnp.argmax(raw_gates, axis=-1)
            mask_1 = jax.nn.one_hot(index_1, e, dtype=raw_gates.dtype)
            gates_without_top1 = raw_gates * (1.0 - mask_1)
            gate_2 = jnp.max(gates_without_top1, axis=-1)
            index_2 = jnp.argmax(gates_without_top1, axis=-1)
            mask_2 = jax.nn.one_hot(index_2, e, dtype=raw_gates.dtype)
            denom = gate_1 + gate_2 + EPS
            gate_1 = gate_1 / denom
            gate_2 = gate_2 / denom
            density_1 = jnp.mean(mask_1, axis=-2)
            density_1_proxy = jnp.mean(raw_gates, axis=-2)
            loss = jnp.mean(density_1_proxy * density_1) * float(e * e)
            capacity = max(min(n, int(n * 2 * CAPACITY_FACTOR / e)), MIN_EXPERT_CAPACITY)
            cap_f = float(capacity)
            pos1 = cumsum_exclusive(mask_1, axis=-2) * mask_1
            mask_1 = mask_1 * (pos1 < cap_f).astype(mask_1.dtype)
            mask_1_count = jnp.sum(mask_1, axis=-2, keepdims=True)
            mask_1_flat = jnp.sum(mask_1, axis=-1)
            pos1 = jnp.sum(pos1, axis=-1)
            gate_1 = gate_1 * mask_1_flat
            pos2 = (cumsum_exclusive(mask_2, axis=-2) + mask_1_count) * mask_2
            mask_2 = mask_2 * (pos2 < cap_f).astype(mask_2.dtype)
            mask_2_flat = jnp.sum(mask_2, axis=-1)
            pos2 = jnp.sum(pos2, axis=-1)
            gate_2 = gate_2 * mask_2_flat
            combine = gate_1[..., None, None] * mask_1_flat[..., None, None] * jax.nn.one_hot(index_1, e, dtype=x.dtype)[..., None] * safe_one_hot(pos1.astype(jnp.int32), capacity)[..., None, :] + gate_2[..., None, None] * mask_2_flat[..., None, None] * jax.nn.one_hot(index_2, e, dtype=x.dtype)[..., None] * safe_one_hot(pos2.astype(jnp.int32), capacity)[..., None, :]
            dispatch = (combine > 0).astype(combine.dtype)
            return (dispatch, combine, loss)
        dispatch, combine, loss = top2_gating(x, w_gating)
        expert_inputs = jnp.einsum('bnd,bnec->ebcd', x, dispatch)
        hidden = jax.nn.relu(jnp.einsum('ebcd,edh->ebch', expert_inputs, w1))
        expert_outputs = jnp.einsum('ebch,ehd->ebcd', hidden, w2)
        output = jnp.einsum('ebcd,bnec->bnd', expert_outputs, combine)
        return output
    edge_index = jnp.stack([src, dst])
    deg = jnp.maximum(jax.ops.segment_sum(jnp.ones(dst.shape, jnp.float32), dst, num_segments=1250), 1.0)
    xn = _layernorm(x, axis=-1)
    x = x + _L0_gnn_ref(xn, src, dst, deg, L0_gnn_W_self, L0_gnn_W_neigh, L0_gnn_bias, L0_gnn_gamma, L0_gnn_beta) + _L0_mix_ref(xn[None], L0_mix_Wq, L0_mix_bq, L0_mix_Wk, L0_mix_bk, L0_mix_Wv, L0_mix_bv)[0]
    x = x + _L0_ffn_ref(_layernorm(x, axis=-1)[None], L0_ffn_w_gate, L0_ffn_w_up, L0_ffn_w_down)[0]
    xn = _layernorm(x, axis=-1)
    x = x + _L1_gnn_ref(xn, edge_index, L1_gnn_W_l, L1_gnn_b_l, L1_gnn_W_r, L1_gnn_gamma, L1_gnn_beta) + _L1_mix_ref(xn[None], L1_mix_w_qkv, L1_mix_proj_mat, L1_mix_w_proj, L1_mix_b_proj)[0]
    x = x + _L1_ffn_ref(_layernorm(x, axis=-1)[None], L1_ffn_w_gating, L1_ffn_w1, L1_ffn_w2)[0]
    return x

_drawn_inputs = setup_inputs


def setup_inputs(seed=0):
    import zlib

    import numpy as np

    out = dict(_drawn_inputs(seed))
    spreads = {'L0_gnn_bias': (0.0, 0.1),
     'L0_gnn_gamma': (1.0, 0.2),
     'L0_gnn_beta': (0.0, 0.1),
     'L1_gnn_b_l': (0.0, 0.1),
     'L1_gnn_gamma': (1.0, 0.2),
     'L1_gnn_beta': (0.0, 0.1)}
    factors = {'L0_mix_Wq': 8.0,
     'L0_mix_bq': 25.392,
     'L0_mix_Wk': 8.0,
     'L0_mix_bk': 64.0,
     'L0_mix_Wv': 5.514,
     'L0_mix_bv': 6.303,
     'L1_mix_proj_mat': 2.86,
     'L1_mix_b_proj': 3.229}
    for name, (base, spread) in spreads.items():
        noise = np.random.default_rng([zlib.crc32(name.encode()), seed]).standard_normal(out[name].shape)
        drawn = base * np.exp(spread * noise) if base else spread * noise
        out[name] = jnp.asarray(drawn.astype(out[name].dtype))
    for name, factor in factors.items():
        out[name] = (out[name] * factor).astype(out[name].dtype)
    return out
```

```python
from contextlib import ExitStack, contextmanager

import concourse.bass as bass
from concourse import mybir

F32, F16, I32 = mybir.dt.float32, mybir.dt.float16, mybir.dt.int32
ALU, ACT, AX = mybir.AluOpType, mybir.ActivationFunctionType, mybir.AxisListType
ds = bass.ds

N, D, E = 1250, 512, 41250
TP, NT = 125, 10
KT = D // 128
CHUNKS = [(0, 418), (418, 416), (834, 416)]
H, DH = 8, 64
FFN, FT = 1408, 11
NE, HID, CAP = 16, 256, 312
CT = CAP // 3
SLOTS = NE * CAP
A_SCALE, W_SCALE = 16.0, 64.0
UNSCALE = 1.0 / (A_SCALE * W_SCALE)
EPS = 1e-5
PASSES = [(0, 0), (0, 1), (1, 0)]

EC, ER = 128, E // 128
NCH = 384
SEG = 12
RING = 4
BASE = 4096.0
HS = N // 2
HW = 314
ONE_COL = 626
FAR = 2048.0


class Own:

    def __init__(self, eng, sem):
        self.eng, self.sem, self.base, self.k = eng, sem, 0, 0

    def mark(self, ins):
        ins.then_inc(self.sem, 1)
        self.k += 1
        return self.base + self.k

    def after(self, mark):
        self.eng.wait_ge(self.sem, mark)

    def step(self, ins):
        self.after(self.mark(ins))

    @contextmanager
    def loop(self, count, marks):
        base = self.base + self.k
        with self.eng.Fori(0, count) as i:
            self.base, self.k = i * marks + base, 0
            yield i
            assert self.k == marks, (self.k, marks)
        self.base, self.k = base + count * marks, 0


class Banks:

    def __init__(self, full, free):
        self.full, self.free, self.before, self.uses, self.count = full, free, {}, {}, [0] * 8

    def stage(self, name, uses):
        self.before[name], self.uses[name] = list(self.count), uses
        for b, n in uses.items():
            self.count[b] += n

    def acquire(self, eng, stage, b, k):
        eng.wait_ge(self.free[b], k + (self.before[stage][b] + 1))

    def filled(self, eng, stage, b, k):
        eng.wait_ge(self.full[b], k + (self.before[stage][b] + 1))

    def emptied(self, eng, stage, b, k):
        eng.wait_ge(self.free[b], k + (self.before[stage][b] + 2))

    def after_products(self, eng, stage):
        for b, n in self.uses[stage].items():
            eng.wait_ge(self.full[b], self.before[stage][b] + n)

    def after_evacuation(self, eng, stage):
        for b, n in self.uses[stage].items():
            eng.wait_ge(self.free[b], self.before[stage][b] + n + 1)


def gps_two_layers(nc, t, out):
    ctx = ExitStack()
    with ctx:
        top = nc.sbuf_base + 31
        top -= top % 32
        start = {}

        def region(name, size):
            nonlocal top
            start[name] = top
            top += size + (-size) % 32
            assert top <= nc.sbuf_usable_end, (name, top)

        def at(name, shape, dt, where, offset=0):
            return nc.alloc_sbuf_tensor_at(name, shape, dt, offset=start[where] + offset)

        for name, size in (("X", 20480), ("XN", 20480), ("XK", 20480), ("MT", 20480), ("XT", 20480),
                           ("AT", 50016), ("W", 24576), ("STG", 16384), ("BC", 12288), ("C", 7168)):
            region(name, size)
        X = at("X", [TP, NT, D], F32, "X")
        XN = at("XN", [TP, NT, D], F32, "XN")
        XK = at("XK", [TP, 2, NT, D], F16, "XK")
        XT = at("XT", [128, 2, KT, N], F16, "XT")
        MT = at("MT", [128, 2, KT, N], F16, "MT")
        AT = at("AT", [TP, 2, NT, N], F16, "AT")
        W = [at(f"W{s}", [128, 2, 2048], F16, "W", 8192 * s) for s in range(3)]
        STG = [at(f"STG{s}", [128, 2048], F32, "STG", 8192 * s) for s in range(2)]

        def rows(s):
            return W[s][:, :, :].rearrange("p a (k o) -> p a k o", k=KT)

        BC = at("BC", [TP, 6, D], F32, "BC")
        BQ, BV, BIAS, GAMMA, BETA, BPROJ = (BC[:, n, :] for n in range(6))
        QT = at("QT", [128, KT, N], F32, "XN")
        V = at("V", [TP, NT, D], F32, "MT")
        EKT = at("EKT", [128, KT, N], F32, "AT")
        EK = at("EK", [TP, NT, D], F32, "AT", 20000)
        QW = at("QW", [TP, 2, D], F32, "AT", 40512)
        CTX = at("CTX", [128, KT, 128], F32, "AT", 44608)
        IDX = at("IDX", [128, 2, 3, EC], I32, "AT", 46656)
        IDXF = at("IDXF", [128, 2, 3, EC], F32, "MT")
        SRC, SRCV, DST = (at(n, [128, NCH], F32, "MT", 3072 + 1536 * k) for k, n in enumerate(("SRC", "SRCV", "DST")))
        DREL = at("DREL", [128, 2, NCH], F32, "MT", 7680)
        I2 = at("I2", [TP, 2, 2, HW], I32, "MT", 10752)
        TMP = at("TMP", [128, 3, EC], F32, "MT", 15776 + 32)
        ONEHOT_S = at("ONEHOT_S", [128, RING, 2 * HW], F16, "XN")
        ONEHOT_D = at("ONEHOT_D", [128, RING, 128], F16, "XN", 5056)
        ACC = [at(f"ACC{n}", [TP, 2, 2 * HW], F32, "XN", 6080 + 5024 * n) for n in range(2)]
        ACCI = [at(f"ACCI{n}", [TP, 2, 2 * HW], I32, "XN", 6080 + 5024 * n) for n in range(2)]
        RANGE = at("RANGE", [128, 2, 3, NT, 3], F32, "XN", 16128)
        LH = at("LH", [TP, 2, 2 * HW], I32, "W", 16384)
        DG = at("DG", [128, N], F32, "XN")
        DIAG = at("DIAG", [TP, NT, TP], F32, "XN", 5024)
        MTMP = at("MTMP", [128, 2, 3, 418], F32, "XN", 10048)
        STEPS = at("STEPS", [1, NT, 32], F32, "XN", 17504)
        HT = at("HT", [128, 2, FT, N], F16, "XN")
        GATED = at("GATED", [128, 3, 418], F32, "XN", 55008)
        WD = at("WD", [128, 2, FT, D], F16, "W")
        GU = at("GU", [128, 2, 2, 2, KT * 128], F16, "BC")
        MAG = at("MAG", [128, 3, 512], F32, "AT", 25024)
        TERN = at("TERN", [128, 3, 512], F16, "AT", 31168)
        QUANT = at("QUANT", [128, 2, 3, 512], F32, "AT", 34240)
        G = at("G", [128, KT, N], F32, "AT")
        QP = at("QP", [128, KT, N], F32, "AT", 20000)
        PTMP = at("PTMP", [128, 3, 418], F32, "AT", 40000)
        OW = at("OW", [TP, 2, D], F32, "AT", 45024)
        QF = at("QF", [128, KT, N], F32, "XK")
        KF = at("KF", [128, KT, N], F32, "MT")
        KP = at("KP", [TP, NT, D], F32, "XK")
        V1 = at("V1", [TP, NT, D], F32, "XN")
        PB = at("PB", [128, KT, 128], F32, "BC")
        KVB = at("KVB", [128, KT, 128], F32, "BC", 2048)
        ZB = at("ZB", [128, KT, 2], F32, "BC", 4096)
        IDNS = at("IDNS", [128, 128], F32, "BC", 4128)
        WG = at("WG", [128, KT * NE], F32, "BC", 4640)
        WGS = at("WGS", [128, 2, KT, NE], F16, "BC", 4896)
        GSTATS = at("GSTATS", [128, KT, 3, 6], F32, "BC", 5152)
        GMV = at("GMV", [128, KT, 2], F32, "BC", 5440)
        GCOL = at("GCOL", [128, 4, KT], F32, "BC", 5472)
        ZERO = at("ZERO", [128, 512], F32, "MT")
        XET = at("XET", [128, 2, 2, KT, CAP], F16, "XK")
        XE = at("XE", [CT, 2, 3, D], F32, "MT")
        HTMP = at("HTMP", [128, 2, 2 * CAP], F32, "AT")
        HH = at("HH", [128, 2, 2, 2, CAP], F16, "AT", 4992)
        EO = at("EO", [CT, 2, 3, D], F32, "AT", 9984)
        GATHER = at("GATHER", [TP, 4, D], F32, "AT", 22272)
        ROUTE = at("ROUTE", [TP, 12, NT, NE], F32, "AT", 30464)
        CARRY = at("CARRY", [TP, NT + 1, 2 * NE], F32, "AT", 38144)
        MASK = at("MASK", [TP, NT, 2, NE], F16, "AT", 39584)
        TOK = at("TOK", [TP, 12, NT], F32, "AT", 40224)
        SIDX = at("SIDX", [TP, 2, NT], I32, "AT", 40736)
        GIDX = at("GIDX", [TP, 2, NT], I32, "AT", 40832)
        EBASE = at("EBASE", [TP, 2, NE], F32, "AT", 40928)
        DUMP = at("DUMP", [TP, 2, NT], F32, "AT", 41088)
        slots_in = nc.dram_tensor("slots_in", [SLOTS + 2 * N, D], F32).ap()
        slots_out = nc.dram_tensor("slots_out", [SLOTS, D], F32).ap()
        counts_low_kept = nc.dram_tensor("counts_low_kept", [TP, NT, N], F16).ap()
        used = [0]

        def small(name, shape, dt):
            size = mybir.dt.size(dt) if hasattr(mybir.dt, "size") else {F32: 4, F16: 2, I32: 4}[dt]
            for n in shape[1:]:
                size *= n
            x = at(name, shape, dt, "C", used[0])
            used[0] += size + (-size) % 32
            assert used[0] <= 7168, name
            return x

        IDN = small("IDN", [128, 128], F32)
        ONES = small("ONES", [128, 128], F32)
        ONES16 = small("ONES16", [128, 128], F16)
        TRI16 = small("TRI16", [128, 128], F16)
        IOTA_S = small("IOTA_S", [128, ONE_COL], F16)
        IOTA_D = small("IOTA_D", [128, 128], F16)
        STATS = small("STATS", [TP, NT, 6], F32)
        MV = small("MV", [TP, NT, 2], F32)
        STD = small("STD", [TP, NT], F32)
        RSTD = small("RSTD", [TP, NT], F32)
        SM8 = small("SM8", [TP, 2, 3, H], F32)
        COL = small("COL", [128, 8, KT], F32)
        KSUM3 = small("KSUM3", [128, KT, 3], F32)
        KMX = small("KMX", [128, 3], F32)
        BK, BL, G1, B1, KMAX, KBIAS, KSUM, KREC = (COL[:, n, :] for n in range(8))
        DEG = small("DEG", [TP, NT], F32)
        RDEG = small("RDEG", [TP, NT], F32)
        THR = small("THR", [128, NT], F32)
        CID = small("CID", [128, 2, 3], F32)
        RED = small("RED", [128, 2, 3], F32)
        LOHI = small("LOHI", [128, 2, NT], F32)
        LOHIR = small("LOHIR", [128, 2, NT], F32)
        PLAN = small("PLAN", [1, 3, NT + 1], F32)
        MULT = small("MULT", [1, 32], F32)
        PLANI = small("PLANI", [1, 3, NT + 1], I32)
        EPSC = small("EPSC", [128, 1], F32)
        EPSW = small("EPSW", [128, 1], F32)
        PS = ctx.enter_context(nc.psum_tensor("PS", [128, 8, 512], F32))
        B = [PS[:, b, :] for b in range(8)]

        def sem(name):
            return ctx.enter_context(nc.semaphore(name))

        bank_full = [sem(f"bank{b}_full") for b in range(8)]
        bank_free = [sem(f"bank{b}_free") for b in range(8)]
        bk = Banks(bank_full, bank_free)
        stages = [
            ("ln0_T", {0: 5, 1: 5}), ("mix_q", {2: 5, 3: 5}), ("mix_qT", {4: 5, 5: 5}),
            ("mix_k", {0: 2, 1: 2, 6: 2, 7: 2, 4: 2, 5: 2}), ("mix_kT", {2: 5, 3: 5}),
            ("mix_v", {0: 5, 1: 5}), ("mix_ctx", {2: 1}), ("mix_out", {3: 5, 4: 5}),
            ("edges", {0: 1, 1: 1}), ("counts_T", {0: 10, 1: 10, 2: 10}),
            ("deg0", {0: 1, 1: 1, 2: 1}), ("agg0", {b: 2 for b in range(6)}), ("gnn0", {6: 5, 7: 5}),
            ("ln1_T", {0: 5, 1: 5}), ("ffn_scale", {6: 2 * FT, 7: FT}), ("ffn", {b: FT for b in range(6)}),
            ("down", {6: 5, 7: 5}), ("ln2_T", {2: 5, 3: 5}), ("deg1", {0: 1, 1: 1, 2: 1}), ("agg1", {b: 2 for b in range(6)}),
            ("gnn1", {b: 2 for b in range(6)}), ("qk1", {b: 4 for b in range(6)}), ("v1", {6: 5, 7: 5}),
            ("phi_q", {b: 2 for b in range(6)}), ("phi_k", {6: 5, 7: 5}), ("kv", {0: 1, 1: 1}), ("att", {2: 5, 3: 5}),
            ("z", {4: 5, 5: 5}), ("att_T", {6: 5, 7: 5}), ("proj", {0: 5, 1: 5}), ("ln3_T", {2: 5, 3: 5}),
            ("gate", {4: 1}), ("places", {5: 1, 6: 1}), ("slots_T", {0: NE, 1: NE, 2: NE}), ("hidden", {3: NE, 4: NE}),
            ("expert", {5: NE, 6: NE, 7: NE}),
        ]
        for s in stages:
            bk.stage(*s)
        x_loaded = [sem(f"x_loaded{n}") for n in range(2)]
        small_loaded = sem("small_loaded")
        consts_made = sem("consts_made")
        staged = [sem(f"staged{s}") for s in range(2)]
        high_split = sem("high_split")
        weight_ready = sem("weight_ready")
        stored = sem("stored")
        dve_own, act_own, pool_own = sem("dve_own"), sem("act_own"), sem("pool_own")
        std_ready, xn_ready, xk_high, xk_low, xt_high = (
            sem("std_ready"), sem("xn_ready"), sem("xk_high"), sem("xk_low"), sem("xt_high"))
        var_ready = sem("var_ready")
        q_shifted, q_exp, q_soft = sem("q_shifted"), sem("q_exp"), sem("q_soft")
        kbias_ready = sem("kbias_ready")
        ctx_ready = sem("ctx_ready")
        edges_loaded, edges_float = sem("edges_loaded"), sem("edges_float")
        lohi_local, lohi_all, plan_ready = sem("lohi_local"), sem("lohi_all"), sem("plan_ready")
        dve_free = sem("dve_free")
        onehot_ready, onehot_free = sem("onehot_ready"), sem("onehot_free")
        seg_int, lohi_ready, acc_added = sem("seg_int"), sem("lohi_ready"), sem("acc_added")
        counts_high, deg_ready, diag_ready = sem("counts_high"), sem("deg_ready"), sem("diag_ready")
        mean_raw, mean_high, mean_ready = sem("mean_raw"), sem("mean_high"), sem("mean_ready")
        x1_ready = sem("x1_ready")
        beta_added, gnn_var, gnn_std = sem("beta_added"), sem("gnn_var"), sem("gnn_std")

        qkv = t["L1_mix_w_qkv"]
        units = [t["L0_mix_WqT"], t["L0_mix_WkT"], t["L0_mix_WvT"], t["L0_gnn_W_selfT"], t["L0_gnn_W_neighT"],
                 t["L1_gnn_W_lT"], t["L1_gnn_W_rT"], qkv[:, 0:D], qkv[:, D:2 * D], qkv[:, 2 * D:], t["L1_mix_w_proj"]]
        NU = len(units)
        unit_slot = [0, 1, 2, 0, 1, 0, 1, 2, 0, 1, 2]
        last_use = {3: "mix_q", 4: "mix_k", 5: "down", 6: "down", 7: "down", 8: "gnn1", 9: "gnn1", 10: "qk1"}

        def stage_slot(n):
            return n % 2 if n < 5 else (n + 1) % 2

        def staged_count(n):
            return 16 * sum(stage_slot(m) == stage_slot(n) for m in range(min(n, NU) + 1)) if n < NU else None

        def plan(eng, T):
            lo = eng.value_load(PLANI[0:1, 0, T:T + 1], min_val=0, max_val=ER)
            n = eng.value_load(PLANI[0:1, 1, T:T + 1], min_val=1, max_val=(ER + SEG) // SEG + 1)
            before = eng.value_load(PLANI[0:1, 2, T:T + 1], min_val=0, max_val=NT * ((ER + SEG) // SEG + 1))
            return lo, n, before

        ffn_staged = [sem(f"ffn_staged{n}") for n in range(2)]
        magnitude, scales, ternary, quantised, ffn_high, ffn_low = (
            sem(n) for n in ("magnitude", "scales", "ternary", "quantised", "ffn_high", "ffn_low"))
        gate_silu, hidden_high, counts_spilled, counts_back, wide_own = (
            sem(n) for n in ("gate_silu", "hidden_high", "counts_spilled", "counts_back", "wide_own"))
        gnn1_var, gnn1_std, gnn1_done, phi_min, phi_exp, kmin, kexp, att_ready, bproj_added = (
            sem(n) for n in ("gnn1_var", "gnn1_std", "gnn1_done", "phi_min", "phi_exp", "kmin", "kexp", "att_ready", "bproj_added"))
        route_loaded, route_consts, wg_high, wg_ready, gate_exp_in, gate_exp, masks_ready, places_ready = (
            sem(n) for n in ("route_loaded", "route_consts", "wg_high", "wg_ready", "gate_exp_in", "gate_exp", "masks_ready", "places_ready"))
        zero_made, zero_stored, scattered, slots_high, relu_made, relu_high, relu_low = (
            sem(n) for n in ("zero_made", "zero_stored", "scattered", "slots_high", "relu_made", "relu_high", "relu_low"))
        slots_loaded = [sem(f"slots_loaded{n}") for n in range(2)]
        outs_stored = [sem(f"outs_stored{n}") for n in range(2)]
        gathered = [sem(f"gathered{n}") for n in range(4)]
        half_added, y_ready = sem("half_added"), sem("y_ready")

        prescaled, expert_prescaled = sem("prescaled"), sem("expert_prescaled")
        hidden_done = sem("hidden_done")

        def expert_staged(e, par):
            slot = (par + NU + 1) % 2
            return 16 * sum(stage_slot(m) == slot for m in range(NU)) + 32 * (e // 2 + 1)

        def stored_count(e, par):
            return 16 * (e // 2)

        block = ctx.enter_context(nc.Block())

        @block.sync
        def _(sp):
            for n in range(2):
                sp.dma_start(X[:, 5 * n:5 * n + 5, :], t["x"].rearrange("(t p) d -> p t d", p=TP)[:, 5 * n:5 * n + 5, :])\
                  .then_inc(x_loaded[n], 16)
            for dst, name in ((BQ, "L0_mix_bq"), (BV, "L0_mix_bv"), (BIAS, "L0_gnn_bias"), (GAMMA, "L0_gnn_gamma"),
                              (BETA, "L0_gnn_beta"), (BPROJ, "L1_mix_b_proj")):
                sp.dma_start(dst, t[name].partition_broadcast(TP)).then_inc(small_loaded, 16)
            for dst, name in ((BK, "L0_mix_bkC"), (BL, "L1_gnn_b_lC"), (G1, "L1_gnn_gammaC"), (B1, "L1_gnn_betaC")):
                sp.dma_start(dst, t[name]).then_inc(small_loaded, 16)
            sp.wait_ge(edges_loaded, 1)
            for a, name in enumerate(("src", "dst")):
                e = t[name]
                sp.dma_start(IDX[:, a, 0:2, :], e[0:256 * EC].rearrange("(g p e) -> p g e", p=128, e=EC)).then_inc(edges_loaded, 16)
                sp.dma_start(IDX[0:ER - 256, a, 2, :], e[256 * EC:ER * EC].rearrange("(p e) -> p e", e=EC)).then_inc(edges_loaded, 16)
                sp.dma_start(IDX[ER - 256:ER - 255, a, 2, 0:E - ER * EC], e[ER * EC:E].rearrange("(p e) -> p e", p=1)).then_inc(edges_loaded, 16)
            sp.wait_ge(zero_made, 1)
            sp.dma_start(slots_in[0:SLOTS, :].rearrange("(p r) d -> p r d", p=128),
                         ZERO[:, :].unsqueeze(1).to_broadcast([128, SLOTS // 128, D])).then_inc(zero_stored, 16)

            def load_weight(n):
                sl = stage_slot(n)
                sp.dma_start(STG[sl][:, :].rearrange("p (k o) -> p k o", k=KT), units[n].rearrange("(k p) o -> p k o", p=128))\
                  .then_inc(staged[sl], 16)

            for n in range(5):
                if n >= 2:
                    sp.wait_ge(weight_ready, n - 1)
                load_weight(n)
            wide = [t[x].rearrange("(k p) f -> p k f", p=128) for x in ("L0_ffn_w_gateT", "L0_ffn_w_upT")]
            for n in range(FT):
                if n == 2:
                    bk.after_evacuation(sp, "counts_T")
                    sp.dma_start(counts_low_kept, AT[:, 1, :, :]).then_inc(counts_spilled, 16)
                if n < 2:
                    sp.wait_ge(weight_ready, 4 + n)
                else:
                    sp.wait_ge(ternary, n - 1)
                st = STG[(n + 1) % 2]
                for a in range(2):
                    sp.dma_start(st[:, a * 512:(a + 1) * 512].rearrange("p (k f) -> p k f", k=KT), wide[a][:, :, n * 128:(n + 1) * 128])\
                      .then_inc(ffn_staged[n % 2], 16)
                sp.dma_start(st[:, 1024:1536], t["L0_ffn_w_downT"][n * 128:(n + 1) * 128, :]).then_inc(ffn_staged[n % 2], 16)
            for n in (5, 6):
                sp.wait_ge(ternary, FT - 1 + n - 5)
                load_weight(n)
            bk.after_products(sp, "ffn")
            sp.wait_ge(ffn_low, FT)
            sp.dma_start(AT[:, 1, :, :], counts_low_kept).then_inc(counts_back, 16)
            sp.dma_start(WG[:, :].rearrange("p (k e) -> p k e", k=KT), t["L1_ffn_w_gating"].rearrange("(k p) e -> p k e", p=128)).then_inc(route_loaded, 16)
            sp.wait_ge(wide_own, 1)
            for h in range(H):
                p = slice(64 * (h % 2), 64 * (h % 2) + 64)
                sp.dma_start(PB[p, h // 2, p], t["L1_mix_proj_mat"][h, :, :]).then_inc(route_loaded, 16)
            for n in range(7, NU):
                sp.wait_ge(weight_ready, n - 1)
                load_weight(n)

            def load_expert(e, par):
                st = STG[(par + NU + 1) % 2]
                sp.wait_ge(weight_ready, e + (NU - 1))
                sp.dma_start(st[:, 0:1024].rearrange("p (k h) -> p k h", k=KT), t["L1_ffn_w1"][ds(e, 1), :, :].rearrange("a (k p) h -> p (a k) h", p=128))\
                  .then_inc(staged[(par + NU + 1) % 2], 16)
                sp.dma_start(st[:, 1024:2048].rearrange("p (k d) -> p k d", k=2), t["L1_ffn_w2"][ds(e, 1), :, :].rearrange("a (k p) d -> p (a k) d", p=128))\
                  .then_inc(staged[(par + NU + 1) % 2], 16)

            def load_slots(e, par):
                if not isinstance(e, int):
                    bk.filled(sp, "slots_T", 2, e - 2)
                sp.dma_start(XE[:, par, :, :], slots_in[ds(e * CAP, CAP), :].rearrange("(c p) d -> p c d", p=CT)).then_inc(slots_loaded[par], 16)

            def store_slots(e, par):
                bk.emptied(sp, "expert", 7, e)
                sp.dma_start(slots_out[ds(e * CAP, CAP), :].rearrange("(c p) d -> p c d", p=CT), EO[:, par, :, :]).then_inc(outs_stored[par], 16)

            for par in range(2):
                load_expert(par, par)
            sp.wait_ge(scattered, 16 * 2 * NT)
            for par in range(2):
                load_slots(par, par)
            with sp.Fori(0, NE // 2 - 1) as i:
                for par in range(2):
                    load_expert(i * 2 + (par + 2), par)
                    load_slots(i * 2 + (par + 2), par)
                    store_slots(i * 2 + par, par)
            for par in range(2):
                store_slots(NE - 2 + par, par)
            for i in range(NT):
                sp.wait_ge(y_ready, i + 1)
                sp.dma_start(out[i * TP:(i + 1) * TP, :], X[:, i, :]).then_inc(stored, 16)
            sp.wait_ge(stored, 16 * NT)

        @block.gpsimd
        def _(pool):
            g = nc.gpsimd
            own = Own(pool, pool_own)
            g.memset(IDX[:, :, 2, :], -1).then_inc(edges_loaded, 1)
            g.memset(ZERO[:, :], 0.0).then_inc(zero_made, 1)
            own.step(g.memset(IDN[:, :], 0.0))
            g.affine_select(out=IDN[:, :], in_=IDN[:, :], compare_op=ALU.not_equal, fill=1.0, base=0,
                            pattern=[[-1, 128]], channel_multiplier=1).then_inc(consts_made, 1)
            g.memset(ONES[:, :], 1.0).then_inc(consts_made, 1)
            g.memset(ONES16[:, :], 1.0).then_inc(consts_made, 1)
            pool.wait_ge(consts_made, 3)
            g.affine_select(out=TRI16[:, :], in_=ONES16[:, :], compare_op=ALU.is_gt, fill=0.0, base=0,
                            pattern=[[1, 128]], channel_multiplier=-1).then_inc(consts_made, 1)
            g.iota(IOTA_S[:, :], [[1, ONE_COL]], base=0, channel_multiplier=0, allow_small_or_imprecise_dtypes=True)\
             .then_inc(consts_made, 1)
            g.iota(IOTA_D[:, :], [[1, 128]], base=0, channel_multiplier=0, allow_small_or_imprecise_dtypes=True)\
             .then_inc(consts_made, 1)
            g.memset(EPSC[:, :], EPS).then_inc(consts_made, 1)
            g.memset(EPSW[:, :], EPS * W_SCALE).then_inc(consts_made, 1)
            g.iota(MULT[:, :], [[SEG, 32]], base=0, channel_multiplier=0, allow_small_or_imprecise_dtypes=True).then_inc(consts_made, 1)
            g.iota(THR[:, :], [[TP, NT]], base=0, channel_multiplier=0, allow_small_or_imprecise_dtypes=True).then_inc(consts_made, 1)
            g.iota(CID[:, 0, :], [[-128, 3]], base=512, channel_multiplier=-1, allow_small_or_imprecise_dtypes=True).then_inc(consts_made, 1)
            g.iota(CID[:, 1, :], [[128, 3]], base=1, channel_multiplier=1, allow_small_or_imprecise_dtypes=True).then_inc(consts_made, 1)

            def prescale(n):
                st = STG[stage_slot(n)]
                pool.wait_ge(staged[stage_slot(n)], staged_count(n))
                g.tensor_scalar(st[:, :], st[:, :], W_SCALE, 1.0, ALU.mult, ALU.mult).then_inc(prescaled, 1)

            def split_low(n):
                prescale(n)
                pool.wait_ge(high_split, n + 1)
                w = W[unit_slot[n]]
                g.tensor_tensor(w[:, 1, :], STG[stage_slot(n)][:, :], w[:, 0, :], ALU.subtract)\
                 .then_inc(weight_ready, 1)

            def keep_low(done):
                with pool.Fori(0, NT) as i:
                    pool.wait_ge(xk_high, i + (done + 1))
                    g.tensor_tensor(XK[:, 1, ds(i, 1), :], XN[:, ds(i, 1), :], XK[:, 0, ds(i, 1), :], ALU.subtract).then_inc(xk_low, 1)

            split_low(0)
            keep_low(0)
            split_low(1)
            for n in (2, 3, 4):
                split_low(n)
            bk.after_evacuation(pool, "mix_out")
            with pool.Fori(0, NT) as i:
                g.tensor_tensor(X[:, ds(i, 1), :], X[:, ds(i, 1), :], BETA.unsqueeze(1), ALU.add).then_inc(beta_added, 1)
            pool.wait_ge(lohi_local, 1)
            g.partition_all_reduce(LOHIR[:, :, :].rearrange("p a t -> p (a t)"), LOHI[:, :, :].rearrange("p a t -> p (a t)"), 128,
                                   bass.bass_isa.ReduceOp.max).then_inc(lohi_all, 1)
            pool.wait_ge(plan_ready, 1)
            pool.sem_inc(acc_added, 2)
            for T in range(NT):
                _, n, before = plan(pool, T)
                acc = ACCI[T % 2]
                if T >= 2:
                    bk.filled(pool, "counts_T", 2, T - 2)
                own.step(g.memset(acc[:, :, :], 0))
                with pool.Fori(0, n) as i:
                    pool.wait_ge(lohi_ready, before + i + 3)
                    pool.wait_ge(acc_added, before + i + 2)
                    g.tensor_tensor(acc[:, :, :], acc[:, :, :], LH[:, :, :], ALU.add).then_inc(acc_added, 1)
                pool.wait_ge(acc_added, before + n + 2)
                ones = acc[:, :, ONE_COL:ONE_COL + 1]
                own.step(g.tensor_tensor(ones[:, 0, :], ones[:, 0, :], ones[:, 1, :], ALU.add))
                own.step(g.tensor_copy(DEG[:, T:T + 1], ones[:, 0, :]))
                g.tensor_copy(ACC[T % 2][:, :, :], acc[:, :, :]).then_inc(deg_ready, 1)

            def quantise(n, par):
                pool.wait_ge(ternary, n + 1)
                g.tensor_tensor(QUANT[:, par, :, :], TERN[:, :, :], QUANT[:, par, :, :], ALU.mult)\
                 .then_inc(quantised, 1)

            def quantised_low(n, par):
                pool.wait_ge(ffn_high, n * 2 + 2)
                own.mark(g.tensor_tensor(GU[:, par, :, 1, :], QUANT[:, par, 0:2, :], GU[:, par, :, 0, :], ALU.subtract))
                g.tensor_tensor(WD[:, 1, ds(n, 1), :], QUANT[:, par, 2:3, :], WD[:, 0, ds(n, 1), :], ALU.subtract).then_inc(ffn_low, 1)

            quantise(0, 0)
            quantise(1, 1)
            quantised_low(0, 0)
            with own.loop(4, 2) as i:
                for u in range(2):
                    quantised_low(i * 2 + (u + 1), 1 - u)
                    quantise(i * 2 + (u + 2), u)
            quantised_low(9, 1)
            quantise(10, 0)
            quantised_low(10, 0)

            split_low(5)
            split_low(6)
            bk.after_products(pool, "ffn")
            own.step(g.memset(IDNS[:, :], 0.0))
            own.mark(g.affine_select(out=IDNS[:, :], in_=IDNS[:, :], compare_op=ALU.not_equal, fill=A_SCALE * W_SCALE, base=0,
                                     pattern=[[-1, 128]], channel_multiplier=1))
            own.mark(g.memset(ZB[:, :, :], 0.0))
            own.step(g.memset(KVB[:, :, :], 0.0))
            g.memset(PB[:, :, :], 0.0).then_inc(wide_own, 1)
            keep_low(NT)
            pool.wait_ge(xn_ready, 3 * NT)
            with pool.Fori(0, NT) as i:
                g.tensor_tensor(X[:, ds(i, 1), :], X[:, ds(i, 1), :], BPROJ.unsqueeze(1), ALU.add).then_inc(bproj_added, 1)
            for n in range(7, NU):
                split_low(n)
            bk.after_products(pool, "proj")
            g.iota(EBASE[:, 0, :], [[CAP, NE]], base=0, channel_multiplier=0, allow_small_or_imprecise_dtypes=True).then_inc(route_consts, 1)
            g.iota(EBASE[:, 1, :], [[-1, NE]], base=NE, channel_multiplier=0, allow_small_or_imprecise_dtypes=True).then_inc(route_consts, 1)
            g.iota(DUMP[:, :, :], [[1, 2], [2 * TP, NT]], base=SLOTS, channel_multiplier=2, allow_small_or_imprecise_dtypes=True).then_inc(route_consts, 1)

            def expert_low(e, par):
                pool.wait_ge(high_split, e + (NU + 1))
                g.tensor_tensor(W[par][:, 1, :], STG[(par + NU + 1) % 2][:, :], W[par][:, 0, :], ALU.subtract)\
                 .then_inc(weight_ready, 1)

            expert_low(0, 0)
            expert_low(1, 1)
            pool.wait_ge(places_ready, 2)
            pool.wait_ge(zero_stored, 16)
            for i in range(NT):
                for c in range(2):
                    g.indirect_dma_start(out=slots_in, out_offset=bass.IndirectOffsetOnAxis(ap=SIDX[:, c, i:i + 1], axis=0),
                                         in_=XN[:, i, :], in_offset=None).then_inc(scattered, 16)
            with pool.Fori(0, NE // 2 - 1) as i:
                for u in range(2):
                    expert_low(i * 2 + (u + 2), u)
            for u in range(2):
                pool.wait_ge(outs_stored[u], 16 * (NE // 2))
            for n in range(2 * NT):
                if n >= 4:
                    pool.wait_ge(half_added if n % 2 == 0 else y_ready, (n - 4) // 2 + 1)
                g.indirect_dma_start(out=GATHER[:, n % 4, :], out_offset=None, in_=slots_out,
                                     in_offset=bass.IndirectOffsetOnAxis(ap=GIDX[:, n % 2, n // 2:n // 2 + 1], axis=0))\
                 .then_inc(gathered[n % 4], 16)

        @block.scalar
        def _(act):
            s = nc.scalar
            own = Own(act, act_own)

            def split_high(n):
                act.wait_ge(prescaled, n + 1)
                if n in last_use:
                    bk.after_products(act, last_use[n])
                s.activation(W[unit_slot[n]][:, 0, :], STG[stage_slot(n)][:, :], ACT.Copy).then_inc(high_split, 1)

            def norm_parts(stage, banks, done, std_done, keep):
                act.wait_ge(var_ready, std_done + 1)
                if std_done == 0:
                    act.wait_ge(consts_made, 12)
                s.activation(STD[:, :], MV[:, :, 1], ACT.Sqrt, bias=EPSC[:TP, :]).then_inc(std_ready, 1)
                with act.Fori(0, NT // 2) as i:
                    for u in range(2):
                        if keep:
                            act.wait_ge(xn_ready, i * 2 + (done + u + 1))
                            s.activation(XK[:, 0, ds(i * 2 + u, 1), :], XN[:, ds(i * 2 + u, 1), :], ACT.Copy).then_inc(xk_high, 1)
                        bk.filled(act, stage, banks[u], i)
                        s.activation(XT[:, 0, :, ds(i * (2 * TP) + u * TP, TP)],
                                     B[banks[u]][:, 0:KT * TP].rearrange("p (k n) -> p k n", k=KT), ACT.Copy).then_inc(xt_high, 1)

            split_high(0)
            norm_parts("ln0_T", (0, 1), 0, 0, True)
            split_high(1)
            split_high(2)

            act.wait_ge(xk_low, NT)
            with act.Fori(0, NT // 2) as i:
                for u in range(2):
                    act.wait_ge(q_shifted, i * 2 + (u + 1))
                    s.activation(QW[:, u, :], QW[:, u, :], ACT.Exp).then_inc(q_exp, 1)
                for u in range(2):
                    bk.filled(act, "mix_qT", 4 + u, i)
                    s.activation(QT[:, :, ds(i * (2 * TP) + u * TP, TP)],
                                 B[4 + u][:, 0:KT * TP].rearrange("p (k n) -> p k n", k=KT), ACT.Copy)\
                     .then_inc(bank_free[4 + u], 1)
            split_high(3)
            for m in range(KT):
                act.wait_ge(kbias_ready, m + 1)
                for c, (lo, n) in enumerate(CHUNKS):
                    b = (0, 1, 6, 7, 4, 5)[3 * (m % 2) + c]
                    s.activation(EKT[:, m, lo:lo + n], B[b][:, 0:n], ACT.Exp, bias=KBIAS[:, m:m + 1], scale=UNSCALE,
                                 accum_out=KSUM3[:, m, c:c + 1]).then_inc(bank_free[b], 1)
            split_high(4)
            with act.Fori(0, NT // 2) as i:
                for u in range(2):
                    bk.filled(act, "mix_kT", 2 + u, i)
                    s.activation(EK[:, ds(i * 2 + u, 1), :], B[2 + u][:TP, :].rearrange("p (a n) -> p a n", a=1), ACT.Copy)\
                     .then_inc(bank_free[2 + u], 1)

            def counts_high_part(T):
                for b in range(3):
                    n = min(4, NT - 4 * b)
                    bk.filled(act, "counts_T", b, T)
                    s.activation(AT[:, 0, 4 * b:4 * b + n, T * TP:(T + 1) * TP], B[b][:TP, 0:n * TP].rearrange("p (s d) -> p s d", s=n),
                                 ACT.Copy).then_inc(counts_high, 1)

            act.wait_ge(plan_ready, 1)
            bk.after_evacuation(act, "mix_out")
            for T in range(NT):
                _, n, before = plan(act, T)
                with act.Fori(0, n) as i:
                    act.wait_ge(onehot_free, (before + i) * SEG + (SEG + RING))
                    act.wait_ge(lohi_ready, before + i + 1)
                    s.activation(I2[:, ds((before + i) % 2, 1), :, :].rearrange("p a h c -> p (a h) c"),
                                 PS[:TP, ds((before + i) % 2 * 2 + 4, 2), 0:HW], ACT.Copy).then_inc(seg_int, 1)
                if T:
                    counts_high_part(T - 1)
            counts_high_part(NT - 1)

            def means_high(stage):
                with act.Fori(0, KT // 2) as i:
                    for u in range(2):
                        for c, (lo, n) in enumerate(CHUNKS):
                            bk.emptied(act, stage, 3 * u + c, i)
                            s.activation(MT[:, 0, ds(i * 2 + u, 1), lo:lo + n], MTMP[:, u, c:c + 1, 0:n], ACT.Copy)\
                             .then_inc(mean_high, 1)

            means_high("agg0")
            act.wait_ge(gnn_var, 1)
            s.activation(STD[:, :], MV[:, :, 1], ACT.Sqrt, bias=EPSC[:TP, :]).then_inc(gnn_std, 1)

            norm_parts("ln1_T", (0, 1), NT, 1, False)

            def magnitudes(n, par):
                if not (isinstance(n, int) and n == 0):
                    act.wait_ge(ternary, n)
                act.wait_ge(ffn_staged[par], (n // 2) * 48 + 48 if isinstance(n, int) else n)
                s.activation(MAG[:, :, :].rearrange("p a c -> p (a c)"), STG[(par + 1) % 2][:, 0:1536], ACT.Abs).then_inc(magnitude, 1)

            def scale_rows(n, par):
                for a in range(3):
                    b = (6, 7, 6)[a]
                    bk.filled(act, "ffn_scale", b, n * 2 + (a // 2) if b == 6 else n)
                    if a == 0 and not (isinstance(n, int) and n < 2):
                        act.wait_ge(ffn_low, n - 1)
                    s.activation(QUANT[:, par, a, :], B[b][:, :], ACT.Identity, bias=EPSW[:, :], scale=W_SCALE / 128)\
                     .then_inc(bank_free[b], 1)

            def quantised_high(n, par):
                act.wait_ge(quantised, n + 1)
                s.activation(GU[:, par, :, 0, :], QUANT[:, par, 0:2, :], ACT.Copy).then_inc(ffn_high, 1)
                s.activation(WD[:, 0, ds(n, 1), :], QUANT[:, par, 2:3, :], ACT.Copy).then_inc(ffn_high, 1)

            def gates(j):
                for c, (lo, n) in enumerate(CHUNKS):
                    bk.filled(act, "ffn", c, j)
                    if not (isinstance(j, int) and j == 0):
                        act.wait_ge(hidden_done, j * 3 + (c + 1 - 3))
                    s.activation(GATED[:, c, 0:n], B[c][:, 0:n], ACT.Silu, scale=UNSCALE).then_inc(bank_free[c], 1)
                for c, (lo, n) in enumerate(CHUNKS):
                    bk.emptied(act, "ffn", 3 + c, j)
                    s.activation(HT[:, 0, ds(j, 1), lo:lo + n], GATED[:, c:c + 1, 0:n], ACT.Copy).then_inc(hidden_high, 1)

            act.wait_ge(counts_spilled, 16)
            magnitudes(0, 0)
            scale_rows(0, 0)
            magnitudes(1, 1)
            scale_rows(1, 1)
            quantised_high(0, 0)
            quantised_high(1, 1)
            magnitudes(2, 0)
            for j in range(FT):
                if j + 2 < FT:
                    scale_rows(j + 2, j % 2)
                if j + 3 < FT:
                    magnitudes(j + 3, (j + 1) % 2)
                gates(j)
                if j + 2 < FT:
                    quantised_high(j + 2, j % 2)

            split_high(5)
            split_high(6)
            norm_parts("ln2_T", (2, 3), 2 * NT, 2, True)
            means_high("agg1")
            split_high(7)
            for m in range(KT):
                for c, (lo, n) in enumerate(CHUNKS):
                    b = 3 * (m % 2) + c
                    bk.filled(act, "gnn1", b, m // 2)
                    s.activation(G[:, m, lo:lo + n], B[b][:, 0:n], ACT.Relu, bias=BL[:, m:m + 1], scale=UNSCALE).then_inc(bank_free[b], 1)
            split_high(8)
            split_high(9)
            act.wait_ge(gnn1_var, 1)
            s.activation(GCOL[:, 0, :], GMV[:, :, 1], ACT.Sqrt, bias=EPSC[:, :]).then_inc(gnn1_std, 1)
            for m in range(2 * KT):
                for c, (lo, n) in enumerate(CHUNKS):
                    b = 3 * (m % 2) + c
                    bk.filled(act, "qk1", b, m // 2)
                    s.activation((QF if m < KT else KF)[:, m % KT, lo:lo + n], B[b][:, 0:n], ACT.Copy, scale=UNSCALE)\
                     .then_inc(bank_free[b], 1)
            split_high(10)
            for m in range(KT):
                for c, (lo, n) in enumerate(CHUNKS):
                    act.wait_ge(phi_min, 3 * m + c + 1)
                    s.activation(PTMP[:, c, 0:n], PTMP[:, c, 0:n], ACT.Exp).then_inc(phi_exp, 1)
            with act.Fori(0, NT // 2) as i:
                for u in range(2):
                    act.wait_ge(kmin, i * 2 + (u + 1))
                    s.activation(OW[:, u, :], OW[:, u, :], ACT.Exp).then_inc(kexp, 1)

            def parts_T(stage, banks):
                with act.Fori(0, NT // 2) as i:
                    for u in range(2):
                        bk.filled(act, stage, banks[u], i)
                        s.activation(XT[:, 0, :, ds(i * (2 * TP) + u * TP, TP)],
                                     B[banks[u]][:, 0:KT * TP].rearrange("p (k n) -> p k n", k=KT), ACT.Copy,
                                     scale=A_SCALE).then_inc(xt_high, 1)

            parts_T("att_T", (6, 7))
            act.wait_ge(route_loaded, 16)
            s.activation(WGS[:, 0, :, :].rearrange("p k e -> p (k e)"), WG[:, :], ACT.Copy, scale=W_SCALE).then_inc(wg_high, 1)

            def expert_high(e, par):
                act.wait_ge(expert_prescaled, e + 1)
                if isinstance(e, int) and e < 2:
                    bk.after_products(act, "v1")
                else:
                    for b in (5, 6, 7):
                        bk.filled(act, "expert", b, e - 2)
                s.activation(W[par][:, 0, :], STG[(par + NU + 1) % 2][:, :], ACT.Copy).then_inc(high_split, 1)

            expert_high(0, 0)
            expert_high(1, 1)
            norm_parts("ln3_T", (2, 3), 3 * NT, 3, False)
            act.wait_ge(gate_exp_in, 1)
            s.activation(ROUTE[:, 0, :, :], ROUTE[:, 0, :, :], ACT.Exp).then_inc(gate_exp, 1)

            def slots_high_parts(e, par):
                for b in range(3):
                    bk.filled(act, "slots_T", b, e)
                    s.activation(XET[:, par, 0, :, b * CT:(b + 1) * CT], B[b][:, 0:KT * CT].rearrange("p (k n) -> p k n", k=KT),
                                 ACT.Copy).then_inc(slots_high, 1)

            def relus(e, par):
                for m in range(2):
                    bk.filled(act, "hidden", 3 + m, e)
                    s.activation(HTMP[:, par, m * CAP:(m + 1) * CAP], B[3 + m][:, 0:CAP], ACT.Relu, scale=UNSCALE * A_SCALE)\
                     .then_inc(bank_free[3 + m], 1)
                for m in range(2):
                    bk.emptied(act, "hidden", 3 + m, e)
                s.activation(HH[:, par, 0, :, :].rearrange("p m c -> p (m c)"), HTMP[:, par, :], ACT.Copy).then_inc(relu_high, 1)

            def first_out(e, par):
                bk.filled(act, "expert", 5, e)
                if not (isinstance(e, int) and e < 2):
                    act.wait_ge(outs_stored[par], stored_count(e, par))
                s.activation(EO[:, par, 0, :], B[5][:CT, :], ACT.Copy, scale=UNSCALE).then_inc(bank_free[5], 1)

            slots_high_parts(0, 0)
            for e in range(NE):
                relus(e, e % 2)
                if e + 1 < NE:
                    slots_high_parts(e + 1, (e + 1) % 2)
                first_out(e, e % 2)
                if e + 2 < NE:
                    expert_high(e + 2, e % 2)

        @block.tensor
        def _(pe):
            te = nc.tensor
            for b in range(8):
                pe.sem_inc(bank_free[b], 1)
            pe.wait_ge(consts_made, 12)

            def sum_products(dst, pairs):
                for n, (a, b) in enumerate(pairs):
                    last = te.matmul(dst, a, b, start=(n == 0), stop=(n == len(pairs) - 1))
                return last

            def normed_T(stage, banks, done):
                for i in range(NT):
                    pe.wait_ge(xn_ready, done + i + 1)
                    bk.acquire(pe, stage, banks[i % 2], i // 2)
                    for k in range(KT):
                        last = te.transpose(B[banks[i % 2]][:, k * TP:(k + 1) * TP], XN[:, i, k * 128:(k + 1) * 128],
                                            IDN[:TP, :TP])
                    last.then_inc(bank_full[banks[i % 2]], 1)

            def by_token(stage, banks, terms, weights_done=0):
                with pe.Fori(0, NT // 2) as i:
                    for u in range(2):
                        bk.acquire(pe, stage, banks[u], i)
                        sum_products(B[banks[u]][:TP, :], [
                            (a[:, pa, k, ds(i * (2 * TP) + u * TP, TP)], w[:, pw, k, :])
                            for a, w, kt in terms for k in range(kt) for pa, pw in PASSES
                        ]).then_inc(bank_full[banks[u]], 1)

            def by_feature(stage, banks, m, terms, use):
                for c, (lo, n) in enumerate(CHUNKS):
                    bk.acquire(pe, stage, banks[c], use)
                    sum_products(B[banks[c]][:, 0:n], [
                        (w[:, pw, k, m * 128:(m + 1) * 128], a[:, pa, k, lo:lo + n])
                        for a, w in terms for k in range(KT) for pw, pa in PASSES
                    ]).then_inc(bank_full[banks[c]], 1)

            normed_T("ln0_T", (0, 1), 0)
            bk.after_evacuation(pe, "ln0_T")
            pe.wait_ge(weight_ready, 1)
            def q_transposes(i):
                for u in range(2):
                    tt = 2 * i + u
                    pe.wait_ge(q_soft, tt + 1)
                    bk.acquire(pe, "mix_qT", 4 + u, i)
                    for k in range(KT):
                        last = te.transpose(B[4 + u][:, k * TP:(k + 1) * TP], QW[:, u, k * 128:(k + 1) * 128],
                                            IDN[:TP, :TP])
                    last.then_inc(bank_full[4 + u], 1)
            with pe.Fori(0, NT // 2) as i:
                for u in range(2):
                    bk.acquire(pe, "mix_q", 2 + u, i)
                    sum_products(B[2 + u][:TP, :], [
                        (XT[:, pa, k, ds(i * (2 * TP) + u * TP, TP)], rows(0)[:, pw, k, :])
                        for k in range(KT) for pa, pw in PASSES
                    ]).then_inc(bank_full[2 + u], 1)
                q_transposes(i)
            pe.wait_ge(weight_ready, 2)
            for m in range(KT):
                by_feature("mix_k", (0, 1, 6) if m % 2 == 0 else (7, 4, 5), m, [(XT, rows(1))], m // 2)
            pe.wait_ge(weight_ready, 3)
            by_token("mix_v", (0, 1), [(XT, rows(2), KT)])
            bk.after_evacuation(pe, "mix_k")
            for i in range(NT):
                bk.acquire(pe, "mix_kT", 2 + i % 2, i // 2)
                for k in range(KT):
                    last = te.transpose(B[2 + i % 2][:TP, k * 128:(k + 1) * 128], EKT[:, k, i * TP:(i + 1) * TP], IDN[:, :])
                last.then_inc(bank_full[2 + i % 2], 1)
            bk.after_evacuation(pe, "mix_v")
            bk.after_evacuation(pe, "mix_kT")
            bk.acquire(pe, "mix_ctx", 2, 0)
            for m in range(KT):
                last = sum_products(B[2][:, m * 128:(m + 1) * 128], [
                    (EK[:, i, m * 128:(m + 1) * 128], V[:, i, m * 128:(m + 1) * 128]) for i in range(NT)])
            last.then_inc(bank_full[2], 1)
            bk.after_evacuation(pe, "mix_qT")
            bk.after_evacuation(pe, "mix_ctx")
            for i in range(NT):
                bk.acquire(pe, "mix_out", 3 + i % 2, i // 2)
                for m in range(KT):
                    last = te.matmul(B[3 + i % 2][:TP, m * 128:(m + 1) * 128], QT[:, m, i * TP:(i + 1) * TP],
                                     CTX[:, m, :], start=True, stop=True)
                last.then_inc(bank_full[3 + i % 2], 1)

            pe.wait_ge(edges_float, 1)
            for a in range(2):
                bk.acquire(pe, "edges", a, 0)
                for gg in range(3):
                    last = te.transpose(B[a][:, gg * EC:(gg + 1) * EC], IDXF[:, a, gg, :], IDN[:, :])
                last.then_inc(bank_full[a], 1)

            def counts_transposes(T):
                pe.wait_ge(deg_ready, T + 1)
                for b in range(3):
                    bk.acquire(pe, "counts_T", b, T)
                    for j in range(min(4, NT - 4 * b)):
                        sb = 4 * b + j
                        last = te.transpose(B[b][:TP, j * TP:(j + 1) * TP], ACC[T % 2][:, sb // 5, sb % 5 * TP:(sb % 5 + 1) * TP],
                                            IDN[:TP, :TP])
                    last.then_inc(bank_full[b], 1)

            pe.wait_ge(plan_ready, 1)
            pe.sem_inc(onehot_free, RING)
            pe.sem_inc(seg_int, 2)
            bk.after_evacuation(pe, "mix_out")
            for T in range(NT):
                _, n, before = plan(pe, T)
                with pe.Fori(0, n) as i:
                    pe.wait_ge(seg_int, before + i + 1)
                    for j in range(SEG):
                        pe.wait_ge(onehot_ready, (before + i) * (2 * SEG) + (2 * j + 2))
                        for h in range(2):
                            last = te.matmul(PS[:, ds((before + i) % 2 * 2 + (4 + h), 1), 0:HW].rearrange("p a c -> p (a c)"),
                                             ONEHOT_D[:, j % RING, :], ONEHOT_S[:, j % RING, h * HW:(h + 1) * HW],
                                             start=(j == 0), stop=(j == SEG - 1))
                        last.then_inc(onehot_free, 1)
                if T:
                    counts_transposes(T - 1)
            counts_transposes(NT - 1)

            def degrees(stage, done):
                pe.wait_ge(diag_ready, done + 1)
                for b, (lo, n) in enumerate(CHUNKS):
                    bk.acquire(pe, stage, b, 0)
                    te.matmul(B[b][:, 0:n], ONES[:TP, :], DIAG[:, :, :].rearrange("p a b -> p (a b)")[:, lo:lo + n], start=True,
                              stop=True).then_inc(bank_full[b], 1)

            def neighbours(stage):
                with pe.Fori(0, KT // 2) as i:
                    for u in range(2):
                        for c, (lo, n) in enumerate(CHUNKS):
                            bk.acquire(pe, stage, 3 * u + c, i)
                            sum_products(B[3 * u + c][:, 0:n], [
                                (XK[:, pa, sb, ds(i * 256 + 128 * u, 128)], AT[:, pb, sb, lo:lo + n])
                                for sb in range(NT) for pa, pb in PASSES
                            ]).then_inc(bank_full[3 * u + c], 1)

            degrees("deg0", 0)
            bk.after_evacuation(pe, "counts_T")
            neighbours("agg0")
            pe.wait_ge(weight_ready, 5)
            pe.wait_ge(mean_ready, 3 * KT)
            by_token("gnn0", (6, 7), [(XT, rows(0), KT), (MT, rows(1), KT)])

            normed_T("ln1_T", (0, 1), NT)

            def scale_sum(n, a):
                b = (6, 7, 6)[a]
                pe.wait_ge(magnitude, n + 1)
                bk.acquire(pe, "ffn_scale", b, n * 2 + (a // 2) if b == 6 else n)
                te.matmul(B[b][:, :], ONES[:, :], MAG[:, a, :], start=True, stop=True).then_inc(bank_full[b], 1)

            def gate_up(j, par, ahead):
                pe.wait_ge(ffn_low, j + 1)
                if ahead:
                    scale_sum(j + 2, 0)
                    scale_sum(j + 2, 1)
                for a in range(2):
                    for c, (lo, n) in enumerate(CHUNKS):
                        b = 3 * a + c
                        bk.acquire(pe, "ffn", b, j)
                        sum_products(B[b][:, 0:n], [
                            (GU[:, par, a, pw, k * 128:(k + 1) * 128], XT[:, pa, k, lo:lo + n]) for k in range(KT) for pw, pa in PASSES
                        ]).then_inc(bank_full[b], 1)
                        if ahead and a == 0 and c == 0:
                            scale_sum(j + 2, 2)

            for n in range(2):
                for a in range(3):
                    scale_sum(n, a)
            bk.after_evacuation(pe, "ln1_T")
            with pe.Fori(0, 4) as i:
                for u in range(2):
                    gate_up(i * 2 + u, u, True)
            gate_up(8, 0, True)
            gate_up(9, 1, False)
            gate_up(10, 0, False)
            pe.wait_ge(hidden_done, 3 * FT)
            by_token("down", (6, 7), [(HT, WD, FT)])

            normed_T("ln2_T", (2, 3), 2 * NT)
            degrees("deg1", 1)
            pe.wait_ge(counts_back, 16)
            pe.wait_ge(xk_low, 2 * NT)
            neighbours("agg1")
            pe.wait_ge(weight_ready, 7)
            pe.wait_ge(mean_ready, 6 * KT)
            bk.after_evacuation(pe, "ln2_T")
            for m in range(KT):
                by_feature("gnn1", (0, 1, 2) if m % 2 == 0 else (3, 4, 5), m, [(MT, rows(0)), (XT, rows(1))], m // 2)
            for m in range(2 * KT):
                if m % KT == 0:
                    pe.wait_ge(weight_ready, 8 + m // KT)
                by_feature("qk1", (0, 1, 2) if m % 2 == 0 else (3, 4, 5), m % KT, [(XT, rows(2 if m < KT else 0))], m // 2)
            pe.wait_ge(weight_ready, 10)
            by_token("v1", (6, 7), [(XT, rows(1), KT)])
            pe.wait_ge(route_loaded, 16 * 9)
            bk.after_evacuation(pe, "qk1")
            for m in range(KT):
                for c, (lo, n) in enumerate(CHUNKS):
                    b = 3 * (m % 2) + c
                    bk.acquire(pe, "phi_q", b, m // 2)
                    te.matmul(B[b][:, 0:n], PB[:, m, :], QF[:, m, lo:lo + n], start=True, stop=True).then_inc(bank_full[b], 1)
            for i in range(NT):
                bk.acquire(pe, "phi_k", 6 + i % 2, i // 2)
                for m in range(KT):
                    last = te.matmul(B[6 + i % 2][:TP, m * 128:(m + 1) * 128], KF[:, m, i * TP:(i + 1) * TP], PB[:, m, :],
                                     start=True, stop=True)
                last.then_inc(bank_full[6 + i % 2], 1)
            bk.after_evacuation(pe, "v1")
            bk.after_evacuation(pe, "phi_k")
            for b in range(2):
                bk.acquire(pe, "kv", b, 0)
                for m in range(KT):
                    cols = slice(m * 128, (m + 1) * 128)
                    last = sum_products(B[b][:, 0:D].rearrange("p (m c) -> p m c", m=KT)[:, m, :] if b == 0 else B[b][:, 2 * m:2 * m + 2], [
                        (KP[:, i, cols], V1[:, i, cols] if b == 0 else ONES[:TP, 0:2]) for i in range(NT)])
                last.then_inc(bank_full[b], 1)
            bk.after_evacuation(pe, "kv")
            bk.after_evacuation(pe, "phi_q")

            def att_transposes(i):
                pe.wait_ge(att_ready, i + 1)
                bk.acquire(pe, "att_T", 6 + i % 2, i // 2)
                for k in range(KT):
                    last = te.transpose(B[6 + i % 2][:, k * TP:(k + 1) * TP], OW[:, i % 2, k * 128:(k + 1) * 128], IDN[:TP, :TP])
                last.then_inc(bank_full[6 + i % 2], 1)

            for i in range(NT):
                for stage, b0, rhs, w in (("att", 2, KVB, 128), ("z", 4, ZB, 2)):
                    b = b0 + i % 2
                    bk.acquire(pe, stage, b, i // 2)
                    for m in range(KT):
                        last = te.matmul(B[b][:TP, m * w:(m + 1) * w], QP[:, m, i * TP:(i + 1) * TP], rhs[:, m, :], start=True, stop=True)
                    last.then_inc(bank_full[b], 1)
                if i:
                    att_transposes(i - 1)
            att_transposes(NT - 1)
            pe.wait_ge(weight_ready, NU)
            pe.wait_ge(gnn1_done, KT)
            bk.after_evacuation(pe, "att_T")
            for i in range(NT):
                b = i % 2
                cols = slice(i * TP, (i + 1) * TP)
                bk.acquire(pe, "proj", b, i // 2)
                for k in range(KT):
                    te.matmul(B[b][:TP, k * 128:(k + 1) * 128], G[:, k, cols], IDNS[:, :], start=(k == 0), stop=False,
                              skip_group_check=True)
                terms = [(k, pa, pw) for k in range(KT) for pa, pw in PASSES]
                for n, (k, pa, pw) in enumerate(terms):
                    last = te.matmul(B[b][:TP, :], XT[:, pa, k, cols], rows(2)[:, pw, k, :], start=False, stop=(n == len(terms) - 1),
                                     skip_group_check=True)
                last.then_inc(bank_full[b], 1)

            normed_T("ln3_T", (2, 3), 3 * NT)
            pe.wait_ge(wg_ready, 1)
            bk.after_evacuation(pe, "ln3_T")
            bk.acquire(pe, "gate", 4, 0)
            for i in range(NT):
                last = sum_products(B[4][:TP, i * NE:(i + 1) * NE], [
                    (XT[:, pa, k, i * TP:(i + 1) * TP], WGS[:, pw, k, :]) for k in range(KT) for pa, pw in PASSES])
            last.then_inc(bank_full[4], 1)
            pe.wait_ge(masks_ready, 2)
            for b, lhs in ((5, TRI16), (6, ONES16)):
                bk.acquire(pe, "places", b, 0)
                te.matmul(B[b][:TP, 0:NT * 2 * NE], lhs[:TP, :TP], MASK[:, :, :, :].rearrange("p t c e -> p (t c e)"), start=True, stop=True)\
                  .then_inc(bank_full[b], 1)

            def slots_transposes(e, par):
                pe.wait_ge(slots_loaded[par], (e // 2 + 1) * 16)
                for b in range(3):
                    bk.acquire(pe, "slots_T", b, e)
                    for k in range(KT):
                        last = te.transpose(B[b][:, k * CT:(k + 1) * CT], XE[:, par, b, k * 128:(k + 1) * 128], IDN[:CT, :CT])
                    last.then_inc(bank_full[b], 1)

            def hidden(e, par):
                pe.wait_ge(weight_ready, e + (NU + 1))
                for b in range(3):
                    bk.emptied(pe, "slots_T", b, e)
                w1 = W[par][:, :, 0:1024].rearrange("p a (k h) -> p a k h", k=KT)
                for m in range(2):
                    bk.acquire(pe, "hidden", 3 + m, e)
                    sum_products(B[3 + m][:, 0:CAP], [
                        (w1[:, pw, k, m * 128:(m + 1) * 128], XET[:, par, pa, k, :]) for k in range(KT) for pw, pa in PASSES
                    ]).then_inc(bank_full[3 + m], 1)

            def expert_out(e, par):
                pe.wait_ge(relu_low, e + 1)
                w2 = W[par][:, :, 1024:2048].rearrange("p a (k d) -> p a k d", k=2)
                for c in range(3):
                    bk.acquire(pe, "expert", 5 + c, e)
                    sum_products(B[5 + c][:CT, :], [
                        (HH[:, par, pa, k, c * CT:(c + 1) * CT], w2[:, pw, k, :]) for k in range(2) for pa, pw in PASSES
                    ]).then_inc(bank_full[5 + c], 1)

            slots_transposes(0, 0)
            for e in range(NE):
                hidden(e, e % 2)
                if e + 1 < NE:
                    slots_transposes(e + 1, (e + 1) % 2)
                expert_out(e, e % 2)

        @block.vector
        def _(dve):
            v = nc.vector
            own = Own(dve, dve_own)

            def heads(x):
                return x.rearrange("p (h d) -> p h d", h=H)

            def norm(stage, banks, n, keep_low_waits=None):
                for i in range(NT):
                    if stage == "ln0_T" and i % 5 == 0:
                        dve.wait_ge(x_loaded[i // 5], 16)
                    m = own.mark(v.bn_stats(STATS[:, i, :], X[:, i, :]))
                own.after(m)
                for i in range(NT):
                    last = v.bn_aggr(MV[:, i, :], STATS[:, i, :])
                    if i < NT - 1:
                        m = own.mark(last)
                    else:
                        last.then_inc(var_ready, 1)
                own.after(m)
                dve.wait_ge(std_ready, n + 1)
                own.step(v.reciprocal(RSTD[:, :], STD[:, :]))
                own.step(v.tensor_scalar(RSTD[:, :], RSTD[:, :], A_SCALE, None, ALU.mult))
                with dve.Fori(0, NT // 2) as i:
                    for u in range(2):
                        v.tensor_scalar(XN[:, ds(i * 2 + u, 1), :], X[:, ds(i * 2 + u, 1), :], MV[:, ds(i * 2 + u, 1), 0:1].rearrange("p a b -> p (a b)"),
                                        RSTD[:, ds(i * 2 + u, 1)], ALU.subtract, ALU.mult).then_inc(xn_ready, 1)
                with dve.Fori(0, NT // 2) as i:
                    for u in range(2):
                        dve.wait_ge(xt_high, i * 2 + (NT * (n + (n == 3)) + u + 1))
                        cols = ds(i * (2 * TP) + u * TP, TP)
                        v.scalar_tensor_tensor(XT[:, 1, :, cols], B[banks[u]][:, 0:KT * TP].rearrange("p (k n) -> p k n", k=KT),
                                               1.0, XT[:, 0, :, cols], ALU.mult, ALU.subtract).then_inc(bank_free[banks[u]], 1)

            norm("ln0_T", (0, 1), 0)
            dve.wait_ge(small_loaded, 160)
            with own.loop(NT // 2, 6) as i:
                for u in range(2):
                    bk.filled(dve, "mix_q", 2 + u, i)
                    bk.acquire(dve, "mix_qT", 4 + u, i)
                    ins = v.scalar_tensor_tensor(QW[:, u, :], B[2 + u][:TP, :], UNSCALE, BQ, ALU.mult, ALU.add)
                    ins.then_inc(bank_free[2 + u], 1)
                for u in range(2):
                    dve.wait_ge(bank_free[2 + u], i + (bk.before["mix_q"][2 + u] + 2))
                    m = own.mark(v.tensor_reduce(SM8[:, u, 0, :], heads(QW[:, u, :]), AX.X, ALU.max))
                own.after(m)
                for u in range(2):
                    v.tensor_tensor(heads(QW[:, u, :]), heads(QW[:, u, :]), SM8[:, u, 0, :].unsqueeze(2).to_broadcast([TP, H, DH]),
                                    ALU.subtract).then_inc(q_shifted, 1)
                for u in range(2):
                    dve.wait_ge(q_exp, i * 2 + (u + 1))
                    m = own.mark(v.tensor_reduce(SM8[:, u, 1, :], heads(QW[:, u, :]), AX.X, ALU.add))
                own.after(m)
                for u in range(2):
                    m = own.mark(v.reciprocal(SM8[:, u, 2, :], SM8[:, u, 1, :]))
                own.after(m)
                for u in range(2):
                    v.scalar_tensor_tensor(heads(QW[:, u, :]), heads(QW[:, u, :]), DH ** -0.5,
                                           SM8[:, u, 2, :].unsqueeze(2).to_broadcast([TP, H, DH]), ALU.mult, ALU.mult)\
                     .then_inc(q_soft, 1)
            for m in range(KT):
                for c, (lo, n) in enumerate(CHUNKS):
                    b = (0, 1, 6, 7, 4, 5)[3 * (m % 2) + c]
                    bk.filled(dve, "mix_k", b, m // 2)
                    mm = own.mark(v.tensor_reduce(KMX[:, c:c + 1], B[b][:, 0:n], AX.X, ALU.max))
                own.after(mm)
                own.step(v.tensor_reduce(KMAX[:, m:m + 1], KMX[:, :], AX.X, ALU.max))
                own.step(v.scalar_tensor_tensor(KMAX[:, m:m + 1], KMAX[:, m:m + 1], UNSCALE, BK[:, m:m + 1], ALU.mult, ALU.add))
                v.tensor_tensor(KBIAS[:, m:m + 1], BK[:, m:m + 1], KMAX[:, m:m + 1], ALU.subtract).then_inc(kbias_ready, 1)
            with dve.Fori(0, NT // 2) as i:
                for u in range(2):
                    bk.filled(dve, "mix_v", u, i)
                    v.scalar_tensor_tensor(V[:, ds(i * 2 + u, 1), :], B[u][:TP, :].rearrange("p (a d) -> p a d", a=1), UNSCALE, BV.rearrange("p (a d) -> p a d", a=1), ALU.mult, ALU.add)\
                     .then_inc(bank_free[u], 1)
            bk.after_evacuation(dve, "mix_k")
            own.step(v.tensor_reduce(KSUM, KSUM3[:, :, :], AX.X, ALU.add))
            own.mark(v.reciprocal(KREC, KSUM))
            own.step(v.memset(CTX[:, :, :], 0.0))
            bk.filled(dve, "mix_ctx", 2, 0)
            for hh in range(2):
                p = slice(64 * hh, 64 * hh + 64)
                last = v.tensor_tensor(CTX[p, :, p], B[2][p, :].rearrange("p (m d) -> p m d", m=KT)[:, :, p],
                                KREC[p, :].unsqueeze(2).to_broadcast([64, KT, 64]), ALU.mult)
                last.then_inc(bank_free[2] if hh else dve_own, 1)
            own.k += 1
            with dve.Fori(0, NT // 2) as i:
                for u in range(2):
                    bk.filled(dve, "mix_out", 3 + u, i)
                    v.tensor_tensor(X[:, ds(i * 2 + u, 1), :], B[3 + u][:TP, :].rearrange("p (a d) -> p a d", a=1), X[:, ds(i * 2 + u, 1), :], ALU.add)\
                     .then_inc(bank_free[3 + u], 1)

            dve.wait_ge(edges_loaded, 97)
            own.step(v.tensor_copy(IDXF[:, :, :, :], IDX[:, :, :, :]))
            v.tensor_scalar(TMP[:, :, :], IDXF[:, 1, :, :], 0.0, 2.0 * N, ALU.is_lt, ALU.mult).then_inc(edges_float, 1)
            own.mark(v.tensor_reduce(RED[:, 0, :], IDXF[:, 1, :, :], AX.X, ALU.max))
            dve.wait_ge(edges_float, 1)
            own.step(v.tensor_tensor(TMP[:, :, :], TMP[:, :, :], IDXF[:, 1, :, :], ALU.add))
            own.step(v.tensor_reduce(RED[:, 1, :], TMP[:, :, :], AX.X, ALU.min))
            thr = THR[:, :].unsqueeze(2).to_broadcast([128, NT, 3])

            def per_tile(x):
                return x.unsqueeze(1).to_broadcast([128, NT, 3])

            own.mark(v.scalar_tensor_tensor(RANGE[:, 0, 0, :, :], per_tile(RED[:, 0, :]), 0.5, thr, ALU.add, ALU.is_gt))
            own.step(v.scalar_tensor_tensor(RANGE[:, 0, 1, :, :], per_tile(RED[:, 1, :]), TP - 0.5, thr, ALU.subtract, ALU.is_lt))
            own.step(v.tensor_tensor(RANGE[:, 0, 2, :, :], RANGE[:, 0, 0, :, :], RANGE[:, 0, 1, :, :], ALU.mult))
            for a in range(2):
                m = own.mark(v.tensor_tensor(RANGE[:, 1, a, :, :], RANGE[:, 0, 2, :, :], per_tile(CID[:, a, :]), ALU.mult))
            own.after(m)
            v.tensor_reduce(LOHI[:, :, :], RANGE[:, 1, 0:2, :, :], AX.X, ALU.max).then_inc(lohi_local, 1)
            bk.filled(dve, "edges", 1, 0)
            v.tensor_copy(DST[:, :], B[1][:, 0:NCH]).then_inc(bank_free[1], 1)
            bk.filled(dve, "edges", 0, 0)
            own.mark(v.tensor_copy(SRC[:, :], B[0][:, 0:NCH]))
            v.tensor_scalar(SRCV[:, :], B[0][:, 0:NCH], float(HS), BASE - 1.0, ALU.is_ge, ALU.mult).then_inc(bank_free[0], 1)
            bk.after_evacuation(dve, "edges")
            own.step(v.tensor_scalar(SRCV[:, :], SRCV[:, :], 1.0, None, ALU.add))
            tmp = TMP[:, :, :].rearrange("p g e -> p (g e)")
            own.step(v.tensor_scalar(tmp, SRC[:, :], float(HS), float(HS), ALU.is_ge, ALU.mult))
            own.step(v.tensor_tensor(SRC[:, :], SRC[:, :], tmp, ALU.subtract))
            own.mark(v.memset(ONEHOT_S[:, :, ONE_COL:ONE_COL + 1], 1.0))
            own.mark(v.memset(ONEHOT_S[:, :, ONE_COL + 1:2 * HW], 0.0))
            own.step(v.memset(I2[:, :, :, :], 0))
            dve.wait_ge(lohi_all, 1)
            own.mark(v.memset(PLAN[:, :, :], 0.0))
            own.step(v.tensor_scalar(LOHI[0:1, 0, :], LOHIR[0:1, 0, :], -1.0, 512.0, ALU.mult, ALU.add))
            own.step(v.tensor_scalar(PLAN[0:1, 0, 0:NT], LOHI[0:1, 0, :], float(ER), None, ALU.min))
            own.step(v.tensor_scalar(LOHI[0:1, 0, :], PLAN[0:1, 0, 0:NT], 1.0, None, ALU.add))
            own.step(v.tensor_tensor(LOHI[0:1, 1, :], LOHIR[0:1, 1, :], LOHI[0:1, 0, :], ALU.max))
            own.step(v.tensor_tensor(LOHI[0:1, 1, :], LOHI[0:1, 1, :], PLAN[0:1, 0, 0:NT], ALU.subtract))
            own.step(v.tensor_tensor(STEPS[:, :, :], LOHI[0:1, 1, :].unsqueeze(2).to_broadcast([1, NT, 32]),
                                     MULT[:, :].unsqueeze(1).to_broadcast([1, NT, 32]), ALU.is_gt))
            own.step(v.tensor_reduce(PLAN[0:1, 1, 0:NT], STEPS[:, :, :], AX.X, ALU.add))
            for T in range(NT):
                own.step(v.tensor_tensor(PLAN[0:1, 2, T + 1:T + 2], PLAN[0:1, 2, T:T + 1], PLAN[0:1, 1, T:T + 1], ALU.add))
            v.tensor_copy(PLANI[:, :, :], PLAN[:, :, :]).then_inc(plan_ready, 1)
            dve.wait_ge(plan_ready, 1)
            dve.sem_inc(lohi_ready, 1)

            def unpack(f):
                dve.wait_ge(seg_int, f + 2)
                dve.wait_ge(acc_added, f + 1)
                both = I2[:, ds((f + 1) % 2, 1), :, :].rearrange("p a h c -> p (a h c)")
                v.tensor_scalar(LH[:, 0, :], both, int(BASE) - 1, None, ALU.bitwise_and).then_inc(dve_free, 1)
                v.tensor_scalar(LH[:, 1, :], both, 12, None, ALU.logical_shift_right).then_inc(lohi_ready, 1)

            def counts_low(T):
                for b in range(3):
                    n = min(4, NT - 4 * b)
                    dve.wait_ge(counts_high, 3 * T + b + 1)
                    cols = slice(T * TP, (T + 1) * TP)
                    v.scalar_tensor_tensor(AT[:, 1, 4 * b:4 * b + n, cols], B[b][:TP, 0:n * TP].rearrange("p (s d) -> p s d", s=n),
                                           1.0, AT[:, 0, 4 * b:4 * b + n, cols], ALU.mult, ALU.subtract).then_inc(bank_free[b], 1)

            for T in range(NT):
                lo, n, before = plan(dve, T)
                own.step(v.tensor_scalar(DREL[:, T % 2, :], DST[:, :], -float(TP * T), None, ALU.add))
                with dve.Fori(0, n) as i:
                    first = nc.s_assert_within(lo + i * SEG, 0, NCH - SEG, skip_runtime_bounds_check_because="the plan's last segment starts before the last chunk")
                    for j in range(SEG):
                        dve.wait_ge(onehot_free, (before + i) * SEG + (j + 1))
                        v.tensor_scalar(ONEHOT_D[:, j % RING, :], IOTA_D[:, :], DREL[:, T % 2, ds(first + j, 1)], None, ALU.is_equal)\
                         .then_inc(onehot_ready, 1)
                        v.tensor_scalar(ONEHOT_S[:, j % RING, 0:ONE_COL], IOTA_S[:, :], SRC[:, ds(first + j, 1)],
                                        SRCV[:, ds(first + j, 1)], ALU.is_equal, ALU.mult).then_inc(onehot_ready, 1)
                        if j == SEG // 2:
                            unpack(before + i)
                if T >= 2:
                    counts_low(T - 2)
            unpack(before + n)
            counts_low(NT - 2)
            counts_low(NT - 1)

            def means(stage_deg, stage, done):
                dve.wait_ge(deg_ready, NT)
                if done == 0:
                    own.step(v.tensor_scalar(DEG[:, :], DEG[:, :], 1.0, None, ALU.max))
                    own.step(v.reciprocal(RDEG[:, :], DEG[:, :]))
                v.tensor_tensor(DIAG[:, :, :], IDN[:TP, :TP].unsqueeze(1).to_broadcast([TP, NT, TP]),
                                RDEG[:, :].unsqueeze(2).to_broadcast([TP, NT, TP]), ALU.mult).then_inc(diag_ready, 1)
                for b, (lo, n) in enumerate(CHUNKS):
                    bk.filled(dve, stage_deg, b, 0)
                    v.tensor_copy(DG[:, lo:lo + n], B[b][:, 0:n]).then_inc(bank_free[b], 1)
                bk.after_evacuation(dve, stage_deg)
                with dve.Fori(0, KT // 2) as i:
                    for u in range(2):
                        for c, (lo, n) in enumerate(CHUNKS):
                            bk.filled(dve, stage, 3 * u + c, i)
                            v.tensor_tensor(MTMP[:, u, c, 0:n], B[3 * u + c][:, 0:n], DG[:, lo:lo + n], ALU.mult).then_inc(bank_free[3 * u + c], 1)
                        for c, (lo, n) in enumerate(CHUNKS):
                            dve.wait_ge(mean_high, i * 6 + (3 * u + c + 1 + 3 * KT * done))
                            v.tensor_tensor(MT[:, 1, ds(i * 2 + u, 1), lo:lo + n], MTMP[:, u, c:c + 1, 0:n],
                                            MT[:, 0, ds(i * 2 + u, 1), lo:lo + n], ALU.subtract).then_inc(mean_ready, 1)

            means("deg0", "agg0", 0)
            with own.loop(NT // 2, 2) as i:
                for u in range(2):
                    bk.filled(dve, "gnn0", 6 + u, i)
                    v.scalar_tensor_tensor(XN[:, ds(i * 2 + u, 1), :], B[6 + u][:TP, :].unsqueeze(1), UNSCALE, BIAS.unsqueeze(1),
                                           ALU.mult, ALU.add).then_inc(bank_free[6 + u], 1)
                for u in range(2):
                    bk.emptied(dve, "gnn0", 6 + u, i)
                    own.mark(v.bn_stats(STATS[:, ds(i * 2 + u, 1), :].rearrange("p a b -> p (a b)"), XN[:, ds(i * 2 + u, 1), :].rearrange("p a b -> p (a b)")))
            own.after(own.base + own.k)
            for i in range(NT):
                last = v.bn_aggr(MV[:, i, :], STATS[:, i, :])
                if i < NT - 1:
                    m = own.mark(last)
                else:
                    last.then_inc(gnn_var, 1)
            own.after(m)
            dve.wait_ge(gnn_std, 1)
            own.step(v.reciprocal(RSTD[:, :], STD[:, :]))
            dve.wait_ge(beta_added, NT)
            for i in range(NT):
                m = own.mark(v.tensor_scalar(XN[:, i, :], XN[:, i, :], MV[:, i, 0:1], RSTD[:, i:i + 1], ALU.subtract, ALU.mult))
            own.after(m)
            for i in range(NT):
                m = own.mark(v.tensor_tensor(XN[:, i, :], XN[:, i, :], GAMMA, ALU.mult))
            own.after(m)
            for i in range(NT):
                v.tensor_tensor(X[:, i, :], X[:, i, :], XN[:, i, :], ALU.add).then_inc(x1_ready, 1)

            dve.wait_ge(x1_ready, NT)
            norm("ln1_T", (0, 1), 1)

            def ternaries(n, par):
                w = STG[(par + 1) % 2][:, 0:1536].rearrange("p (a c) -> p a c", a=3)
                bk.emptied(dve, "ffn_scale", 6, n * 2 + 1)
                bk.emptied(dve, "ffn_scale", 7, n)
                if not (isinstance(n, int) and n == 0):
                    dve.wait_ge(quantised, n)
                own.mark(v.scalar_tensor_tensor(MAG[:, :, :], QUANT[:, par, :, :], 0.5 / W_SCALE, w, ALU.mult, ALU.is_lt))
                own.step(v.scalar_tensor_tensor(TERN[:, :, :], QUANT[:, par, :, :], -0.5 / W_SCALE, w, ALU.mult, ALU.is_gt))
                v.tensor_tensor(TERN[:, :, :], MAG[:, :, :], TERN[:, :, :], ALU.subtract).then_inc(ternary, 1)

            def hiddens(j):
                for c, (lo, n) in enumerate(CHUNKS):
                    bk.filled(dve, "ffn", 3 + c, j)
                    bk.emptied(dve, "ffn", c, j)
                    v.scalar_tensor_tensor(GATED[:, c, 0:n], B[3 + c][:, 0:n], UNSCALE * A_SCALE, GATED[:, c, 0:n], ALU.mult, ALU.mult)\
                     .then_inc(bank_free[3 + c], 1)
                for c, (lo, n) in enumerate(CHUNKS):
                    dve.wait_ge(hidden_high, j * 3 + (c + 1))
                    v.tensor_tensor(HT[:, 1, ds(j, 1), lo:lo + n], GATED[:, c:c + 1, 0:n], HT[:, 0, ds(j, 1), lo:lo + n], ALU.subtract)\
                     .then_inc(hidden_done, 1)

            ternaries(0, 0)
            ternaries(1, 1)
            with own.loop(4, 4) as i:
                for u in range(2):
                    ternaries(i * 2 + (u + 2), u)
                    hiddens(i * 2 + u)
            ternaries(10, 0)
            for j in (8, 9, 10):
                hiddens(j)
            x2_ready = own.base + own.k
            for i in range(NT):
                b = 6 + i % 2
                bk.filled(dve, "down", b, i // 2)
                v.scalar_tensor_tensor(X[:, i, :], B[b][:TP, :], UNSCALE, X[:, i, :], ALU.mult, ALU.add).then_inc(bank_free[b], 1)
            bk.after_evacuation(dve, "down")
            norm("ln2_T", (2, 3), 2)
            dve.wait_ge(xk_low, 2 * NT)
            bk.after_evacuation(dve, "ln2_T")
            means("deg1", "agg1", 1)

            for m in range(KT):
                for c, (lo, n) in enumerate(CHUNKS):
                    bk.emptied(dve, "gnn1", 3 * (m % 2) + c, m // 2)
                    mm = own.mark(v.bn_stats(GSTATS[:, m, c, :], G[:, m, lo:lo + n]))
            own.after(mm)
            for m in range(KT):
                ins = v.bn_aggr(GMV[:, m, :], GSTATS[:, m, :, :])
                if m < KT - 1:
                    mm = own.mark(ins)
                else:
                    ins.then_inc(gnn1_var, 1)
            dve.wait_ge(gnn1_var, 1)
            dve.wait_ge(gnn1_std, 1)
            own.step(v.reciprocal(GCOL[:, 1, :], GCOL[:, 0, :]))
            own.step(v.tensor_tensor(GCOL[:, 2, :], GCOL[:, 1, :], G1, ALU.mult))
            own.step(v.tensor_tensor(GCOL[:, 3, :], GMV[:, :, 0], GCOL[:, 2, :], ALU.mult))
            own.step(v.tensor_tensor(GCOL[:, 3, :], B1, GCOL[:, 3, :], ALU.subtract))
            for m in range(KT):
                v.tensor_scalar(G[:, m, :], G[:, m, :], GCOL[:, 2, m:m + 1], GCOL[:, 3, m:m + 1], ALU.mult, ALU.add).then_inc(gnn1_done, 1)
            with dve.Fori(0, NT // 2) as i:
                for u in range(2):
                    bk.filled(dve, "v1", 6 + u, i)
                    v.tensor_scalar(V1[:, ds(i * 2 + u, 1), :], B[6 + u][:TP, :].unsqueeze(1), UNSCALE, None, ALU.mult).then_inc(bank_free[6 + u], 1)
            for m in range(KT):
                for c, (lo, n) in enumerate(CHUNKS):
                    b = 3 * (m % 2) + c
                    bk.filled(dve, "phi_q", b, m // 2)
                    if m:
                        bk.emptied(dve, "phi_q", 3 * ((m - 1) % 2) + c, (m - 1) // 2)
                    v.tensor_scalar(PTMP[:, c, 0:n], B[b][:, 0:n], 0.0, None, ALU.min).then_inc(phi_min, 1)
                for c, (lo, n) in enumerate(CHUNKS):
                    b = 3 * (m % 2) + c
                    dve.wait_ge(phi_exp, 3 * m + c + 1)
                    v.scalar_tensor_tensor(QP[:, m, lo:lo + n], B[b][:, 0:n], 0.0, PTMP[:, c, 0:n], ALU.max, ALU.add).then_inc(bank_free[b], 1)
            bk.after_products(dve, "phi_q")
            with dve.Fori(0, NT // 2) as i:
                for u in range(2):
                    bk.filled(dve, "phi_k", 6 + u, i)
                    bk.acquire(dve, "phi_k", 6 + u, i)
                    v.tensor_scalar(OW[:, u, :], B[6 + u][:TP, :], 0.0, None, ALU.min).then_inc(kmin, 1)
                for u in range(2):
                    dve.wait_ge(kexp, i * 2 + (u + 1))
                    v.scalar_tensor_tensor(KP[:, ds(i * 2 + u, 1), :], B[6 + u][:TP, :].unsqueeze(1), 0.0, OW[:, u:u + 1, :], ALU.max, ALU.add)\
                     .then_inc(bank_free[6 + u], 1)
            dve.wait_ge(wide_own, 1)
            bk.after_products(dve, "kv")
            for hh in range(2):
                p = slice(64 * hh, 64 * hh + 64)
                own.mark(v.tensor_copy(KVB[p, :, p], B[0][p, :].rearrange("p (m d) -> p m d", m=KT)[:, :, p])) if hh == 0 else \
                    v.tensor_copy(KVB[p, :, p], B[0][p, :].rearrange("p (m d) -> p m d", m=KT)[:, :, p]).then_inc(bank_free[0], 1)
                ins = v.tensor_copy(ZB[p, :, hh:hh + 1], B[1][p, 0:2 * KT].rearrange("p (m c) -> p m c", m=KT)[:, :, 0:1])
                ins.then_inc(bank_free[1] if hh else dve_own, 1)
                own.k += 1 - hh
            bk.after_evacuation(dve, "phi_k")

            def expert_prescale(e, par):
                st = STG[(par + NU + 1) % 2]
                dve.wait_ge(staged[(par + NU + 1) % 2], expert_staged(e, par))
                v.tensor_scalar(st[:, :], st[:, :], W_SCALE, None, ALU.mult).then_inc(expert_prescaled, 1)

            def att_low(i):
                b, cols = 6 + i % 2, slice(i * TP, (i + 1) * TP)
                dve.wait_ge(xt_high, 3 * NT + i + 1)
                v.scalar_tensor_tensor(XT[:, 1, :, cols], B[b][:, 0:KT * TP].rearrange("p (k n) -> p k n", k=KT), A_SCALE,
                                       XT[:, 0, :, cols], ALU.mult, ALU.subtract).then_inc(bank_free[b], 1)

            for i in range(NT):
                if i >= 2:
                    att_low(i - 2)
                bk.filled(dve, "z", 4 + i % 2, i // 2)
                v.reciprocal(SM8[:, i % 2, 2, :], B[4 + i % 2][:TP, 0:H]).then_inc(bank_free[4 + i % 2], 1)
                bk.emptied(dve, "z", 4 + i % 2, i // 2)
                bk.filled(dve, "att", 2 + i % 2, i // 2)
                if i >= 2:
                    bk.filled(dve, "att_T", 6 + i % 2, i // 2 - 1)
                v.tensor_tensor(heads(OW[:, i % 2, :]), heads(B[2 + i % 2][:TP, :]), SM8[:, i % 2, 2, :].unsqueeze(2).to_broadcast([TP, H, DH]),
                                ALU.mult).then_inc(att_ready, 1)
                bk_free = bank_free[2 + i % 2]
                dve.wait_ge(att_ready, i + 1)
                dve.sem_inc(bk_free, 1)
            att_low(NT - 2)
            att_low(NT - 1)
            expert_prescale(0, 0)
            expert_prescale(1, 1)
            dve.wait_ge(wg_high, 1)
            v.scalar_tensor_tensor(WGS[:, 1, :, :].rearrange("p k e -> p (k e)"), WG[:, :], W_SCALE, WGS[:, 0, :, :].rearrange("p k e -> p (k e)"),
                                   ALU.mult, ALU.subtract).then_inc(wg_ready, 1)
            dve.wait_ge(bproj_added, NT)
            for i in range(NT):
                b = i % 2
                bk.filled(dve, "proj", b, i // 2)
                v.scalar_tensor_tensor(X[:, i, :], B[b][:TP, :], UNSCALE, X[:, i, :], ALU.mult, ALU.add).then_inc(bank_free[b], 1)
            bk.after_evacuation(dve, "proj")
            norm("ln3_T", (2, 3), 3)

            R = [ROUTE[:, n, :, :] for n in range(12)]
            K = [TOK[:, n, :] for n in range(12)]

            def by_expert(x):
                return x.unsqueeze(2).to_broadcast([TP, NT, NE])

            def by_tokens(x):
                return x.unsqueeze(1).to_broadcast([TP, NT, NE])

            bk.filled(dve, "gate", 4, 0)
            v.tensor_scalar(R[0], B[4][:TP, 0:NT * NE].rearrange("p (t e) -> p t e", t=NT), UNSCALE, None, ALU.mult).then_inc(bank_free[4], 1)
            bk.after_evacuation(dve, "gate")
            own.step(v.tensor_reduce(K[0], R[0], AX.X, ALU.max))
            v.tensor_tensor(R[0], R[0], by_expert(K[0]), ALU.subtract).then_inc(gate_exp_in, 1)
            dve.wait_ge(gate_exp, 1)
            own.step(v.tensor_reduce(K[0], R[0], AX.X, ALU.add))
            own.step(v.reciprocal(K[1], K[0]))
            own.step(v.tensor_tensor(R[0], R[0], by_expert(K[1]), ALU.mult))
            dve.wait_ge(route_consts, 3)
            for c in range(2):
                own.step(v.tensor_reduce(K[2 + c], R[c], AX.X, ALU.max))
                own.step(v.tensor_tensor(R[2], R[c], by_expert(K[2 + c]), ALU.is_equal))
                own.step(v.tensor_tensor(R[2], R[2], by_tokens(EBASE[:, 1, :]), ALU.mult))
                own.step(v.tensor_reduce(K[4], R[2], AX.X, ALU.max))
                own.step(v.tensor_tensor(R[3 + c], R[2], by_expert(K[4]), ALU.is_equal))
                v.tensor_copy(MASK[:, :, c, :], R[3 + c]).then_inc(masks_ready, 1)
                if c == 0:
                    own.step(v.tensor_tensor(R[2], R[0], R[3], ALU.mult))
                    own.step(v.tensor_tensor(R[1], R[0], R[2], ALU.subtract))
            own.step(v.tensor_tensor(K[4], K[2], K[3], ALU.add))
            own.step(v.tensor_scalar(K[4], K[4], 1e-9, None, ALU.add))
            own.step(v.reciprocal(K[4], K[4]))
            own.mark(v.tensor_tensor(K[2], K[2], K[4], ALU.mult))
            own.step(v.tensor_tensor(K[3], K[3], K[4], ALU.mult))
            own.mark(v.memset(CARRY[:, 0, :], 0.0))
            bk.filled(dve, "places", 6, 0)
            own.step(v.tensor_copy(CARRY[:, 1, :], B[6][:TP, 0:2 * NE]))
            for i in range(1, NT):
                ins = v.tensor_tensor(CARRY[:, i + 1, :], B[6][:TP, i * 2 * NE:(i + 1) * 2 * NE], CARRY[:, i, :], ALU.add)
                if i < NT - 1:
                    own.step(ins)
                else:
                    ins.then_inc(bank_free[6], 1)
            bk.emptied(dve, "places", 6, 0)
            own.step(v.tensor_scalar(CARRY[:, NT, 0:NE], CARRY[:, NT, 0:NE], float(CAP), None, ALU.min))
            bk.filled(dve, "places", 5, 0)
            within = B[5][:TP, 0:NT * 2 * NE].rearrange("p (t c e) -> p t c e", t=NT, c=2)
            carry = CARRY[:, 0:NT, :].rearrange("p t (c e) -> p t c e", c=2)
            own.mark(v.tensor_tensor(R[5], within[:, :, 0, :], carry[:, :, 0, :], ALU.add))
            v.tensor_tensor(R[6], within[:, :, 1, :], carry[:, :, 1, :], ALU.add).then_inc(bank_free[5], 1)
            bk.emptied(dve, "places", 5, 0)
            own.step(v.tensor_tensor(R[6], R[6], by_tokens(CARRY[:, NT, 0:NE]), ALU.add))
            for c in range(2):
                own.step(v.tensor_tensor(R[7], R[5 + c], R[3 + c], ALU.mult))
                own.step(v.tensor_reduce(K[5], R[7], AX.X, ALU.add))
                own.step(v.tensor_tensor(R[8], R[3 + c], by_tokens(EBASE[:, 0, :]), ALU.mult))
                own.step(v.tensor_reduce(K[6], R[8], AX.X, ALU.add))
                own.mark(v.tensor_tensor(K[6], K[6], K[5], ALU.add))
                own.step(v.tensor_scalar(K[7], K[5], float(CAP), None, ALU.is_lt))
                own.mark(v.tensor_tensor(K[2 + c], K[2 + c], K[7], ALU.mult))
                own.mark(v.tensor_tensor(K[8], K[6], K[7], ALU.mult))
                own.step(v.tensor_tensor(K[9], K[6], DUMP[:, c, :], ALU.subtract))
                own.step(v.tensor_tensor(K[9], K[9], K[7], ALU.mult))
                own.step(v.tensor_tensor(K[9], K[9], DUMP[:, c, :], ALU.add))
                own.mark(v.tensor_copy(GIDX[:, c, :], K[8]))
                v.tensor_copy(SIDX[:, c, :], K[9]).then_inc(places_ready, 1)
                dve.wait_ge(places_ready, c + 1)

            def slots_low(e, par):
                for b in range(3):
                    dve.wait_ge(slots_high, e * 3 + (b + 1))
                    cols = slice(b * CT, (b + 1) * CT)
                    v.scalar_tensor_tensor(XET[:, par, 1, :, cols], B[b][:, 0:KT * CT].rearrange("p (k n) -> p k n", k=KT), 1.0,
                                           XET[:, par, 0, :, cols], ALU.mult, ALU.subtract).then_inc(bank_free[b], 1)

            def relu_lows(e, par):
                dve.wait_ge(relu_high, e + 1)
                v.tensor_tensor(HH[:, par, 1, :, :].rearrange("p m c -> p (m c)"), HTMP[:, par, :], HH[:, par, 0, :, :].rearrange("p m c -> p (m c)"),
                                ALU.subtract).then_inc(relu_low, 1)

            def outs(e, par):
                if not (isinstance(e, int) and e < 2):
                    dve.wait_ge(outs_stored[par], stored_count(e, par))
                for c in (1, 2):
                    bk.filled(dve, "expert", 5 + c, e)
                    if c == 2:
                        bk.emptied(dve, "expert", 5, e)
                    v.tensor_scalar(EO[:, par, c, :], B[5 + c][:CT, :], UNSCALE, None, ALU.mult).then_inc(bank_free[5 + c], 1)

            slots_low(0, 0)
            for e in range(NE):
                relu_lows(e, e % 2)
                if e + 1 < NE:
                    slots_low(e + 1, (e + 1) % 2)
                if e + 2 < NE:
                    expert_prescale(e + 2, e % 2)
                outs(e, e % 2)
            for i in range(NT):
                for c in range(2):
                    n = 2 * i + c
                    dve.wait_ge(gathered[n % 4], 16 * (n // 4 + 1))
                    if c:
                        dve.wait_ge(half_added, i + 1)
                    v.scalar_tensor_tensor(X[:, i, :], GATHER[:, n % 4, :], K[2 + c][:, i:i + 1], X[:, i, :], ALU.mult, ALU.add)\
                     .then_inc(y_ready if c else half_added, 1)


def arrange(inputs):
    import numpy as np

    put = {}
    for name, a in inputs.items():
        a = np.asarray(a)
        if name in ("L0_mix_Wq", "L0_mix_Wk", "L0_mix_Wv", "L0_gnn_W_self", "L0_gnn_W_neigh", "L0_ffn_w_gate",
                    "L0_ffn_w_up", "L0_ffn_w_down", "L1_gnn_W_l", "L1_gnn_W_r"):
            put[name + "T"] = np.ascontiguousarray(a.T)
        elif name in ("L0_mix_bk", "L1_gnn_b_l", "L1_gnn_gamma", "L1_gnn_beta"):
            put[name + "C"] = np.ascontiguousarray(a.reshape(KT, 128).T)
        else:
            put[name] = np.ascontiguousarray(a)
    return put


def kernel(**inputs):
    import concourse.bacc as bacc
    from concourse import mybir as mb
    from concourse.bass_utils import run_bass_kernel_spmd

    nc = bacc.Bacc("TRN2", target_bir_lowering=False, num_devices=1)
    arrays = {f"in_{k}_dram": a for k, a in arrange(inputs).items()}
    t = {k[3:-5]: nc.dram_tensor(k, a.shape, mb.dt.from_np(a.dtype), kind="ExternalInput").ap() for k, a in arrays.items()}
    out = nc.dram_tensor("out_dram", (N, D), F32, kind="ExternalOutput").ap()
    gps_two_layers(nc, t, out)
    return run_bass_kernel_spmd(nc, [arrays], core_ids=[0]).results[0]["out_dram"]
```

```python
from contextlib import ExitStack, contextmanager

import concourse.bass as bass
from concourse import mybir

F32, F16, I32 = mybir.dt.float32, mybir.dt.float16, mybir.dt.int32
ALU, ACT, AX = mybir.AluOpType, mybir.ActivationFunctionType, mybir.AxisListType
ds = bass.ds

N, D, E = 1250, 512, 41250
TP, NT = 125, 10
KT = D // 128
CHUNKS = [(0, 418), (418, 416), (834, 416)]
H, DH = 8, 64
FFN, FT = 1408, 11
NE, HID, CAP = 16, 256, 312
CT = CAP // 3
SLOTS = NE * CAP
A_SCALE, W_SCALE = 16.0, 64.0
UNSCALE = 1.0 / (A_SCALE * W_SCALE)
EPS = 1e-5
PASSES = [(0, 0), (0, 1), (1, 0)]

EC, ER = 128, E // 128
NCH = 384
SEG = 12
RING = 6
SHARE = 4
BASE = 4096.0
HS = N // 2
HW = 314
ONE_COL = 626
Q_BANKS = [(2, 3), (0, 1)]
PER_SEG = 1 + SEG - SEG // SHARE
EXACT = 2048


class Own:

    def __init__(self, eng, sem):
        self.eng, self.sem, self.base, self.k = eng, sem, 0, 0

    def mark(self, ins):
        ins.then_inc(self.sem, 1)
        self.k += 1
        return self.base + self.k

    def after(self, mark):
        self.eng.wait_ge(self.sem, mark)

    def step(self, ins):
        self.after(self.mark(ins))

    @contextmanager
    def loop(self, count, marks):
        base = self.base + self.k
        with self.eng.Fori(0, count) as i:
            self.base, self.k = i * marks + base, 0
            yield i
            assert self.k == marks, (self.k, marks)
        self.base, self.k = base + count * marks, 0


class Banks:

    def __init__(self, full, free):
        self.full, self.free, self.before, self.uses, self.count = full, free, {}, {}, [0] * 8

    def stage(self, name, uses):
        self.before[name], self.uses[name] = list(self.count), uses
        for b, n in uses.items():
            self.count[b] += n

    def acquire(self, eng, stage, b, k):
        eng.wait_ge(self.free[b], k + (self.before[stage][b] + 1))

    def filled(self, eng, stage, b, k):
        eng.wait_ge(self.full[b], k + (self.before[stage][b] + 1))

    def emptied(self, eng, stage, b, k):
        eng.wait_ge(self.free[b], k + (self.before[stage][b] + 2))

    def after_products(self, eng, stage):
        for b, n in self.uses[stage].items():
            eng.wait_ge(self.full[b], self.before[stage][b] + n)

    def after_evacuation(self, eng, stage):
        for b, n in self.uses[stage].items():
            eng.wait_ge(self.free[b], self.before[stage][b] + n + 1)


def gps_two_layers(nc, t, out):
    ctx = ExitStack()
    with ctx:
        top = nc.sbuf_base + 31
        top -= top % 32
        start = {}

        def region(name, size):
            nonlocal top
            start[name] = top
            top += size + (-size) % 32
            assert top <= nc.sbuf_usable_end, (name, top)

        def at(name, shape, dt, where, offset=0):
            return nc.alloc_sbuf_tensor_at(name, shape, dt, offset=start[where] + offset)

        for name, size in (("X", 20480), ("XN", 20480), ("XK", 20480), ("MT", 20480), ("XT", 20480),
                           ("AT", 50016), ("W", 24576), ("STG", 16384), ("BC", 12288), ("C", 7168)):
            region(name, size)
        X = at("X", [TP, NT, D], F32, "X")
        XN = at("XN", [TP, NT, D], F32, "XN")
        XK = at("XK", [TP, 2, NT, D], F16, "XK")
        XT = at("XT", [128, 2, KT, N], F16, "XT")
        MT = at("MT", [128, 2, KT, N], F16, "MT")
        AT = at("AT", [TP, 2, NT, N], F16, "AT")
        W = [at(f"W{s}", [128, 2, 2048], F16, "W", 8192 * s) for s in range(3)]
        STG = [at(f"STG{s}", [128, 2048], F32, "STG", 8192 * s) for s in range(2)]

        def rows(s):
            return W[s][:, :, :].rearrange("p a (k o) -> p a k o", k=KT)

        BC = at("BC", [TP, 6, D], F32, "BC")
        BQ, BV, BIAS, GAMMA, BETA, BPROJ = (BC[:, n, :] for n in range(6))
        QT = at("QT", [128, KT, N], F32, "XN")
        EK = at("EK", [TP, NT, D], F32, "AT")
        V = at("V", [TP, NT, KT, 130], F32, "AT", 20480)
        QW = at("QW", [TP, 2, 2, D], F32, "AT", 20480)
        CTX = at("CTX", [128, KT, 128], F32, "AT", 41280)
        KTOP = at("KTOP", [TP, D], F32, "AT", 43328)
        KDIAG = at("KDIAG", [128, KT, 128], F32, "AT", 45376)
        IDX = at("IDX", [128, 2, 3, EC], I32, "MT", 17408)
        IDXF = at("IDXF", [128, 2, 3, EC], F32, "MT")
        SRC, SRCV, DST, SRCB = (at(n, [128, NCH], F32, "MT", 5024 + 1536 * k) for k, n in enumerate(("SRC", "SRCV", "DST", "SRCB")))
        DREL = at("DREL", [128, 2, NCH], F16, "MT", 11168)
        I2 = at("I2", [TP, 2, 2, HW], I32, "MT")
        TMP = at("TMP", [128, 3, EC], F32, "MT", 12704)
        ONEHOT_D = at("ONEHOT_D", [128, 2, SEG, 128], F16, "MT", 14240)
        ONEHOT_S = at("ONEHOT_S", [128, RING, 2 * HW], F16, "XN")
        AWAY = at("AWAY", [128, ONE_COL], F32, "XN", 7552)
        ACC = [at(f"ACC{n}", [TP, 2, 2 * HW], F32, "XN", 10080 + 5024 * n) for n in range(2)]
        ACCI = [at(f"ACCI{n}", [TP, 2, 2 * HW], I32, "XN", 10080 + 5024 * n) for n in range(2)]
        RANGE = at("RANGE", [128, 2, 3, NT, 3], F32, "AT", 47424)
        LH = at("LH", [TP, 2, 2 * HW], I32, "W", 16384)
        DG = at("DG", [128, N], F32, "XN")
        DIAG = at("DIAG", [TP, NT, TP], F32, "XN", 5024)
        MTMP = at("MTMP", [128, 2, 3, 418], F32, "XN", 10048)
        STEPS = at("STEPS", [1, NT, 32], F32, "AT", 48160)
        HT = at("HT", [128, 2, FT, N], F16, "XN")
        GATED = at("GATED", [128, 3, 418], F32, "XN", 55008)
        WD = at("WD", [128, 2, FT, D], F16, "W")
        GU = at("GU", [128, 2, 2, 2, KT * 128], F16, "BC")
        MAG = at("MAG", [128, 3, 512], F32, "AT", 25024)
        TERN = at("TERN", [128, 3, 512], F16, "AT", 31168)
        QUANT = at("QUANT", [128, 2, 3, 512], F32, "AT", 34240)
        XN2 = at("XN2", [TP, NT, D], F32, "AT", 25024)
        G = at("G", [128, KT, N], F32, "AT")
        QP = at("QP", [128, KT, N], F32, "AT", 20000)
        PTMP = at("PTMP", [128, 3, 418], F32, "AT", 40000)
        OW = at("OW", [TP, 2, D], F32, "AT", 45024)
        QF = at("QF", [128, KT, N], F32, "XK")
        KF = at("KF", [128, KT, N], F32, "MT")
        KP = at("KP", [TP, NT, D], F32, "XK")
        V1 = at("V1", [TP, NT, D], F32, "XN")
        PB = at("PB", [128, KT, 128], F32, "BC")
        KVB = at("KVB", [128, KT, 128], F32, "BC", 2048)
        ZB = at("ZB", [128, KT, 2], F32, "BC", 4096)
        IDNS = at("IDNS", [128, 128], F32, "BC", 4128)
        WG = at("WG", [128, KT * NE], F32, "BC", 4640)
        WGS = at("WGS", [128, 2, KT, NE], F16, "BC", 4896)
        GSTATS = at("GSTATS", [128, KT, 3, 6], F32, "BC", 5152)
        GMV = at("GMV", [128, KT, 2], F32, "BC", 5440)
        GCOL = at("GCOL", [128, 4, KT], F32, "BC", 5472)
        ZERO = at("ZERO", [128, 512], F32, "STG", 1536 * 4)
        XET = at("XET", [128, 2, 2, KT, CAP], F16, "XK")
        XE = at("XE", [CT, 2, 3, D], F32, "MT")
        HTMP = at("HTMP", [128, 2, 2 * CAP], F32, "AT")
        HH = at("HH", [128, 2, 2, 2, CAP], F16, "AT", 4992)
        EO = at("EO", [CT, 2, 3, D], F32, "AT", 9984)
        GATHER = at("GATHER", [TP, 4, D], F32, "AT", 22272)
        ROUTE = at("ROUTE", [TP, 12, NT, NE], F32, "AT", 30464)
        CARRY = at("CARRY", [TP, NT + 1, 2 * NE], F32, "AT", 38144)
        MASK = at("MASK", [TP, NT, 2, NE], F16, "AT", 39584)
        TOK = at("TOK", [TP, 12, NT], F32, "AT", 40224)
        SIDX = at("SIDX", [TP, 2, NT], I32, "AT", 40736)
        GIDX = at("GIDX", [TP, 2, NT], I32, "AT", 40832)
        EBASE = at("EBASE", [TP, 2, NE], F32, "AT", 40928)
        DUMP = at("DUMP", [TP, 2, NT], F32, "AT", 41088)
        slots_in = nc.dram_tensor("slots_in", [SLOTS + 2 * N, D], F32).ap()
        slots_out = nc.dram_tensor("slots_out", [SLOTS, D], F32).ap()
        counts_low_kept = nc.dram_tensor("counts_low_kept", [TP, NT, N], F16).ap()
        used = [0]

        def small(name, shape, dt):
            size = mybir.dt.size(dt) if hasattr(mybir.dt, "size") else {F32: 4, F16: 2, I32: 4}[dt]
            for n in shape[1:]:
                size *= n
            x = at(name, shape, dt, "C", used[0])
            used[0] += size + (-size) % 32
            assert used[0] <= 7168, name
            return x

        IDN = small("IDN", [128, 128], F32)
        ONES = small("ONES", [128, 128], F32)
        ONES16 = small("ONES16", [128, 128], F16)
        TRI16 = small("TRI16", [128, 128], F16)
        IOTA_S = small("IOTA_S", [128, ONE_COL], F16)
        IOTA_D = small("IOTA_D", [128, 128], F16)
        STATS = small("STATS", [TP, NT, 6], F32)
        MV = small("MV", [TP, NT, 2], F32)
        STD = small("STD", [TP, NT], F32)
        RSTD = small("RSTD", [TP, NT], F32)
        SM8 = small("SM8", [TP, 2, 3, H], F32)
        COL = small("COL", [128, 8, KT], F32)
        KSUM3 = small("KSUM3", [128, KT, 3], F32)
        KMX = small("KMX", [128, 3], F32)
        BK, BL, G1, B1, KMAX, KBIAS, KSUM, KREC = (COL[:, n, :] for n in range(8))
        VALUES = small("VALUES", [128, SEG], F32)
        FAR = small("FAR", [1, 2], F32)
        FARI = small("FARI", [1, 1], I32)
        DEG = small("DEG", [TP, NT], F32)
        RDEG = small("RDEG", [TP, NT], F32)
        THR = small("THR", [128, NT], F32)
        CID = small("CID", [128, 2, 3], F32)
        RED = small("RED", [128, 2, 3], F32)
        LOHI = small("LOHI", [128, 2, NT], F32)
        LOHIR = small("LOHIR", [128, 2, NT], F32)
        PLAN = small("PLAN", [1, 3, NT + 1], F32)
        MULT = small("MULT", [1, 32], F32)
        PLANI = small("PLANI", [1, 3, NT + 1], I32)
        EPSC = small("EPSC", [128, 1], F32)
        EPSA = small("EPSA", [128, 1], F32)
        EPSW = small("EPSW", [128, 1], F32)
        PS = ctx.enter_context(nc.psum_tensor("PS", [128, 8, 512], F32))
        B = [PS[:, b, :] for b in range(8)]

        def sem(name):
            return ctx.enter_context(nc.semaphore(name))

        bank_full = [sem(f"bank{b}_full") for b in range(8)]
        bank_free = [sem(f"bank{b}_free") for b in range(8)]
        bk = Banks(bank_full, bank_free)
        stages = [
            ("ln0_T", {0: 5, 1: 5}), ("mix_k", {6: 5, 7: 5}), ("mix_kmax", {4: 1}), ("edges", {0: 1, 1: 1}), ("mix_kbias", {7: 1}), ("mix_q", {2: 3, 3: 3, 0: 2, 1: 2}), ("mix_qT", {4: 5, 5: 5}),
            ("mix_v", {0: 5, 1: 5}), ("mix_ctx", {6: 1, 7: 1}), ("mix_out", {2: 5, 3: 5}),
            ("counts_T", {0: 10, 1: 10, 2: 10}),
            ("deg0", {0: 1, 1: 1, 2: 1}), ("agg0", {b: 2 for b in range(6)}), ("scale0", {6: 2, 7: 1}), ("gnn0", {6: 5, 7: 5}),
            ("ln1_T", {0: 5, 1: 5}), ("ffn_scale", {6: 2 * (FT - 1), 7: FT - 1}), ("ffn", {b: FT for b in range(6)}),
            ("down", {6: 5, 7: 5}), ("ln2_T", {2: 5, 3: 5}), ("deg1", {0: 1, 1: 1, 2: 1}), ("agg1", {b: 2 for b in range(6)}),
            ("gnn1", {b: 2 for b in range(6)}), ("qk1", {b: 4 for b in range(6)}), ("v1", {6: 5, 7: 5}),
            ("phi_q", {b: 2 for b in range(6)}), ("phi_k", {6: 5, 7: 5}), ("kv", {0: 1, 1: 1}), ("att", {2: 5, 3: 5}),
            ("z", {4: 5, 5: 5}), ("att_T", {6: 5, 7: 5}), ("proj", {0: 5, 1: 5}), ("ln3_T", {2: 5, 3: 5}),
            ("gate", {4: 1}), ("places", {5: 1, 6: 1}), ("slots_T", {0: NE, 1: NE, 2: NE}), ("hidden", {3: NE, 4: NE}),
            ("expert", {5: NE, 6: NE, 7: NE}),
        ]
        for s in stages:
            bk.stage(*s)
        x_loaded = [sem(f"x_loaded{n}") for n in range(2)]
        small_loaded = sem("small_loaded")
        consts_made = sem("consts_made")
        staged = [sem(f"staged{s}") for s in range(2)]
        high_split = sem("high_split")
        weight_ready = sem("weight_ready")
        stored = sem("stored")
        dve_own, act_own, pool_own = sem("dve_own"), sem("act_own"), sem("pool_own")
        std_ready, xn_ready, xk_high, xk_low, xt_high = (
            sem("std_ready"), sem("xn_ready"), sem("xk_high"), sem("xk_low"), sem("xt_high"))
        var_ready = sem("var_ready")
        q_shifted, q_exp, q_soft = sem("q_shifted"), sem("q_exp"), sem("q_soft")
        k_seen, kdiag_ready, kbias_ready, k_shifted, k_exp = (
            sem(n) for n in ("k_seen", "kdiag_ready", "kbias_ready", "k_shifted", "k_exp"))
        edges_loaded, edges_float = sem("edges_loaded"), sem("edges_float")
        lohi_local, lohi_all, plan_ready = sem("lohi_local"), sem("lohi_all"), sem("plan_ready")
        dve_free = sem("dve_free")
        onehot_ready, onehot_free, away_ready, act_onehot_ready = (
            sem(n) for n in ("onehot_ready", "onehot_free", "away_ready", "act_onehot_ready"))
        seg_int, lohi_ready, acc_added = sem("seg_int"), sem("lohi_ready"), sem("acc_added")
        counts_high, deg_ready, diag_ready = sem("counts_high"), sem("deg_ready"), sem("diag_ready")
        mean_raw, mean_high, mean_ready = sem("mean_raw"), sem("mean_high"), sem("mean_ready")
        x1_ready = sem("x1_ready")
        beta_added, gnn_var, gnn_std = sem("beta_added"), sem("gnn_var"), sem("gnn_std")

        qkv = t["L1_mix_w_qkv"]
        units = [t["L0_mix_WkT"], t["L0_mix_WqT"], t["L0_mix_WvT"], t["L0_gnn_W_selfT"], t["L0_gnn_W_neighT"],
                 t["L1_gnn_W_lT"], t["L1_gnn_W_rT"], qkv[:, 0:D], qkv[:, D:2 * D], qkv[:, 2 * D:], t["L1_mix_w_proj"]]
        NU = len(units)
        unit_slot = [0, 1, 2, 0, 1, 0, 1, 2, 0, 1, 2]
        last_use = {3: "mix_k", 4: "mix_q", 5: "down", 6: "down", 7: "down", 8: "gnn1", 9: "gnn1", 10: "qk1"}

        def stage_slot(n):
            return n % 2 if n < 5 else (n + 1) % 2

        def staged_count(n):
            return 16 * sum(stage_slot(m) == stage_slot(n) for m in range(min(n, NU) + 1)) if n < NU else None

        def plan(eng, T):
            lo = eng.value_load(PLANI[0:1, 0, T:T + 1], min_val=0, max_val=ER)
            n = eng.value_load(PLANI[0:1, 1, T:T + 1], min_val=1, max_val=(ER + SEG) // SEG + 1)
            before = eng.value_load(PLANI[0:1, 2, T:T + 1], min_val=0, max_val=NT * ((ER + SEG) // SEG + 1))
            return lo, n, before

        ffn_staged = [sem(f"ffn_staged{n}") for n in range(2)]
        magnitude, scales, ternary, quantised, ffn_high, ffn_low = (
            sem(n) for n in ("magnitude", "scales", "ternary", "quantised", "ffn_high", "ffn_low"))
        far_known = sem("far_known")
        gate_silu, hidden_high, counts_spilled, counts_back, wide_own = (
            sem(n) for n in ("gate_silu", "hidden_high", "counts_spilled", "counts_back", "wide_own"))
        gnn1_var, gnn1_std, gnn1_done, phi_min, phi_exp, kmin, kexp, att_ready, bproj_added = (
            sem(n) for n in ("gnn1_var", "gnn1_std", "gnn1_done", "phi_min", "phi_exp", "kmin", "kexp", "att_ready", "bproj_added"))
        route_loaded, route_consts, wg_high, wg_ready, gate_exp_in, gate_exp, masks_ready, places_ready = (
            sem(n) for n in ("route_loaded", "route_consts", "wg_high", "wg_ready", "gate_exp_in", "gate_exp", "masks_ready", "places_ready"))
        zero_made, zero_stored, scattered, slots_high, relu_made, relu_high, relu_low = (
            sem(n) for n in ("zero_made", "zero_stored", "scattered", "slots_high", "relu_made", "relu_high", "relu_low"))
        slots_loaded = [sem(f"slots_loaded{n}") for n in range(2)]
        outs_stored = [sem(f"outs_stored{n}") for n in range(2)]
        gathered = [sem(f"gathered{n}") for n in range(4)]
        half_added, y_ready = sem("half_added"), sem("y_ready")

        prescaled, expert_prescaled = sem("prescaled"), sem("expert_prescaled")
        hidden_done = sem("hidden_done")

        def expert_staged(e, par):
            slot = (par + NU + 1) % 2
            return 16 * sum(stage_slot(m) == slot for m in range(NU)) + 32 * (e // 2 + 1)

        def stored_count(e, par):
            return 16 * (e // 2)

        def scale_use(n, a):
            stage, n = ("scale0", 0) if isinstance(n, int) and n == 0 else ("ffn_scale", n - 1)
            return (stage, 7, n) if a == 1 else (stage, 6, n * 2 + a // 2)

        block = ctx.enter_context(nc.Block())

        @block.sync
        def _(sp):
            for n in range(2):
                sp.dma_start(X[:, 5 * n:5 * n + 5, :], t["x"].rearrange("(t p) d -> p t d", p=TP)[:, 5 * n:5 * n + 5, :])\
                  .then_inc(x_loaded[n], 16)
            def load_weight(n):
                sl = stage_slot(n)
                sp.dma_start(STG[sl][:, :].rearrange("p (k o) -> p k o", k=KT), units[n].rearrange("(k p) o -> p k o", p=128))\
                  .then_inc(staged[sl], 16)

            load_weight(0)
            for dst, name in ((BQ, "L0_mix_bq"), (BV, "L0_mix_bv"), (BIAS, "L0_gnn_bias"), (GAMMA, "L0_gnn_gamma"),
                              (BETA, "L0_gnn_beta"), (BPROJ, "L1_mix_b_proj")):
                sp.dma_start(dst, t[name].partition_broadcast(TP)).then_inc(small_loaded, 16)
            for dst, name in ((BK, "L0_mix_bkC"), (BL, "L1_gnn_b_lC"), (G1, "L1_gnn_gammaC"), (B1, "L1_gnn_betaC")):
                sp.dma_start(dst, t[name]).then_inc(small_loaded, 16)
            load_weight(1)
            sp.wait_ge(edges_loaded, 1)
            for a, name in enumerate(("src", "dst")):
                e = t[name]
                sp.dma_start(IDX[:, a, 0:2, :], e[0:256 * EC].rearrange("(g p e) -> p g e", p=128, e=EC)).then_inc(edges_loaded, 16)
                sp.dma_start(IDX[0:ER - 256, a, 2, :], e[256 * EC:ER * EC].rearrange("(p e) -> p e", e=EC)).then_inc(edges_loaded, 16)
                sp.dma_start(IDX[ER - 256:ER - 255, a, 2, 0:E - ER * EC], e[ER * EC:E].rearrange("(p e) -> p e", p=1)).then_inc(edges_loaded, 16)

            for n in (2, 3, 4):
                sp.wait_ge(weight_ready, n - 1)
                load_weight(n)
            wide = [t[x].rearrange("(k p) f -> p k f", p=128) for x in ("L0_ffn_w_gateT", "L0_ffn_w_upT")]
            for n in range(FT):
                if n == 2:
                    bk.after_evacuation(sp, "counts_T")
                    sp.dma_start(counts_low_kept, AT[:, 1, :, :]).then_inc(counts_spilled, 16)
                if n < 2:
                    sp.wait_ge(weight_ready, 4 + n)
                else:
                    sp.wait_ge(ternary, n - 1)
                st = STG[(n + 1) % 2]
                for a in range(2):
                    sp.dma_start(st[:, a * 512:(a + 1) * 512].rearrange("p (k f) -> p k f", k=KT), wide[a][:, :, n * 128:(n + 1) * 128])\
                      .then_inc(ffn_staged[n % 2], 16)
                sp.dma_start(st[:, 1024:1536], t["L0_ffn_w_downT"][n * 128:(n + 1) * 128, :]).then_inc(ffn_staged[n % 2], 16)
                if n == 3:
                    sp.wait_ge(zero_made, 1)
                    sp.dma_start(slots_in[0:SLOTS, :].rearrange("(p r) d -> p r d", p=128),
                                 ZERO[:, :].unsqueeze(1).to_broadcast([128, SLOTS // 128, D])).then_inc(zero_stored, 16)
            sp.wait_ge(zero_stored, 16)
            for n in (5, 6):
                sp.wait_ge(ternary, FT - 1 + n - 5)
                load_weight(n)
            bk.after_products(sp, "ffn")
            sp.dma_start(WG[:, :].rearrange("p (k e) -> p k e", k=KT), t["L1_ffn_w_gating"].rearrange("(k p) e -> p k e", p=128)).then_inc(route_loaded, 16)
            sp.wait_ge(wide_own, 1)
            for h in range(H):
                p = slice(64 * (h % 2), 64 * (h % 2) + 64)
                sp.dma_start(PB[p, h // 2, p], t["L1_mix_proj_mat"][h, :, :]).then_inc(route_loaded, 16)
            bk.after_products(sp, "ln2_T")
            sp.wait_ge(xk_low, 2 * NT)
            far = sp.value_load(FARI[0:1, 0:1], min_val=0, max_val=1)
            with sp.If(far == 1):
                sp.dma_start(AT[:, 1, :, :], counts_low_kept).then_inc(counts_back, 16)
            for n in range(7, NU):
                sp.wait_ge(weight_ready, n - 1)
                load_weight(n)

            def load_expert(e, par):
                st = STG[(par + NU + 1) % 2]
                sp.wait_ge(weight_ready, e + (NU - 1))
                sp.dma_start(st[:, 0:1024].rearrange("p (k h) -> p k h", k=KT), t["L1_ffn_w1"][ds(e, 1), :, :].rearrange("a (k p) h -> p (a k) h", p=128))\
                  .then_inc(staged[(par + NU + 1) % 2], 16)
                sp.dma_start(st[:, 1024:2048].rearrange("p (k d) -> p k d", k=2), t["L1_ffn_w2"][ds(e, 1), :, :].rearrange("a (k p) d -> p (a k) d", p=128))\
                  .then_inc(staged[(par + NU + 1) % 2], 16)

            def load_slots(e, par):
                if not isinstance(e, int):
                    bk.filled(sp, "slots_T", 2, e - 2)
                sp.dma_start(XE[:, par, :, :], slots_in[ds(e * CAP, CAP), :].rearrange("(c p) d -> p c d", p=CT)).then_inc(slots_loaded[par], 16)

            def store_slots(e, par):
                bk.emptied(sp, "expert", 7, e)
                sp.dma_start(slots_out[ds(e * CAP, CAP), :].rearrange("(c p) d -> p c d", p=CT), EO[:, par, :, :]).then_inc(outs_stored[par], 16)

            for par in range(2):
                load_expert(par, par)
            sp.wait_ge(scattered, 16 * 2 * NT)
            for par in range(2):
                load_slots(par, par)
            with sp.Fori(0, NE // 2 - 1) as i:
                for par in range(2):
                    load_expert(i * 2 + (par + 2), par)
                    load_slots(i * 2 + (par + 2), par)
                    store_slots(i * 2 + par, par)
            for par in range(2):
                store_slots(NE - 2 + par, par)
            for i in range(NT):
                sp.wait_ge(y_ready, i + 1)
                sp.dma_start(out[i * TP:(i + 1) * TP, :], X[:, i, :]).then_inc(stored, 16)
            sp.wait_ge(stored, 16 * NT)

        @block.gpsimd
        def _(pool):
            g = nc.gpsimd
            own = Own(pool, pool_own)
            g.memset(IDX[:, :, 2, :], -1).then_inc(edges_loaded, 1)
            own.step(g.memset(IDN[:, :], 0.0))
            g.affine_select(out=IDN[:, :], in_=IDN[:, :], compare_op=ALU.not_equal, fill=1.0, base=0,
                            pattern=[[-1, 128]], channel_multiplier=1).then_inc(consts_made, 1)
            g.memset(ONES[:, :], 1.0).then_inc(consts_made, 1)
            g.memset(ONES16[:, :], 1.0).then_inc(consts_made, 1)
            pool.wait_ge(consts_made, 3)
            g.affine_select(out=TRI16[:, :], in_=ONES16[:, :], compare_op=ALU.is_gt, fill=0.0, base=0,
                            pattern=[[1, 128]], channel_multiplier=-1).then_inc(consts_made, 1)
            g.iota(IOTA_S[:, :], [[1, ONE_COL]], base=0, channel_multiplier=0, allow_small_or_imprecise_dtypes=True)\
             .then_inc(consts_made, 1)
            g.iota(IOTA_D[:, :], [[1, 128]], base=0, channel_multiplier=0, allow_small_or_imprecise_dtypes=True)\
             .then_inc(consts_made, 1)
            own.step(g.memset(EPSC[:, :], EPS))
            g.memset(EPSA[:, :], EPS / A_SCALE ** 2).then_inc(consts_made, 1)
            g.memset(EPSW[:, :], EPS * W_SCALE).then_inc(consts_made, 1)
            g.iota(MULT[:, :], [[SEG, 32]], base=0, channel_multiplier=0, allow_small_or_imprecise_dtypes=True).then_inc(consts_made, 1)
            g.iota(THR[:, :], [[TP, NT]], base=0, channel_multiplier=0, allow_small_or_imprecise_dtypes=True).then_inc(consts_made, 1)
            g.iota(CID[:, 0, :], [[-128, 3]], base=512, channel_multiplier=-1, allow_small_or_imprecise_dtypes=True).then_inc(consts_made, 1)
            g.iota(CID[:, 1, :], [[128, 3]], base=1, channel_multiplier=1, allow_small_or_imprecise_dtypes=True).then_inc(consts_made, 1)

            def prescale(n):
                st = STG[stage_slot(n)]
                pool.wait_ge(staged[stage_slot(n)], staged_count(n))
                g.tensor_scalar(st[:, :], st[:, :], W_SCALE, 1.0, ALU.mult, ALU.mult).then_inc(prescaled, 1)

            def split_low(n):
                prescale(n)
                pool.wait_ge(high_split, n + 1)
                w = W[unit_slot[n]]
                g.tensor_tensor(w[:, 1, :], STG[stage_slot(n)][:, :], w[:, 0, :], ALU.subtract)\
                 .then_inc(weight_ready, 1)

            def keep_low(done, XN):
                with pool.Fori(0, NT) as i:
                    pool.wait_ge(xk_high, i + (done + 1))
                    g.tensor_tensor(XK[:, 1, ds(i, 1), :], XN[:, ds(i, 1), :], XK[:, 0, ds(i, 1), :], ALU.subtract).then_inc(xk_low, 1)

            split_low(0)
            keep_low(0, XN)
            split_low(1)
            pool.wait_ge(kbias_ready, 1)
            with pool.Fori(0, NT) as i:
                g.tensor_tensor(EK[:, ds(i, 1), :], EK[:, ds(i, 1), :], KTOP[:, :].unsqueeze(1), ALU.add).then_inc(k_shifted, 1)
            for n in (2, 3, 4):
                split_low(n)
            pool.wait_ge(lohi_local, 1)
            g.partition_all_reduce(LOHIR[:, :, :].rearrange("p a t -> p (a t)"), LOHI[:, :, :].rearrange("p a t -> p (a t)"), 128,
                                   bass.bass_isa.ReduceOp.max).then_inc(lohi_all, 1)
            bk.after_evacuation(pool, "mix_out")
            with pool.Fori(0, NT) as i:
                g.tensor_tensor(X[:, ds(i, 1), :], X[:, ds(i, 1), :], BETA.unsqueeze(1), ALU.add).then_inc(beta_added, 1)
            pool.wait_ge(plan_ready, 1)
            pool.sem_inc(acc_added, 2)
            for T in range(NT):
                _, n, before = plan(pool, T)
                acc = ACCI[T % 2]
                if T >= 2:
                    bk.filled(pool, "counts_T", 2, T - 2)
                own.step(g.memset(acc[:, :, :], 0))
                with pool.Fori(0, n) as i:
                    pool.wait_ge(lohi_ready, before + i + 4)
                    pool.wait_ge(acc_added, before + i + 2)
                    g.tensor_tensor(acc[:, :, :], acc[:, :, :], LH[:, :, :], ALU.add).then_inc(acc_added, 1)
                pool.wait_ge(acc_added, before + n + 2)
                ones = acc[:, :, ONE_COL:ONE_COL + 1]
                own.step(g.tensor_tensor(ones[:, 0, :], ones[:, 0, :], ones[:, 1, :], ALU.add))
                own.step(g.tensor_copy(DEG[:, T:T + 1], ones[:, 0, :]))
                g.tensor_copy(ACC[T % 2][:, :, :], acc[:, :, :]).then_inc(deg_ready, 1)

            g.memset(ZERO[:, :], 0.0).then_inc(zero_made, 1)

            def quantise(n, par):
                pool.wait_ge(ternary, n + 1)
                g.tensor_tensor(QUANT[:, par, :, :], TERN[:, :, :], QUANT[:, par, :, :], ALU.mult)\
                 .then_inc(quantised, 1)

            def quantised_low(n, par):
                pool.wait_ge(ffn_high, n * 2 + 2)
                own.mark(g.tensor_tensor(GU[:, par, :, 1, :], QUANT[:, par, 0:2, :], GU[:, par, :, 0, :], ALU.subtract))
                g.tensor_tensor(WD[:, 1, ds(n, 1), :], QUANT[:, par, 2:3, :], WD[:, 0, ds(n, 1), :], ALU.subtract).then_inc(ffn_low, 1)

            quantise(0, 0)
            quantise(1, 1)
            quantised_low(0, 0)
            with own.loop(4, 2) as i:
                for u in range(2):
                    quantised_low(i * 2 + (u + 1), 1 - u)
                    quantise(i * 2 + (u + 2), u)
            quantised_low(9, 1)
            quantise(10, 0)
            quantised_low(10, 0)

            bk.after_products(pool, "ffn")
            own.step(g.memset(IDNS[:, :], 0.0))
            own.mark(g.affine_select(out=IDNS[:, :], in_=IDNS[:, :], compare_op=ALU.not_equal, fill=A_SCALE * W_SCALE, base=0,
                                     pattern=[[-1, 128]], channel_multiplier=1))
            own.mark(g.memset(ZB[:, :, :], 0.0))
            own.step(g.memset(KVB[:, :, :], 0.0))
            g.memset(PB[:, :, :], 0.0).then_inc(wide_own, 1)
            keep_low(NT, XN2)
            pool.wait_ge(xn_ready, 3 * NT)
            with pool.Fori(0, NT) as i:
                g.tensor_tensor(X[:, ds(i, 1), :], X[:, ds(i, 1), :], BPROJ.unsqueeze(1), ALU.add).then_inc(bproj_added, 1)
            for n in range(5, NU):
                split_low(n)
            bk.after_products(pool, "proj")
            g.iota(EBASE[:, 0, :], [[CAP, NE]], base=0, channel_multiplier=0, allow_small_or_imprecise_dtypes=True).then_inc(route_consts, 1)
            g.iota(EBASE[:, 1, :], [[-1, NE]], base=NE, channel_multiplier=0, allow_small_or_imprecise_dtypes=True).then_inc(route_consts, 1)
            g.iota(DUMP[:, :, :], [[1, 2], [2 * TP, NT]], base=SLOTS, channel_multiplier=2, allow_small_or_imprecise_dtypes=True).then_inc(route_consts, 1)

            def expert_low(e, par):
                pool.wait_ge(high_split, e + (NU + 1))
                g.tensor_tensor(W[par][:, 1, :], STG[(par + NU + 1) % 2][:, :], W[par][:, 0, :], ALU.subtract)\
                 .then_inc(weight_ready, 1)

            expert_low(0, 0)
            expert_low(1, 1)
            pool.wait_ge(places_ready, 2)
            pool.wait_ge(zero_stored, 16)
            for i in range(NT):
                for c in range(2):
                    g.indirect_dma_start(out=slots_in, out_offset=bass.IndirectOffsetOnAxis(ap=SIDX[:, c, i:i + 1], axis=0),
                                         in_=XN[:, i, :], in_offset=None).then_inc(scattered, 16)
            with pool.Fori(0, NE // 2 - 1) as i:
                for u in range(2):
                    expert_low(i * 2 + (u + 2), u)
            for u in range(2):
                pool.wait_ge(outs_stored[u], 16 * (NE // 2))
            for n in range(2 * NT):
                if n >= 4:
                    pool.wait_ge(half_added if n % 2 == 0 else y_ready, (n - 4) // 2 + 1)
                g.indirect_dma_start(out=GATHER[:, n % 4, :], out_offset=None, in_=slots_out,
                                     in_offset=bass.IndirectOffsetOnAxis(ap=GIDX[:, n % 2, n // 2:n // 2 + 1], axis=0))\
                 .then_inc(gathered[n % 4], 16)

        @block.scalar
        def _(act):
            s = nc.scalar
            own = Own(act, act_own)

            def split_high(n):
                act.wait_ge(prescaled, n + 1)
                if n in last_use:
                    bk.after_products(act, last_use[n])
                s.activation(W[unit_slot[n]][:, 0, :], STG[stage_slot(n)][:, :], ACT.Copy).then_inc(high_split, 1)

            def std_of(n, half, ready):
                rows = slice(half * NT // 2, (half + 1) * NT // 2)
                s.activation(STD[:, rows], MV[:, rows, 1], ACT.Sqrt, bias=EPSA[:TP, :], scale=A_SCALE ** -2).then_inc(ready, 1)

            def keep_high(n, XN=XN):
                with act.Fori(0, NT // 2) as i:
                    act.wait_ge(xn_ready, i + n)
                    s.activation(XK[:, 0, ds(i + (n - 1) % NT, 1), :], XN[:, ds(i + (n - 1) % NT, 1), :], ACT.Copy).then_inc(xk_high, 1)

            def transposed_high(stage, banks):
                with act.Fori(0, NT // 2) as i:
                    for u in range(2):
                        bk.filled(act, stage, banks[u], i)
                        s.activation(XT[:, 0, :, ds(i * (2 * TP) + u * TP, TP)],
                                     B[banks[u]][:, 0:KT * TP].rearrange("p (k n) -> p k n", k=KT), ACT.Copy).then_inc(xt_high, 1)

            def stds(n):
                for half in range(2):
                    act.wait_ge(var_ready, 2 * n + half + 1)
                    std_of(n, half, std_ready)

            act.wait_ge(consts_made, 12)
            act.wait_ge(var_ready, 1)
            std_of(0, 0, std_ready)
            act.wait_ge(var_ready, 2)
            std_of(0, 1, std_ready)
            split_high(0)
            transposed_high("ln0_T", (0, 1))
            keep_high(1)
            keep_high(NT // 2 + 1)
            split_high(1)

            with act.Fori(0, NT // 2) as i:
                for u in range(2):
                    act.wait_ge(k_seen, i * 2 + (u + 2))
                    s.activation(EK[:, ds(i * 2 + u, 1), :], B[6 + u][:TP, :].unsqueeze(1), ACT.Copy, scale=UNSCALE).then_inc(bank_free[6 + u], 1)
            act.wait_ge(edges_loaded, 97)
            s.activation(IDXF[:, :, :, :], IDX[:, :, :, :], ACT.Copy).then_inc(edges_float, 1)
            bk.filled(act, "mix_kbias", 7, 0)
            s.activation(KTOP[:, :], B[7][:TP, :], ACT.Copy).then_inc(kbias_ready, 1)
            act.wait_ge(kbias_ready, 1)
            act.sem_inc(bank_free[7], 1)
            bk.after_evacuation(act, "mix_k")

            def q_exps(i):
                for u in range(2):
                    act.wait_ge(q_shifted, i * 2 + (u + 1))
                    s.activation(QW[:, i % 2, u, :], QW[:, i % 2, u, :], ACT.Exp).then_inc(q_exp, 1)

            act.wait_ge(xk_low, NT)
            q_exps(0)
            for i in range(NT // 2):
                if i + 1 < NT // 2:
                    q_exps(i + 1)
                for u in range(2):
                    bk.filled(act, "mix_qT", 4 + u, i)
                    s.activation(QT[:, :, (2 * i + u) * TP:(2 * i + u + 1) * TP], B[4 + u][:, 0:KT * TP].rearrange("p (k n) -> p k n", k=KT), ACT.Copy)\
                     .then_inc(bank_free[4 + u], 1)
                if i == 0:
                    split_high(2)
            with act.Fori(0, NT) as i:
                act.wait_ge(k_shifted, i + 1)
                s.activation(EK[:, ds(i, 1), :], EK[:, ds(i, 1), :], ACT.Exp).then_inc(k_exp, 1)
            split_high(3)
            split_high(4)

            def counts_high_part(T):
                for b in range(3):
                    n = min(4, NT - 4 * b)
                    bk.filled(act, "counts_T", b, T)
                    s.activation(AT[:, 0, 4 * b:4 * b + n, T * TP:(T + 1) * TP], B[b][:TP, 0:n * TP].rearrange("p (s d) -> p s d", s=n),
                                 ACT.Copy).then_inc(counts_high, 1)

            def as_integers(f):
                act.wait_ge(onehot_free, f * SEG + RING)
                act.wait_ge(lohi_ready, f + 1)
                s.activation(I2[:, ds((f + 1) % 2, 1), :, :].rearrange("p a h c -> p (a h) c"),
                             PS[:TP, ds((f + 1) % 2 * 2 + 4, 2), 0:HW], ACT.Copy).then_inc(seg_int, 1)

            act.wait_ge(plan_ready, 1)
            act.sem_inc(act_onehot_ready, 1)
            bk.after_evacuation(act, "mix_out")
            for T in range(NT):
                lo, n, before = plan(act, T)
                with act.Fori(0, n) as i:
                    first = nc.s_assert_within(lo + i * SEG, 0, NCH - SEG, skip_runtime_bounds_check_because="the plan's last segment starts before the last chunk")
                    for j in range(SHARE - 1, SEG, SHARE):
                        act.wait_ge(onehot_free, (before + i) * SEG + (j + 1))
                        act.wait_ge(act_onehot_ready, (before + i) * (SEG // SHARE) + (j // SHARE + 1))
                        if j == SHARE - 1:
                            s.activation(VALUES[:, j:SEG], SRCV[:, ds(first + j, SEG - j)], ACT.Copy)
                        s.activation(AWAY[:, :], IOTA_S[:, :], ACT.Abs, bias=SRCB[:, ds(first + j, 1)], scale=SRCV[:, ds(first + j, 1)])\
                         .then_inc(away_ready, 1)
                        act.wait_ge(away_ready, (before + i) * (SEG // SHARE) + (j // SHARE + 1))
                        s.activation(ONEHOT_S[:, j % RING, 0:ONE_COL], AWAY[:, :], ACT.Relu, bias=VALUES[:, j:j + 1], scale=-1.0)\
                         .then_inc(act_onehot_ready, 1)
                        if j == SHARE - 1:
                            as_integers(before + i)
                if T:
                    counts_high_part(T - 1)
            as_integers(before + n)
            counts_high_part(NT - 1)

            def means_high(stage):
                with act.Fori(0, KT // 2) as i:
                    for u in range(2):
                        for c, (lo, n) in enumerate(CHUNKS):
                            bk.emptied(act, stage, 3 * u + c, i)
                            s.activation(MT[:, 0, ds(i * 2 + u, 1), lo:lo + n], MTMP[:, u, c:c + 1, 0:n], ACT.Copy)\
                             .then_inc(mean_high, 1)

            means_high("agg0")
            def magnitudes(n, par):
                if not (isinstance(n, int) and n == 0):
                    act.wait_ge(ternary, n)
                act.wait_ge(ffn_staged[par], (n // 2) * 48 + 48 if isinstance(n, int) else n)
                s.activation(MAG[:, :, :].rearrange("p a c -> p (a c)"), STG[(par + 1) % 2][:, 0:1536], ACT.Abs).then_inc(magnitude, 1)

            def scale_rows(n, par):
                for a in range(3):
                    b = (6, 7, 6)[a]
                    bk.filled(act, *scale_use(n, a))
                    if a == 0 and not (isinstance(n, int) and n < 2):
                        act.wait_ge(ffn_low, n - 1)
                    s.activation(QUANT[:, par, a, :], B[b][:, :], ACT.Identity, bias=EPSW[:, :], scale=W_SCALE / 128)\
                     .then_inc(bank_free[b], 1)

            def quantised_high(n, par):
                act.wait_ge(quantised, n + 1)
                s.activation(GU[:, par, :, 0, :], QUANT[:, par, 0:2, :], ACT.Copy).then_inc(ffn_high, 1)
                s.activation(WD[:, 0, ds(n, 1), :], QUANT[:, par, 2:3, :], ACT.Copy).then_inc(ffn_high, 1)

            def gates(j):
                for c, (lo, n) in enumerate(CHUNKS):
                    bk.filled(act, "ffn", c, j)
                    if not (isinstance(j, int) and j == 0):
                        act.wait_ge(hidden_done, j * 3 + (c + 1 - 3))
                    s.activation(GATED[:, c, 0:n], B[c][:, 0:n], ACT.Silu, scale=UNSCALE).then_inc(bank_free[c], 1)
                for c, (lo, n) in enumerate(CHUNKS):
                    bk.emptied(act, "ffn", 3 + c, j)
                    s.activation(HT[:, 0, ds(j, 1), lo:lo + n], GATED[:, c:c + 1, 0:n], ACT.Copy).then_inc(hidden_high, 1)

            act.wait_ge(counts_spilled, 16)
            bk.after_products(act, "agg0")
            magnitudes(0, 0)
            scale_rows(0, 0)
            magnitudes(1, 1)
            act.wait_ge(quantised, 1)
            s.activation(GU[:, 0, :, 0, :], QUANT[:, 0, 0:2, :], ACT.Copy).then_inc(ffn_high, 1)
            for half in range(2):
                act.wait_ge(gnn_var, half + 1)
                std_of(0, half, gnn_std)
                act.wait_ge(var_ready, 2 + half + 1)
                std_of(1, half, std_ready)
            bk.after_products(act, "gnn0")
            s.activation(WD[:, 0, 0:1, :], QUANT[:, 0, 2:3, :], ACT.Copy).then_inc(ffn_high, 1)
            scale_rows(1, 1)
            transposed_high("ln1_T", (0, 1))
            quantised_high(1, 1)
            magnitudes(2, 0)
            for j in range(FT):
                if j + 2 < FT:
                    scale_rows(j + 2, j % 2)
                if j + 3 < FT:
                    magnitudes(j + 3, (j + 1) % 2)
                gates(j)
                if j + 2 < FT:
                    quantised_high(j + 2, j % 2)

            stds(2)
            bk.after_products(act, "down")
            keep_high(2 * NT + 1, XN2)
            keep_high(2 * NT + NT // 2 + 1, XN2)
            transposed_high("ln2_T", (2, 3))
            split_high(5)
            split_high(6)
            means_high("agg1")
            split_high(7)
            for m in range(KT):
                for c, (lo, n) in enumerate(CHUNKS):
                    b = 3 * (m % 2) + c
                    bk.filled(act, "gnn1", b, m // 2)
                    s.activation(G[:, m, lo:lo + n], B[b][:, 0:n], ACT.Relu, bias=BL[:, m:m + 1], scale=UNSCALE).then_inc(bank_free[b], 1)
            split_high(8)
            split_high(9)
            act.wait_ge(gnn1_var, 1)
            s.activation(GCOL[:, 0, :], GMV[:, :, 1], ACT.Sqrt, bias=EPSC[:, :]).then_inc(gnn1_std, 1)
            for m in range(2 * KT):
                for c, (lo, n) in enumerate(CHUNKS):
                    b = 3 * (m % 2) + c
                    bk.filled(act, "qk1", b, m // 2)
                    s.activation((QF if m < KT else KF)[:, m % KT, lo:lo + n], B[b][:, 0:n], ACT.Copy, scale=UNSCALE)\
                     .then_inc(bank_free[b], 1)
            split_high(10)
            for m in range(KT):
                for c, (lo, n) in enumerate(CHUNKS):
                    act.wait_ge(phi_min, 3 * m + c + 1)
                    s.activation(PTMP[:, c, 0:n], PTMP[:, c, 0:n], ACT.Exp).then_inc(phi_exp, 1)
            with act.Fori(0, NT // 2) as i:
                for u in range(2):
                    act.wait_ge(kmin, i * 2 + (u + 1))
                    s.activation(OW[:, u, :], OW[:, u, :], ACT.Exp).then_inc(kexp, 1)

            def parts_T(stage, banks):
                with act.Fori(0, NT // 2) as i:
                    for u in range(2):
                        bk.filled(act, stage, banks[u], i)
                        s.activation(XT[:, 0, :, ds(i * (2 * TP) + u * TP, TP)],
                                     B[banks[u]][:, 0:KT * TP].rearrange("p (k n) -> p k n", k=KT), ACT.Copy,
                                     scale=A_SCALE).then_inc(xt_high, 1)

            parts_T("att_T", (6, 7))
            act.wait_ge(route_loaded, 16)
            s.activation(WGS[:, 0, :, :].rearrange("p k e -> p (k e)"), WG[:, :], ACT.Copy, scale=W_SCALE).then_inc(wg_high, 1)

            def expert_high(e, par):
                act.wait_ge(expert_prescaled, e + 1)
                if isinstance(e, int) and e < 2:
                    bk.after_products(act, "v1")
                else:
                    for b in (5, 6, 7):
                        bk.filled(act, "expert", b, e - 2)
                s.activation(W[par][:, 0, :], STG[(par + NU + 1) % 2][:, :], ACT.Copy).then_inc(high_split, 1)

            expert_high(0, 0)
            expert_high(1, 1)
            stds(3)
            transposed_high("ln3_T", (2, 3))
            act.wait_ge(gate_exp_in, 1)
            s.activation(ROUTE[:, 0, :, :], ROUTE[:, 0, :, :], ACT.Exp).then_inc(gate_exp, 1)

            def slots_high_parts(e, par):
                for b in range(3):
                    bk.filled(act, "slots_T", b, e)
                    s.activation(XET[:, par, 0, :, b * CT:(b + 1) * CT], B[b][:, 0:KT * CT].rearrange("p (k n) -> p k n", k=KT),
                                 ACT.Copy).then_inc(slots_high, 1)

            def relus(e, par):
                for m in range(2):
                    bk.filled(act, "hidden", 3 + m, e)
                    s.activation(HTMP[:, par, m * CAP:(m + 1) * CAP], B[3 + m][:, 0:CAP], ACT.Relu, scale=UNSCALE * A_SCALE)\
                     .then_inc(bank_free[3 + m], 1)
                for m in range(2):
                    bk.emptied(act, "hidden", 3 + m, e)
                s.activation(HH[:, par, 0, :, :].rearrange("p m c -> p (m c)"), HTMP[:, par, :], ACT.Copy).then_inc(relu_high, 1)

            def first_out(e, par):
                bk.filled(act, "expert", 5, e)
                if not (isinstance(e, int) and e < 2):
                    act.wait_ge(outs_stored[par], stored_count(e, par))
                s.activation(EO[:, par, 0, :], B[5][:CT, :], ACT.Copy, scale=UNSCALE).then_inc(bank_free[5], 1)

            slots_high_parts(0, 0)
            for e in range(NE):
                relus(e, e % 2)
                if e + 1 < NE:
                    slots_high_parts(e + 1, (e + 1) % 2)
                first_out(e, e % 2)
                if e + 2 < NE:
                    expert_high(e + 2, e % 2)

        @block.tensor
        def _(pe):
            te = nc.tensor
            for b in range(8):
                pe.sem_inc(bank_free[b], 1)
            pe.wait_ge(consts_made, 12)

            def sum_products(dst, pairs):
                for n, (a, b) in enumerate(pairs):
                    last = te.matmul(dst, a, b, start=(n == 0), stop=(n == len(pairs) - 1))
                return last

            def normed_T(stage, banks, done, XN=XN):
                for i in range(NT):
                    pe.wait_ge(xn_ready, done + i + 1)
                    bk.acquire(pe, stage, banks[i % 2], i // 2)
                    for k in range(KT):
                        last = te.transpose(B[banks[i % 2]][:, k * TP:(k + 1) * TP], XN[:, i, k * 128:(k + 1) * 128],
                                            IDN[:TP, :TP])
                    last.then_inc(bank_full[banks[i % 2]], 1)

            def by_token(stage, banks, terms, weights_done=0):
                with pe.Fori(0, NT // 2) as i:
                    for u in range(2):
                        bk.acquire(pe, stage, banks[u], i)
                        sum_products(B[banks[u]][:TP, :], [
                            (a[:, pa, k, ds(i * (2 * TP) + u * TP, TP)], w[:, pw, k, :])
                            for a, w, kt in terms for k in range(kt) for pa, pw in PASSES
                        ]).then_inc(bank_full[banks[u]], 1)

            def by_feature(stage, banks, m, terms, use):
                for c, (lo, n) in enumerate(CHUNKS):
                    bk.acquire(pe, stage, banks[c], use)
                    sum_products(B[banks[c]][:, 0:n], [
                        (w[:, pw, k, m * 128:(m + 1) * 128], a[:, pa, k, lo:lo + n])
                        for a, w in terms for k in range(KT) for pw, pa in PASSES
                    ]).then_inc(bank_full[banks[c]], 1)

            normed_T("ln0_T", (0, 1), 0)
            bk.after_evacuation(pe, "ln0_T")
            pe.wait_ge(weight_ready, 1)
            by_token("mix_k", (6, 7), [(XT, rows(0), KT)])
            pe.wait_ge(k_seen, NT + 1)
            bk.acquire(pe, "mix_kmax", 4, 0)
            for k in range(KT):
                last = te.transpose(B[4][:, k * TP:(k + 1) * TP], KTOP[:, k * 128:(k + 1) * 128], IDN[:TP, :TP])
            last.then_inc(bank_full[4], 1)
            pe.wait_ge(edges_float, 1)
            for a in range(2):
                bk.acquire(pe, "edges", a, 0)
                for gg in range(3):
                    last = te.transpose(B[a][:, gg * EC:(gg + 1) * EC], IDXF[:, a, gg, :], IDN[:, :])
                last.then_inc(bank_full[a], 1)
            pe.wait_ge(kdiag_ready, 1)
            bk.acquire(pe, "mix_kbias", 7, 0)
            te.matmul(B[7][:TP, :], ONES[:, :TP], KDIAG[:, :, :].rearrange("p k c -> p (k c)"), start=True, stop=True).then_inc(bank_full[7], 1)

            def q_pair(i):
                for u in range(2):
                    b = Q_BANKS[i % 2][u]
                    bk.acquire(pe, "mix_q", b, i // 2)
                    sum_products(B[b][:TP, :], [
                        (XT[:, pa, k, (2 * i + u) * TP:(2 * i + u + 1) * TP], rows(1)[:, pw, k, :])
                        for k in range(KT) for pa, pw in PASSES
                    ]).then_inc(bank_full[b], 1)

            pe.wait_ge(weight_ready, 2)
            q_pair(0)
            q_pair(1)
            for i in range(NT // 2):
                if i + 2 < NT // 2:
                    q_pair(i + 2)
                for u in range(2):
                    pe.wait_ge(q_soft, 2 * i + u + 1)
                    bk.acquire(pe, "mix_qT", 4 + u, i)
                    for k in range(KT):
                        last = te.transpose(B[4 + u][:, k * TP:(k + 1) * TP], QW[:, i % 2, u, k * 128:(k + 1) * 128], IDN[:TP, :TP])
                    last.then_inc(bank_full[4 + u], 1)
            pe.wait_ge(weight_ready, 3)
            by_token("mix_v", (0, 1), [(XT, rows(2), KT)])
            bk.after_evacuation(pe, "mix_v")
            pe.wait_ge(k_exp, NT)
            for b in (6, 7):
                bk.acquire(pe, "mix_ctx", b, 0)
                for m in (2 * (b - 6), 2 * (b - 6) + 1):
                    last = sum_products(B[b][:, m % 2 * 256:m % 2 * 256 + 130], [
                        (EK[:, i, m * 128:(m + 1) * 128], V[:, i, m, :]) for i in range(NT)])
                last.then_inc(bank_full[b], 1)
            bk.after_evacuation(pe, "mix_qT")
            bk.after_evacuation(pe, "mix_ctx")
            for i in range(NT):
                bk.acquire(pe, "mix_out", 2 + i % 2, i // 2)
                for m in range(KT):
                    last = te.matmul(B[2 + i % 2][:TP, m * 128:(m + 1) * 128], QT[:, m, i * TP:(i + 1) * TP],
                                     CTX[:, m, :], start=True, stop=True)
                last.then_inc(bank_full[2 + i % 2], 1)

            def counts_transposes(T):
                pe.wait_ge(deg_ready, T + 1)
                for b in range(3):
                    bk.acquire(pe, "counts_T", b, T)
                    for j in range(min(4, NT - 4 * b)):
                        sb = 4 * b + j
                        last = te.transpose(B[b][:TP, j * TP:(j + 1) * TP], ACC[T % 2][:, sb // 5, sb % 5 * TP:(sb % 5 + 1) * TP],
                                            IDN[:TP, :TP])
                    last.then_inc(bank_full[b], 1)

            pe.wait_ge(plan_ready, 1)
            pe.sem_inc(onehot_free, RING)
            pe.sem_inc(seg_int, 1)
            bk.after_evacuation(pe, "mix_out")
            for T in range(NT):
                _, n, before = plan(pe, T)
                with pe.Fori(0, n) as i:
                    pe.wait_ge(seg_int, before + i + 1)
                    for j in range(SEG):
                        if j % SHARE == SHARE - 1:
                            pe.wait_ge(act_onehot_ready, (before + i) * (SEG // SHARE) + (j // SHARE + 2))
                        else:
                            pe.wait_ge(onehot_ready, (before + i) * PER_SEG + (j - j // SHARE + 2))
                        for h in range(2):
                            last = te.matmul(PS[:, ds((before + i) % 2 * 2 + (4 + h), 1), 0:HW].rearrange("p a c -> p (a c)"),
                                             ONEHOT_D[:, ds((before + i) % 2, 1), j, :].rearrange("p a c -> p (a c)"), ONEHOT_S[:, j % RING, h * HW:(h + 1) * HW],
                                             start=(j == 0), stop=(j == SEG - 1))
                        last.then_inc(onehot_free, 1)
                if T:
                    counts_transposes(T - 1)
            counts_transposes(NT - 1)

            def degrees(stage, done):
                pe.wait_ge(diag_ready, done + 1)
                for b, (lo, n) in enumerate(CHUNKS):
                    bk.acquire(pe, stage, b, 0)
                    te.matmul(B[b][:, 0:n], ONES[:TP, :], DIAG[:, :, :].rearrange("p a b -> p (a b)")[:, lo:lo + n], start=True,
                              stop=True).then_inc(bank_full[b], 1)

            def neighbours(stage):
                pe.wait_ge(far_known, 1)
                far = pe.value_load(FARI[0:1, 0:1], min_val=0, max_val=1)
                with pe.Fori(0, KT // 2) as i:
                    for u in range(2):
                        for c, (lo, n) in enumerate(CHUNKS):
                            bk.acquire(pe, stage, 3 * u + c, i)

                            def products(pa, pb, first, last):
                                for sb in range(NT):
                                    ins = te.matmul(B[3 * u + c][:, 0:n], XK[:, pa, sb, ds(i * 256 + 128 * u, 128)], AT[:, pb, sb, lo:lo + n],
                                                    start=first and sb == 0, stop=last and sb == NT - 1, skip_group_check=True)
                                return ins

                            products(0, 0, True, False)
                            with pe.If(far == 1):
                                if stage == "agg1":
                                    pe.wait_ge(counts_back, 16)
                                products(0, 1, False, False)
                            products(1, 0, False, True).then_inc(bank_full[3 * u + c], 1)

            degrees("deg0", 0)
            bk.after_evacuation(pe, "counts_T")
            neighbours("agg0")
            pe.wait_ge(weight_ready, 5)
            pe.wait_ge(mean_ready, 3 * KT)
            def scale_sum(n, a):
                b = (6, 7, 6)[a]
                pe.wait_ge(magnitude, n + 1)
                bk.acquire(pe, *scale_use(n, a))
                te.matmul(B[b][:, :], ONES[:, :], MAG[:, a, :], start=True, stop=True).then_inc(bank_full[b], 1)

            def gate_up(j, par, ahead):
                pe.wait_ge(ffn_low, j + 1)
                if ahead:
                    scale_sum(j + 2, 0)
                    scale_sum(j + 2, 1)
                for a in range(2):
                    for c, (lo, n) in enumerate(CHUNKS):
                        b = 3 * a + c
                        bk.acquire(pe, "ffn", b, j)
                        sum_products(B[b][:, 0:n], [
                            (GU[:, par, a, pw, k * 128:(k + 1) * 128], XT[:, pa, k, lo:lo + n]) for k in range(KT) for pw, pa in PASSES
                        ]).then_inc(bank_full[b], 1)
                        if ahead and a == 0 and c == 0:
                            scale_sum(j + 2, 2)

            for a in range(3):
                scale_sum(0, a)
            by_token("gnn0", (6, 7), [(XT, rows(0), KT), (MT, rows(1), KT)])
            for a in range(3):
                scale_sum(1, a)
            normed_T("ln1_T", (0, 1), NT)
            bk.after_evacuation(pe, "ln1_T")
            with pe.Fori(0, 4) as i:
                for u in range(2):
                    gate_up(i * 2 + u, u, True)
            gate_up(8, 0, True)
            gate_up(9, 1, False)
            gate_up(10, 0, False)
            pe.wait_ge(hidden_done, 3 * FT)
            by_token("down", (6, 7), [(HT, WD, FT)])

            normed_T("ln2_T", (2, 3), 2 * NT, XN2)
            degrees("deg1", 1)
            pe.wait_ge(xk_low, 2 * NT)
            neighbours("agg1")
            pe.wait_ge(weight_ready, 7)
            pe.wait_ge(mean_ready, 6 * KT)
            bk.after_evacuation(pe, "ln2_T")
            for m in range(KT):
                by_feature("gnn1", (0, 1, 2) if m % 2 == 0 else (3, 4, 5), m, [(MT, rows(0)), (XT, rows(1))], m // 2)
            for m in range(2 * KT):
                if m % KT == 0:
                    pe.wait_ge(weight_ready, 8 + m // KT)
                by_feature("qk1", (0, 1, 2) if m % 2 == 0 else (3, 4, 5), m % KT, [(XT, rows(2 if m < KT else 0))], m // 2)
            pe.wait_ge(weight_ready, 10)
            by_token("v1", (6, 7), [(XT, rows(1), KT)])
            pe.wait_ge(route_loaded, 16 * 9)
            bk.after_evacuation(pe, "qk1")
            for m in range(KT):
                for c, (lo, n) in enumerate(CHUNKS):
                    b = 3 * (m % 2) + c
                    bk.acquire(pe, "phi_q", b, m // 2)
                    te.matmul(B[b][:, 0:n], PB[:, m, :], QF[:, m, lo:lo + n], start=True, stop=True).then_inc(bank_full[b], 1)
            for i in range(NT):
                bk.acquire(pe, "phi_k", 6 + i % 2, i // 2)
                for m in range(KT):
                    last = te.matmul(B[6 + i % 2][:TP, m * 128:(m + 1) * 128], KF[:, m, i * TP:(i + 1) * TP], PB[:, m, :],
                                     start=True, stop=True)
                last.then_inc(bank_full[6 + i % 2], 1)
            bk.after_evacuation(pe, "v1")
            bk.after_evacuation(pe, "phi_k")
            for b in range(2):
                bk.acquire(pe, "kv", b, 0)
                for m in range(KT):
                    cols = slice(m * 128, (m + 1) * 128)
                    last = sum_products(B[b][:, 0:D].rearrange("p (m c) -> p m c", m=KT)[:, m, :] if b == 0 else B[b][:, 2 * m:2 * m + 2], [
                        (KP[:, i, cols], V1[:, i, cols] if b == 0 else ONES[:TP, 0:2]) for i in range(NT)])
                last.then_inc(bank_full[b], 1)
            bk.after_evacuation(pe, "kv")
            bk.after_evacuation(pe, "phi_q")

            def att_transposes(i):
                pe.wait_ge(att_ready, i + 1)
                bk.acquire(pe, "att_T", 6 + i % 2, i // 2)
                for k in range(KT):
                    last = te.transpose(B[6 + i % 2][:, k * TP:(k + 1) * TP], OW[:, i % 2, k * 128:(k + 1) * 128], IDN[:TP, :TP])
                last.then_inc(bank_full[6 + i % 2], 1)

            for i in range(NT):
                for stage, b0, rhs, w in (("att", 2, KVB, 128), ("z", 4, ZB, 2)):
                    b = b0 + i % 2
                    bk.acquire(pe, stage, b, i // 2)
                    for m in range(KT):
                        last = te.matmul(B[b][:TP, m * w:(m + 1) * w], QP[:, m, i * TP:(i + 1) * TP], rhs[:, m, :], start=True, stop=True)
                    last.then_inc(bank_full[b], 1)
                if i:
                    att_transposes(i - 1)
            att_transposes(NT - 1)
            pe.wait_ge(weight_ready, NU)
            pe.wait_ge(gnn1_done, KT)
            bk.after_evacuation(pe, "att_T")
            for i in range(NT):
                b = i % 2
                cols = slice(i * TP, (i + 1) * TP)
                bk.acquire(pe, "proj", b, i // 2)
                for k in range(KT):
                    te.matmul(B[b][:TP, k * 128:(k + 1) * 128], G[:, k, cols], IDNS[:, :], start=(k == 0), stop=False,
                              skip_group_check=True)
                terms = [(k, pa, pw) for k in range(KT) for pa, pw in PASSES]
                for n, (k, pa, pw) in enumerate(terms):
                    last = te.matmul(B[b][:TP, :], XT[:, pa, k, cols], rows(2)[:, pw, k, :], start=False, stop=(n == len(terms) - 1),
                                     skip_group_check=True)
                last.then_inc(bank_full[b], 1)

            normed_T("ln3_T", (2, 3), 3 * NT)
            pe.wait_ge(wg_ready, 1)
            bk.after_evacuation(pe, "ln3_T")
            bk.acquire(pe, "gate", 4, 0)
            for i in range(NT):
                last = sum_products(B[4][:TP, i * NE:(i + 1) * NE], [
                    (XT[:, pa, k, i * TP:(i + 1) * TP], WGS[:, pw, k, :]) for k in range(KT) for pa, pw in PASSES])
            last.then_inc(bank_full[4], 1)
            pe.wait_ge(masks_ready, 2)
            for b, lhs in ((5, TRI16), (6, ONES16)):
                bk.acquire(pe, "places", b, 0)
                te.matmul(B[b][:TP, 0:NT * 2 * NE], lhs[:TP, :TP], MASK[:, :, :, :].rearrange("p t c e -> p (t c e)"), start=True, stop=True)\
                  .then_inc(bank_full[b], 1)

            def slots_transposes(e, par):
                pe.wait_ge(slots_loaded[par], (e // 2 + 1) * 16)
                for b in range(3):
                    bk.acquire(pe, "slots_T", b, e)
                    for k in range(KT):
                        last = te.transpose(B[b][:, k * CT:(k + 1) * CT], XE[:, par, b, k * 128:(k + 1) * 128], IDN[:CT, :CT])
                    last.then_inc(bank_full[b], 1)

            def hidden(e, par):
                pe.wait_ge(weight_ready, e + (NU + 1))
                for b in range(3):
                    bk.emptied(pe, "slots_T", b, e)
                w1 = W[par][:, :, 0:1024].rearrange("p a (k h) -> p a k h", k=KT)
                for m in range(2):
                    bk.acquire(pe, "hidden", 3 + m, e)
                    sum_products(B[3 + m][:, 0:CAP], [
                        (w1[:, pw, k, m * 128:(m + 1) * 128], XET[:, par, pa, k, :]) for k in range(KT) for pw, pa in PASSES
                    ]).then_inc(bank_full[3 + m], 1)

            def expert_out(e, par):
                pe.wait_ge(relu_low, e + 1)
                w2 = W[par][:, :, 1024:2048].rearrange("p a (k d) -> p a k d", k=2)
                for c in range(3):
                    bk.acquire(pe, "expert", 5 + c, e)
                    sum_products(B[5 + c][:CT, :], [
                        (HH[:, par, pa, k, c * CT:(c + 1) * CT], w2[:, pw, k, :]) for k in range(2) for pa, pw in PASSES
                    ]).then_inc(bank_full[5 + c], 1)

            slots_transposes(0, 0)
            for e in range(NE):
                hidden(e, e % 2)
                if e + 1 < NE:
                    slots_transposes(e + 1, (e + 1) % 2)
                expert_out(e, e % 2)

        @block.vector
        def _(dve):
            v = nc.vector
            own = Own(dve, dve_own)

            def heads(x):
                return x.rearrange("p (h d) -> p h d", h=H)

            def stats(i, x):
                return v.bn_stats(STATS[:, i, :], x[:, i, :])

            def mean_var(half, ready):
                for i in range(half * NT // 2, (half + 1) * NT // 2):
                    last = v.bn_aggr(MV[:, i, :], STATS[:, i, :])
                    if i % (NT // 2) < NT // 2 - 1:
                        m = own.mark(last)
                last.then_inc(ready, 1)
                own.after(m)

            def norm(stage, banks, n, evacuate=None, XN=XN):
                for half in range(2):
                    tiles = range(half * NT // 2, (half + 1) * NT // 2)
                    if evacuate:
                        added = evacuate(tiles[0])
                    for i in tiles:
                        if n == 0 and i % 5 == 0:
                            dve.wait_ge(x_loaded[half], 16)
                        if evacuate:
                            before = added
                            if i + 1 in tiles:
                                added = evacuate(i + 1)
                            before()
                        m = own.mark(stats(i, X))
                    own.after(m)
                    mean_var(half, var_ready)
                    dve.wait_ge(std_ready, 2 * n + half + 1)
                    own.step(v.reciprocal(RSTD[:, tiles[0]:tiles[-1] + 1], STD[:, tiles[0]:tiles[-1] + 1]))
                    with dve.Fori(0, NT // 2) as i:
                        tile = ds(i + tiles[0], 1)
                        v.tensor_scalar(XN[:, tile, :], X[:, tile, :], MV[:, tile, 0:1].rearrange("p a b -> p (a b)"), RSTD[:, tile],
                                        ALU.subtract, ALU.mult).then_inc(xn_ready, 1)
                transposed_low(stage, banks, n)

            def transposed_low(stage, banks, n):
                with dve.Fori(0, NT // 2) as i:
                    for u in range(2):
                        dve.wait_ge(xt_high, i * 2 + (NT * (n + (n == 3)) + u + 1))
                        cols = ds(i * (2 * TP) + u * TP, TP)
                        v.scalar_tensor_tensor(XT[:, 1, :, cols], B[banks[u]][:, 0:KT * TP].rearrange("p (k n) -> p k n", k=KT),
                                               1.0, XT[:, 0, :, cols], ALU.mult, ALU.subtract).then_inc(bank_free[banks[u]], 1)

            def add_products(stage, b0):
                def evacuate(i):
                    b = b0 + i % 2
                    bk.filled(dve, stage, b, i // 2)
                    v.scalar_tensor_tensor(X[:, i, :], B[b][:TP, :], UNSCALE, X[:, i, :], ALU.mult, ALU.add).then_inc(bank_free[b], 1)
                    return lambda: bk.emptied(dve, stage, b, i // 2)
                return evacuate

            v.memset(KTOP[:, :], -3e38).then_inc(k_seen, 1)
            norm("ln0_T", (0, 1), 0)
            dve.wait_ge(small_loaded, 160)
            with dve.Fori(0, NT // 2) as i:
                for u in range(2):
                    bk.filled(dve, "mix_k", 6 + u, i)
                    dve.wait_ge(k_seen, i * 2 + (u + 1))
                    v.tensor_tensor(KTOP[:, :], B[6 + u][:TP, :], KTOP[:, :], ALU.max).then_inc(k_seen, 1)
            bk.filled(dve, "mix_kmax", 4, 0)
            own.step(v.tensor_reduce(KMAX, B[4][:, 0:KT * TP].rearrange("p (k n) -> p k n", k=KT), AX.X, ALU.max))
            v.scalar_tensor_tensor(KMAX, KMAX, UNSCALE, BK, ALU.mult, ALU.add).then_inc(bank_free[4], 1)
            bk.after_evacuation(dve, "mix_kmax")
            own.step(v.tensor_tensor(KBIAS, BK, KMAX, ALU.subtract))
            v.tensor_tensor(KDIAG[:, :, :], IDN[:, :].unsqueeze(1).to_broadcast([128, KT, 128]),
                            KBIAS.unsqueeze(2).to_broadcast([128, KT, 128]), ALU.mult).then_inc(kdiag_ready, 1)
            bk.filled(dve, "edges", 1, 0)
            v.tensor_copy(DST[:, :], B[1][:, 0:NCH]).then_inc(bank_free[1], 1)
            bk.filled(dve, "edges", 0, 0)
            own.mark(v.tensor_copy(SRC[:, :], B[0][:, 0:NCH]))
            v.tensor_scalar(SRCV[:, :], B[0][:, 0:NCH], float(HS), BASE - 1.0, ALU.is_ge, ALU.mult).then_inc(bank_free[0], 1)
            bk.after_evacuation(dve, "edges")
            own.step(v.tensor_scalar(SRCV[:, :], SRCV[:, :], 1.0, None, ALU.add))
            tmp = TMP[:, :, :].rearrange("p g e -> p (g e)")
            own.step(v.tensor_scalar(tmp, SRC[:, :], float(HS), float(HS), ALU.is_ge, ALU.mult))
            own.step(v.tensor_tensor(SRC[:, :], SRC[:, :], tmp, ALU.subtract))
            own.step(v.scalar_tensor_tensor(SRCB[:, :], SRC[:, :], -1.0, SRCV[:, :], ALU.mult, ALU.mult))

            def q_shift(i):
                qw = QW[:, i % 2, :, :]
                for u in range(2):
                    b = Q_BANKS[i % 2][u]
                    bk.filled(dve, "mix_q", b, i // 2)
                    if i >= 2:
                        bk.filled(dve, "mix_qT", 4 + u, i - 2)
                    v.scalar_tensor_tensor(qw[:, u, :], B[b][:TP, :], UNSCALE, BQ, ALU.mult, ALU.add).then_inc(bank_free[b], 1)
                for u in range(2):
                    bk.emptied(dve, "mix_q", Q_BANKS[i % 2][u], i // 2)
                    m = own.mark(v.tensor_reduce(SM8[:, u, 0, :], heads(qw[:, u, :]), AX.X, ALU.max))
                own.after(m)
                for u in range(2):
                    v.tensor_tensor(heads(qw[:, u, :]), heads(qw[:, u, :]), SM8[:, u, 0, :].unsqueeze(2).to_broadcast([TP, H, DH]),
                                    ALU.subtract).then_inc(q_shifted, 1)

            q_shift(0)
            for i in range(NT // 2):
                if i + 1 < NT // 2:
                    q_shift(i + 1)
                qw = QW[:, i % 2, :, :]
                for u in range(2):
                    dve.wait_ge(q_exp, i * 2 + (u + 1))
                    m = own.mark(v.tensor_reduce(SM8[:, u, 1, :], heads(qw[:, u, :]), AX.X, ALU.add))
                own.after(m)
                for u in range(2):
                    m = own.mark(v.reciprocal(SM8[:, u, 2, :], SM8[:, u, 1, :]))
                own.after(m)
                for u in range(2):
                    v.scalar_tensor_tensor(heads(qw[:, u, :]), heads(qw[:, u, :]), DH ** -0.5,
                                           SM8[:, u, 2, :].unsqueeze(2).to_broadcast([TP, H, DH]), ALU.mult, ALU.mult)\
                     .then_inc(q_soft, 1)
            own.mark(v.tensor_reduce(RED[:, 0, :], IDXF[:, 1, :, :], AX.X, ALU.max))
            own.step(v.tensor_scalar(TMP[:, :, :], IDXF[:, 1, :, :], 0.0, 2.0 * N, ALU.is_lt, ALU.mult))
            own.step(v.tensor_tensor(TMP[:, :, :], TMP[:, :, :], IDXF[:, 1, :, :], ALU.add))
            own.step(v.tensor_reduce(RED[:, 1, :], TMP[:, :, :], AX.X, ALU.min))
            thr = THR[:, :].unsqueeze(2).to_broadcast([128, NT, 3])

            def per_tile(x):
                return x.unsqueeze(1).to_broadcast([128, NT, 3])

            own.mark(v.scalar_tensor_tensor(RANGE[:, 0, 0, :, :], per_tile(RED[:, 0, :]), 0.5, thr, ALU.add, ALU.is_gt))
            own.step(v.scalar_tensor_tensor(RANGE[:, 0, 1, :, :], per_tile(RED[:, 1, :]), TP - 0.5, thr, ALU.subtract, ALU.is_lt))
            own.step(v.tensor_tensor(RANGE[:, 0, 2, :, :], RANGE[:, 0, 0, :, :], RANGE[:, 0, 1, :, :], ALU.mult))
            for a in range(2):
                m = own.mark(v.tensor_tensor(RANGE[:, 1, a, :, :], RANGE[:, 0, 2, :, :], per_tile(CID[:, a, :]), ALU.mult))
            own.after(m)
            v.tensor_reduce(LOHI[:, :, :], RANGE[:, 1, 0:2, :, :], AX.X, ALU.max).then_inc(lohi_local, 1)
            bk.after_products(dve, "mix_qT")
            own.step(v.memset(V[:, :, :, 128:130], 1.0))
            with dve.Fori(0, NT // 2) as i:
                for u in range(2):
                    bk.filled(dve, "mix_v", u, i)
                    v.scalar_tensor_tensor(V[:, ds(i * 2 + u, 1), :, 0:128].rearrange("p a k c -> p (a k) c"), B[u][:TP, :].rearrange("p (k c) -> p k c", k=KT),
                                           UNSCALE, BV.rearrange("p (k c) -> p k c", k=KT), ALU.mult, ALU.add).then_inc(bank_free[u], 1)
            dve.wait_ge(lohi_all, 1)
            own.mark(v.memset(PLAN[:, :, :], 0.0))
            own.step(v.tensor_scalar(LOHI[0:1, 0, :], LOHIR[0:1, 0, :], -1.0, 512.0, ALU.mult, ALU.add))
            own.step(v.tensor_scalar(PLAN[0:1, 0, 0:NT], LOHI[0:1, 0, :], float(ER), None, ALU.min))
            own.step(v.tensor_scalar(LOHI[0:1, 0, :], PLAN[0:1, 0, 0:NT], 1.0, None, ALU.add))
            own.step(v.tensor_tensor(LOHI[0:1, 1, :], LOHIR[0:1, 1, :], LOHI[0:1, 0, :], ALU.max))
            own.step(v.tensor_tensor(LOHI[0:1, 1, :], LOHI[0:1, 1, :], PLAN[0:1, 0, 0:NT], ALU.subtract))
            own.step(v.tensor_tensor(STEPS[:, :, :], LOHI[0:1, 1, :].unsqueeze(2).to_broadcast([1, NT, 32]),
                                     MULT[:, :].unsqueeze(1).to_broadcast([1, NT, 32]), ALU.is_gt))
            own.step(v.tensor_reduce(PLAN[0:1, 1, 0:NT], STEPS[:, :, :], AX.X, ALU.add))
            for T in range(NT):
                own.step(v.tensor_tensor(PLAN[0:1, 2, T + 1:T + 2], PLAN[0:1, 2, T:T + 1], PLAN[0:1, 1, T:T + 1], ALU.add))
            v.tensor_copy(PLANI[:, :, :], PLAN[:, :, :]).then_inc(plan_ready, 1)
            dve.wait_ge(plan_ready, 1)
            dve.sem_inc(lohi_ready, 2)


            own.step(v.memset(CTX[:, :, :], 0.0))
            bk.after_products(dve, "mix_ctx")
            contexts = PS[:, 6:8, :].rearrange("p b (a c) -> p (b a) c", a=2)
            own.step(v.reciprocal(KREC.unsqueeze(2), contexts[:, :, 128:129]))
            for hh in range(2):
                p = slice(64 * hh, 64 * hh + 64)
                v.tensor_tensor(CTX[p, :, p], contexts[p, :, p], KREC[p, :].unsqueeze(2).to_broadcast([64, KT, 64]), ALU.mult)\
                 .then_inc(bank_free[6 + hh], 1)
            with dve.Fori(0, NT // 2) as i:
                for u in range(2):
                    bk.filled(dve, "mix_out", 2 + u, i)
                    v.tensor_tensor(X[:, ds(i * 2 + u, 1), :], B[2 + u][:TP, :].rearrange("p (a d) -> p a d", a=1), X[:, ds(i * 2 + u, 1), :], ALU.add)\
                     .then_inc(bank_free[2 + u], 1)
            own.mark(v.memset(ONEHOT_S[:, :, ONE_COL:ONE_COL + 1], 1.0))
            own.step(v.memset(ONEHOT_S[:, :, ONE_COL + 1:2 * HW], 0.0))

            def unpack(f):
                dve.wait_ge(seg_int, f + 2)
                dve.wait_ge(acc_added, f + 1)
                both = I2[:, ds((f + 1) % 2, 1), :, :].rearrange("p a h c -> p (a h c)")
                v.tensor_scalar(LH[:, 0, :], both, int(BASE) - 1, None, ALU.bitwise_and).then_inc(dve_free, 1)
                v.tensor_scalar(LH[:, 1, :], both, 12, None, ALU.logical_shift_right).then_inc(lohi_ready, 1)

            def counts_low(T):
                for b in range(3):
                    n = min(4, NT - 4 * b)
                    dve.wait_ge(counts_high, 3 * T + b + 1)
                    cols = slice(T * TP, (T + 1) * TP)
                    v.scalar_tensor_tensor(AT[:, 1, 4 * b:4 * b + n, cols], B[b][:TP, 0:n * TP].rearrange("p (s d) -> p s d", s=n),
                                           1.0, AT[:, 0, 4 * b:4 * b + n, cols], ALU.mult, ALU.subtract).then_inc(bank_free[b], 1)

            for T in range(NT):
                lo, n, before = plan(dve, T)
                own.step(v.tensor_scalar(DREL[:, T % 2, :], DST[:, :], -float(TP * T), None, ALU.add))
                with dve.Fori(0, n) as i:
                    first = nc.s_assert_within(lo + i * SEG, 0, NCH - SEG, skip_runtime_bounds_check_because="the plan's last segment starts before the last chunk")
                    for j in range(SEG):
                        if j % SHARE == SHARE - 1:
                            continue
                        dve.wait_ge(onehot_free, (before + i) * SEG + (j + 1))
                        if j == 0:
                            v.tensor_tensor(ONEHOT_D[:, ds((before + i) % 2, 1), :, :].rearrange("p a s c -> p (a s) c"),
                                            IOTA_D[:, :].unsqueeze(1).to_broadcast([128, SEG, 128]),
                                            DREL[:, T % 2, ds(first, SEG)].unsqueeze(2).to_broadcast([128, SEG, 128]), ALU.is_equal)\
                             .then_inc(onehot_ready, 1)
                        v.tensor_scalar(ONEHOT_S[:, j % RING, 0:ONE_COL], IOTA_S[:, :], SRC[:, ds(first + j, 1)],
                                        SRCV[:, ds(first + j, 1)], ALU.is_equal, ALU.mult).then_inc(onehot_ready, 1)
                        if j == SEG - 2:
                            unpack(before + i)
                if T >= 2:
                    counts_low(T - 2)
            unpack(before + n)
            counts_low(NT - 2)
            counts_low(NT - 1)

            def means(stage_deg, stage, done):
                dve.wait_ge(deg_ready, NT)
                if done == 0:
                    own.step(v.tensor_scalar(DEG[:, :], DEG[:, :], 1.0, None, ALU.max))
                    own.step(v.reciprocal(RDEG[:, :], DEG[:, :]))
                v.tensor_tensor(DIAG[:, :, :], IDN[:TP, :TP].unsqueeze(1).to_broadcast([TP, NT, TP]),
                                RDEG[:, :].unsqueeze(2).to_broadcast([TP, NT, TP]), ALU.mult).then_inc(diag_ready, 1)
                for b, (lo, n) in enumerate(CHUNKS):
                    bk.filled(dve, stage_deg, b, 0)
                    v.tensor_copy(DG[:, lo:lo + n], B[b][:, 0:n]).then_inc(bank_free[b], 1)
                bk.after_evacuation(dve, stage_deg)
                if done == 0:
                    own.step(v.tensor_reduce(FAR[:, 0:1], DG[0:1, :], AX.X, ALU.min))
                    own.step(v.tensor_scalar(FAR[:, 1:2], FAR[:, 0:1], 1 / (EXACT + 0.5), None, ALU.is_lt))
                    v.tensor_copy(FARI[:, :], FAR[:, 1:2]).then_inc(far_known, 1)
                with dve.Fori(0, KT // 2) as i:
                    for u in range(2):
                        for c, (lo, n) in enumerate(CHUNKS):
                            bk.filled(dve, stage, 3 * u + c, i)
                            v.tensor_tensor(MTMP[:, u, c, 0:n], B[3 * u + c][:, 0:n], DG[:, lo:lo + n], ALU.mult).then_inc(bank_free[3 * u + c], 1)
                        for c, (lo, n) in enumerate(CHUNKS):
                            dve.wait_ge(mean_high, i * 6 + (3 * u + c + 1 + 3 * KT * done))
                            v.tensor_tensor(MT[:, 1, ds(i * 2 + u, 1), lo:lo + n], MTMP[:, u, c:c + 1, 0:n],
                                            MT[:, 0, ds(i * 2 + u, 1), lo:lo + n], ALU.subtract).then_inc(mean_ready, 1)

            means("deg0", "agg0", 0)
            def ternaries(n, par):
                w = STG[(par + 1) % 2][:, 0:1536].rearrange("p (a c) -> p a c", a=3)
                for a in (2, 1):
                    bk.emptied(dve, *scale_use(n, a))
                if not (isinstance(n, int) and n == 0):
                    dve.wait_ge(quantised, n)
                own.mark(v.scalar_tensor_tensor(MAG[:, :, :], QUANT[:, par, :, :], 0.5 / W_SCALE, w, ALU.mult, ALU.is_lt))
                own.step(v.scalar_tensor_tensor(TERN[:, :, :], QUANT[:, par, :, :], -0.5 / W_SCALE, w, ALU.mult, ALU.is_gt))
                v.tensor_tensor(TERN[:, :, :], MAG[:, :, :], TERN[:, :, :], ALU.subtract).then_inc(ternary, 1)

            ternaries(0, 0)
            dve.wait_ge(beta_added, NT)
            for half in range(2):
                tiles = range(half * NT // 2, (half + 1) * NT // 2)
                for i in (*tiles, tiles[-1] + 1):
                    if i in tiles:
                        b = 6 + i % 2
                        bk.filled(dve, "gnn0", b, i // 2)
                        v.scalar_tensor_tensor(XN[:, i, :], B[b][:TP, :], UNSCALE, BIAS, ALU.mult, ALU.add).then_inc(bank_free[b], 1)
                    if i > tiles[0]:
                        bk.emptied(dve, "gnn0", 6 + (i - 1) % 2, (i - 1) // 2)
                        m = own.mark(stats(i - 1, XN))
                own.after(m)
                mean_var(half, gnn_var)
                dve.wait_ge(gnn_std, half + 1)
                own.step(v.reciprocal(RSTD[:, tiles[0]:tiles[-1] + 1], STD[:, tiles[0]:tiles[-1] + 1]))
                own.step(v.tensor_scalar(RSTD[:, tiles[0]:tiles[-1] + 1], RSTD[:, tiles[0]:tiles[-1] + 1], 1 / A_SCALE, None, ALU.mult))
                for i in tiles:
                    m = own.mark(v.scalar_tensor_tensor(XN[:, i, :], XN[:, i, :], MV[:, i, 0:1], GAMMA, ALU.subtract, ALU.mult))
                own.after(m)
                for i in tiles:
                    m = own.mark(v.scalar_tensor_tensor(X[:, i, :], XN[:, i, :], RSTD[:, i:i + 1], X[:, i, :], ALU.mult, ALU.add))
                own.after(m)
                for i in tiles:
                    m = own.mark(stats(i, X))
                own.after(m)
                mean_var(half, var_ready)
                dve.wait_ge(std_ready, 2 + half + 1)
                own.step(v.reciprocal(RSTD[:, tiles[0]:tiles[-1] + 1], STD[:, tiles[0]:tiles[-1] + 1]))
                for i in tiles:
                    v.tensor_scalar(XN[:, i, :], X[:, i, :], MV[:, i, 0:1], RSTD[:, i:i + 1], ALU.subtract, ALU.mult).then_inc(xn_ready, 1)
            transposed_low("ln1_T", (0, 1), 1)

            def hiddens(j):
                for c, (lo, n) in enumerate(CHUNKS):
                    bk.filled(dve, "ffn", 3 + c, j)
                    bk.emptied(dve, "ffn", c, j)
                    v.scalar_tensor_tensor(GATED[:, c, 0:n], B[3 + c][:, 0:n], UNSCALE * A_SCALE, GATED[:, c, 0:n], ALU.mult, ALU.mult)\
                     .then_inc(bank_free[3 + c], 1)
                for c, (lo, n) in enumerate(CHUNKS):
                    dve.wait_ge(hidden_high, j * 3 + (c + 1))
                    v.tensor_tensor(HT[:, 1, ds(j, 1), lo:lo + n], GATED[:, c:c + 1, 0:n], HT[:, 0, ds(j, 1), lo:lo + n], ALU.subtract)\
                     .then_inc(hidden_done, 1)

            ternaries(1, 1)
            with own.loop(4, 4) as i:
                for u in range(2):
                    ternaries(i * 2 + (u + 2), u)
                    hiddens(i * 2 + u)
            ternaries(10, 0)
            for j in (8, 9, 10):
                hiddens(j)
            norm("ln2_T", (2, 3), 2, add_products("down", 6), XN2)
            dve.wait_ge(xk_low, 2 * NT)
            bk.after_evacuation(dve, "ln2_T")
            means("deg1", "agg1", 1)

            for m in range(KT):
                for c, (lo, n) in enumerate(CHUNKS):
                    bk.emptied(dve, "gnn1", 3 * (m % 2) + c, m // 2)
                    mm = own.mark(v.bn_stats(GSTATS[:, m, c, :], G[:, m, lo:lo + n]))
            own.after(mm)
            for m in range(KT):
                ins = v.bn_aggr(GMV[:, m, :], GSTATS[:, m, :, :])
                if m < KT - 1:
                    mm = own.mark(ins)
                else:
                    ins.then_inc(gnn1_var, 1)
            dve.wait_ge(gnn1_var, 1)
            dve.wait_ge(gnn1_std, 1)
            own.step(v.reciprocal(GCOL[:, 1, :], GCOL[:, 0, :]))
            own.step(v.tensor_tensor(GCOL[:, 2, :], GCOL[:, 1, :], G1, ALU.mult))
            own.step(v.tensor_tensor(GCOL[:, 3, :], GMV[:, :, 0], GCOL[:, 2, :], ALU.mult))
            own.step(v.tensor_tensor(GCOL[:, 3, :], B1, GCOL[:, 3, :], ALU.subtract))
            for m in range(KT):
                v.tensor_scalar(G[:, m, :], G[:, m, :], GCOL[:, 2, m:m + 1], GCOL[:, 3, m:m + 1], ALU.mult, ALU.add).then_inc(gnn1_done, 1)
            with dve.Fori(0, NT // 2) as i:
                for u in range(2):
                    bk.filled(dve, "v1", 6 + u, i)
                    v.tensor_scalar(V1[:, ds(i * 2 + u, 1), :], B[6 + u][:TP, :].unsqueeze(1), UNSCALE, None, ALU.mult).then_inc(bank_free[6 + u], 1)
            for m in range(KT):
                for c, (lo, n) in enumerate(CHUNKS):
                    b = 3 * (m % 2) + c
                    bk.filled(dve, "phi_q", b, m // 2)
                    if m:
                        bk.emptied(dve, "phi_q", 3 * ((m - 1) % 2) + c, (m - 1) // 2)
                    v.tensor_scalar(PTMP[:, c, 0:n], B[b][:, 0:n], 0.0, None, ALU.min).then_inc(phi_min, 1)
                for c, (lo, n) in enumerate(CHUNKS):
                    b = 3 * (m % 2) + c
                    dve.wait_ge(phi_exp, 3 * m + c + 1)
                    v.scalar_tensor_tensor(QP[:, m, lo:lo + n], B[b][:, 0:n], 0.0, PTMP[:, c, 0:n], ALU.max, ALU.add).then_inc(bank_free[b], 1)
            bk.after_products(dve, "phi_q")
            with dve.Fori(0, NT // 2) as i:
                for u in range(2):
                    bk.filled(dve, "phi_k", 6 + u, i)
                    bk.acquire(dve, "phi_k", 6 + u, i)
                    v.tensor_scalar(OW[:, u, :], B[6 + u][:TP, :], 0.0, None, ALU.min).then_inc(kmin, 1)
                for u in range(2):
                    dve.wait_ge(kexp, i * 2 + (u + 1))
                    v.scalar_tensor_tensor(KP[:, ds(i * 2 + u, 1), :], B[6 + u][:TP, :].unsqueeze(1), 0.0, OW[:, u:u + 1, :], ALU.max, ALU.add)\
                     .then_inc(bank_free[6 + u], 1)
            dve.wait_ge(wide_own, 1)
            bk.after_products(dve, "kv")
            for hh in range(2):
                p = slice(64 * hh, 64 * hh + 64)
                own.mark(v.tensor_copy(KVB[p, :, p], B[0][p, :].rearrange("p (m d) -> p m d", m=KT)[:, :, p])) if hh == 0 else \
                    v.tensor_copy(KVB[p, :, p], B[0][p, :].rearrange("p (m d) -> p m d", m=KT)[:, :, p]).then_inc(bank_free[0], 1)
                ins = v.tensor_copy(ZB[p, :, hh:hh + 1], B[1][p, 0:2 * KT].rearrange("p (m c) -> p m c", m=KT)[:, :, 0:1])
                ins.then_inc(bank_free[1] if hh else dve_own, 1)
                own.k += 1 - hh
            bk.after_evacuation(dve, "phi_k")

            def expert_prescale(e, par):
                st = STG[(par + NU + 1) % 2]
                dve.wait_ge(staged[(par + NU + 1) % 2], expert_staged(e, par))
                v.tensor_scalar(st[:, :], st[:, :], W_SCALE, None, ALU.mult).then_inc(expert_prescaled, 1)

            def att_low(i):
                b, cols = 6 + i % 2, slice(i * TP, (i + 1) * TP)
                dve.wait_ge(xt_high, 3 * NT + i + 1)
                v.scalar_tensor_tensor(XT[:, 1, :, cols], B[b][:, 0:KT * TP].rearrange("p (k n) -> p k n", k=KT), A_SCALE,
                                       XT[:, 0, :, cols], ALU.mult, ALU.subtract).then_inc(bank_free[b], 1)

            for i in range(NT):
                if i >= 2:
                    att_low(i - 2)
                bk.filled(dve, "z", 4 + i % 2, i // 2)
                v.reciprocal(SM8[:, i % 2, 2, :], B[4 + i % 2][:TP, 0:H]).then_inc(bank_free[4 + i % 2], 1)
                bk.emptied(dve, "z", 4 + i % 2, i // 2)
                bk.filled(dve, "att", 2 + i % 2, i // 2)
                if i >= 2:
                    bk.filled(dve, "att_T", 6 + i % 2, i // 2 - 1)
                v.tensor_tensor(heads(OW[:, i % 2, :]), heads(B[2 + i % 2][:TP, :]), SM8[:, i % 2, 2, :].unsqueeze(2).to_broadcast([TP, H, DH]),
                                ALU.mult).then_inc(att_ready, 1)
                bk_free = bank_free[2 + i % 2]
                dve.wait_ge(att_ready, i + 1)
                dve.sem_inc(bk_free, 1)
            att_low(NT - 2)
            att_low(NT - 1)
            expert_prescale(0, 0)
            expert_prescale(1, 1)
            dve.wait_ge(wg_high, 1)
            v.scalar_tensor_tensor(WGS[:, 1, :, :].rearrange("p k e -> p (k e)"), WG[:, :], W_SCALE, WGS[:, 0, :, :].rearrange("p k e -> p (k e)"),
                                   ALU.mult, ALU.subtract).then_inc(wg_ready, 1)
            dve.wait_ge(bproj_added, NT)
            norm("ln3_T", (2, 3), 3, add_products("proj", 0))

            R = [ROUTE[:, n, :, :] for n in range(12)]
            K = [TOK[:, n, :] for n in range(12)]

            def by_expert(x):
                return x.unsqueeze(2).to_broadcast([TP, NT, NE])

            def by_tokens(x):
                return x.unsqueeze(1).to_broadcast([TP, NT, NE])

            bk.filled(dve, "gate", 4, 0)
            v.tensor_scalar(R[0], B[4][:TP, 0:NT * NE].rearrange("p (t e) -> p t e", t=NT), UNSCALE, None, ALU.mult).then_inc(bank_free[4], 1)
            bk.after_evacuation(dve, "gate")
            own.step(v.tensor_reduce(K[0], R[0], AX.X, ALU.max))
            v.tensor_tensor(R[0], R[0], by_expert(K[0]), ALU.subtract).then_inc(gate_exp_in, 1)
            dve.wait_ge(gate_exp, 1)
            own.step(v.tensor_reduce(K[0], R[0], AX.X, ALU.add))
            own.step(v.reciprocal(K[1], K[0]))
            own.step(v.tensor_tensor(R[0], R[0], by_expert(K[1]), ALU.mult))
            dve.wait_ge(route_consts, 3)
            for c in range(2):
                own.step(v.tensor_reduce(K[2 + c], R[c], AX.X, ALU.max))
                own.step(v.tensor_tensor(R[2], R[c], by_expert(K[2 + c]), ALU.is_equal))
                own.step(v.tensor_tensor(R[2], R[2], by_tokens(EBASE[:, 1, :]), ALU.mult))
                own.step(v.tensor_reduce(K[4], R[2], AX.X, ALU.max))
                own.step(v.tensor_tensor(R[3 + c], R[2], by_expert(K[4]), ALU.is_equal))
                v.tensor_copy(MASK[:, :, c, :], R[3 + c]).then_inc(masks_ready, 1)
                if c == 0:
                    own.step(v.tensor_tensor(R[2], R[0], R[3], ALU.mult))
                    own.step(v.tensor_tensor(R[1], R[0], R[2], ALU.subtract))
            own.step(v.tensor_tensor(K[4], K[2], K[3], ALU.add))
            own.step(v.tensor_scalar(K[4], K[4], 1e-9, None, ALU.add))
            own.step(v.reciprocal(K[4], K[4]))
            own.mark(v.tensor_tensor(K[2], K[2], K[4], ALU.mult))
            own.step(v.tensor_tensor(K[3], K[3], K[4], ALU.mult))
            own.mark(v.memset(CARRY[:, 0, :], 0.0))
            bk.filled(dve, "places", 6, 0)
            own.step(v.tensor_copy(CARRY[:, 1, :], B[6][:TP, 0:2 * NE]))
            for i in range(1, NT):
                ins = v.tensor_tensor(CARRY[:, i + 1, :], B[6][:TP, i * 2 * NE:(i + 1) * 2 * NE], CARRY[:, i, :], ALU.add)
                if i < NT - 1:
                    own.step(ins)
                else:
                    ins.then_inc(bank_free[6], 1)
            bk.emptied(dve, "places", 6, 0)
            own.step(v.tensor_scalar(CARRY[:, NT, 0:NE], CARRY[:, NT, 0:NE], float(CAP), None, ALU.min))
            bk.filled(dve, "places", 5, 0)
            within = B[5][:TP, 0:NT * 2 * NE].rearrange("p (t c e) -> p t c e", t=NT, c=2)
            carry = CARRY[:, 0:NT, :].rearrange("p t (c e) -> p t c e", c=2)
            own.mark(v.tensor_tensor(R[5], within[:, :, 0, :], carry[:, :, 0, :], ALU.add))
            v.tensor_tensor(R[6], within[:, :, 1, :], carry[:, :, 1, :], ALU.add).then_inc(bank_free[5], 1)
            bk.emptied(dve, "places", 5, 0)
            own.step(v.tensor_tensor(R[6], R[6], by_tokens(CARRY[:, NT, 0:NE]), ALU.add))
            for c in range(2):
                own.step(v.tensor_tensor(R[7], R[5 + c], R[3 + c], ALU.mult))
                own.step(v.tensor_reduce(K[5], R[7], AX.X, ALU.add))
                own.step(v.tensor_tensor(R[8], R[3 + c], by_tokens(EBASE[:, 0, :]), ALU.mult))
                own.step(v.tensor_reduce(K[6], R[8], AX.X, ALU.add))
                own.mark(v.tensor_tensor(K[6], K[6], K[5], ALU.add))
                own.step(v.tensor_scalar(K[7], K[5], float(CAP), None, ALU.is_lt))
                own.mark(v.tensor_tensor(K[2 + c], K[2 + c], K[7], ALU.mult))
                own.mark(v.tensor_tensor(K[8], K[6], K[7], ALU.mult))
                own.step(v.tensor_tensor(K[9], K[6], DUMP[:, c, :], ALU.subtract))
                own.step(v.tensor_tensor(K[9], K[9], K[7], ALU.mult))
                own.step(v.tensor_tensor(K[9], K[9], DUMP[:, c, :], ALU.add))
                own.mark(v.tensor_copy(GIDX[:, c, :], K[8]))
                v.tensor_copy(SIDX[:, c, :], K[9]).then_inc(places_ready, 1)
                dve.wait_ge(places_ready, c + 1)

            def slots_low(e, par):
                for b in range(3):
                    dve.wait_ge(slots_high, e * 3 + (b + 1))
                    cols = slice(b * CT, (b + 1) * CT)
                    v.scalar_tensor_tensor(XET[:, par, 1, :, cols], B[b][:, 0:KT * CT].rearrange("p (k n) -> p k n", k=KT), 1.0,
                                           XET[:, par, 0, :, cols], ALU.mult, ALU.subtract).then_inc(bank_free[b], 1)

            def relu_lows(e, par):
                dve.wait_ge(relu_high, e + 1)
                v.tensor_tensor(HH[:, par, 1, :, :].rearrange("p m c -> p (m c)"), HTMP[:, par, :], HH[:, par, 0, :, :].rearrange("p m c -> p (m c)"),
                                ALU.subtract).then_inc(relu_low, 1)

            def outs(e, par):
                if not (isinstance(e, int) and e < 2):
                    dve.wait_ge(outs_stored[par], stored_count(e, par))
                for c in (1, 2):
                    bk.filled(dve, "expert", 5 + c, e)
                    if c == 2:
                        bk.emptied(dve, "expert", 5, e)
                    v.tensor_scalar(EO[:, par, c, :], B[5 + c][:CT, :], UNSCALE, None, ALU.mult).then_inc(bank_free[5 + c], 1)

            slots_low(0, 0)
            for e in range(NE):
                relu_lows(e, e % 2)
                if e + 1 < NE:
                    slots_low(e + 1, (e + 1) % 2)
                if e + 2 < NE:
                    expert_prescale(e + 2, e % 2)
                outs(e, e % 2)
            for i in range(NT):
                for c in range(2):
                    n = 2 * i + c
                    dve.wait_ge(gathered[n % 4], 16 * (n // 4 + 1))
                    if c:
                        dve.wait_ge(half_added, i + 1)
                    v.scalar_tensor_tensor(X[:, i, :], GATHER[:, n % 4, :], K[2 + c][:, i:i + 1], X[:, i, :], ALU.mult, ALU.add)\
                     .then_inc(y_ready if c else half_added, 1)


def arrange(inputs):
    import numpy as np

    put = {}
    for name, a in inputs.items():
        a = np.asarray(a)
        if name in ("L0_mix_Wq", "L0_mix_Wk", "L0_mix_Wv", "L0_gnn_W_self", "L0_gnn_W_neigh", "L0_ffn_w_gate",
                    "L0_ffn_w_up", "L0_ffn_w_down", "L1_gnn_W_l", "L1_gnn_W_r"):
            put[name + "T"] = np.ascontiguousarray(a.T)
        elif name in ("L0_mix_bk", "L1_gnn_b_l", "L1_gnn_gamma", "L1_gnn_beta"):
            put[name + "C"] = np.ascontiguousarray(a.reshape(KT, 128).T)
        else:
            put[name] = np.ascontiguousarray(a)
    return put


def kernel(**inputs):
    import concourse.bacc as bacc
    from concourse import mybir as mb
    from concourse.bass_utils import run_bass_kernel_spmd

    nc = bacc.Bacc("TRN2", target_bir_lowering=False, num_devices=1)
    arrays = {f"in_{k}_dram": a for k, a in arrange(inputs).items()}
    t = {k[3:-5]: nc.dram_tensor(k, a.shape, mb.dt.from_np(a.dtype), kind="ExternalInput").ap() for k, a in arrays.items()}
    out = nc.dram_tensor("out_dram", (N, D), F32, kind="ExternalOutput").ap()
    gps_two_layers(nc, t, out)
    return run_bass_kernel_spmd(nc, [arrays], core_ids=[0]).results[0]["out_dram"]
```

```python
from contextlib import ExitStack, contextmanager

import concourse.bass as bass
from concourse import mybir

F32, F16, I32 = mybir.dt.float32, mybir.dt.float16, mybir.dt.int32
ALU, ACT, AX = mybir.AluOpType, mybir.ActivationFunctionType, mybir.AxisListType
ds = bass.ds

N, D, E = 1250, 512, 41250
TP, NT = 125, 10
KT = D // 128
CHUNKS = [(0, 418), (418, 416), (834, 416)]
H, DH = 8, 64
FFN, FT = 1408, 11
NE, HID, CAP = 16, 256, 312
CT = CAP // 3
SLOTS = NE * CAP
A_SCALE, W_SCALE = 16.0, 64.0
UNSCALE = 1.0 / (A_SCALE * W_SCALE)
EPS = 1e-5
PASSES = [(0, 0), (0, 1), (1, 0)]

EC, ER = 128, E // 128
NCH = 384
SEG = 18
BATCH = 6
RING = 6
SHARE = 4
BASE = 4096.0
HS = N // 2
HW = 314
ONE_COL = 626
PHI_BANKS = [(6, 7), (0, 1)]
DEG_BANKS = [(3, 4, 5), (5, 6, 7)]
K_BANKS = (5, 6, 7, 2, 3)
Q_BANKS = [(2, 3), (0, 1)]
PER_SEG = SEG // BATCH + SEG - SEG // SHARE
EXACT = 2048


class Own:

    def __init__(self, eng, sem):
        self.eng, self.sem, self.base, self.k = eng, sem, 0, 0

    def mark(self, ins):
        ins.then_inc(self.sem, 1)
        self.k += 1
        return self.base + self.k

    def after(self, mark):
        self.eng.wait_ge(self.sem, mark)

    def step(self, ins):
        self.after(self.mark(ins))

    @contextmanager
    def loop(self, count, marks):
        base = self.base + self.k
        with self.eng.Fori(0, count) as i:
            self.base, self.k = i * marks + base, 0
            yield i
            assert self.k == marks, (self.k, marks)
        self.base, self.k = base + count * marks, 0


class Banks:

    def __init__(self, full, free):
        self.full, self.free, self.before, self.uses, self.count = full, free, {}, {}, [0] * 8

    def stage(self, name, uses):
        self.before[name], self.uses[name] = list(self.count), uses
        for b, n in uses.items():
            self.count[b] += n

    def acquire(self, eng, stage, b, k):
        eng.wait_ge(self.free[b], k + (self.before[stage][b] + 1))

    def filled(self, eng, stage, b, k):
        eng.wait_ge(self.full[b], k + (self.before[stage][b] + 1))

    def emptied(self, eng, stage, b, k):
        eng.wait_ge(self.free[b], k + (self.before[stage][b] + 2))

    def after_products(self, eng, stage):
        for b, n in self.uses[stage].items():
            eng.wait_ge(self.full[b], self.before[stage][b] + n)

    def after_evacuation(self, eng, stage):
        for b, n in self.uses[stage].items():
            eng.wait_ge(self.free[b], self.before[stage][b] + n + 1)


def peeled(step, count):
    return isinstance(step, int) and step < count


def gps_two_layers(nc, t, out):
    ctx = ExitStack()
    with ctx:
        top = nc.sbuf_base + 31
        top -= top % 32
        start = {}

        def region(name, size):
            nonlocal top
            start[name] = top
            top += size + (-size) % 32
            assert top <= nc.sbuf_usable_end, (name, top)

        def at(name, shape, dt, where, offset=0):
            return nc.alloc_sbuf_tensor_at(name, shape, dt, offset=start[where] + offset)

        for name, size in (("X", 20480), ("XN", 20480), ("XK", 20480), ("MT", 20480), ("XT", 20480),
                           ("AT", 50016), ("W", 24576), ("STG", 16384), ("BC", 12288), ("C", 7168)):
            region(name, size)
        X = at("X", [TP, NT, D], F32, "X")
        XN = at("XN", [TP, NT, D], F32, "XN")
        XK = at("XK", [TP, 2, NT, D], F16, "XK")
        XT = at("XT", [128, 2, KT, N], F16, "XT")
        MT = at("MT", [128, 2, KT, N], F16, "MT")
        AT = at("AT", [TP, 2, NT, N], F16, "AT")
        W = [at(f"W{s}", [128, 2, 2048], F16, "W", 8192 * s) for s in range(3)]
        STG = [at(f"STG{s}", [128, 2048], F32, "STG", 8192 * s) for s in range(2)]

        def rows(s):
            return W[s][:, :, :].rearrange("p a (k o) -> p a k o", k=KT)

        BC = at("BC", [TP, 6, D], F32, "BC")
        BQ, BV, BIAS, GAMMA, BETA, BPROJ = (BC[:, n, :] for n in range(6))
        QT = at("QT", [128, KT, N], F32, "XN")
        EK = at("EK", [TP, NT, D], F32, "AT")
        V = at("V", [TP, NT, KT, 130], F32, "AT", 20480)
        QW = at("QW", [TP, 2, 2, D], F32, "AT", 20480)
        CTX = at("CTX", [128, KT, 128], F32, "AT", 41280)
        KTOP = at("KTOP", [TP, D], F32, "AT", 43328)
        KDIAG = at("KDIAG", [128, KT, 128], F32, "AT", 45376)
        IDX = at("IDX", [128, 2, 3, EC], I32, "MT", 17408)
        IDXF = at("IDXF", [128, 2, 3, EC], F32, "MT")
        SRC, SRCV, DST, SRCB = (at(n, [128, NCH], F32, "MT", 5024 + 1536 * k) for k, n in enumerate(("SRC", "SRCV", "DST", "SRCB")))
        DREL = at("DREL", [128, 2, NCH], F16, "MT", 11168)
        I2 = at("I2", [TP, 2, 2, HW], I32, "MT")
        TMP = at("TMP", [128, 3, EC], F32, "MT", 12704)
        ONEHOT_D = at("ONEHOT_D", [128, SEG // BATCH, BATCH, 128], F16, "MT", 14240)
        ONEHOT_S = at("ONEHOT_S", [128, RING, 2 * HW], F16, "XN")
        AWAY = at("AWAY", [128, ONE_COL], F32, "XN", 7552)
        ACC = [at(f"ACC{n}", [TP, 2, 2 * HW], F32, "XN", 10080 + 5024 * n) for n in range(2)]
        ACCI = [at(f"ACCI{n}", [TP, 2, 2 * HW], I32, "XN", 10080 + 5024 * n) for n in range(2)]
        RANGE = at("RANGE", [128, 2, 3, NT, 3], F32, "AT", 47424)
        LH = at("LH", [TP, 2, 2 * HW], I32, "W", 16384)
        DG = at("DG", [128, N], F32, "XN")
        DIAG = at("DIAG", [TP, NT, TP], F32, "XN", 5024)
        MTMP = at("MTMP", [128, 2, 3, 418], F32, "XN", 10048)
        STEPS = at("STEPS", [1, NT, 32], F32, "AT", 48160)
        HT = at("HT", [128, 2, FT, N], F16, "XN")
        GATED = at("GATED", [128, 3, 418], F32, "XN", 55008)
        WD = at("WD", [128, 2, FT, D], F16, "W")
        GU = at("GU", [128, 2, 2, 2, KT * 128], F16, "BC")
        MAG = at("MAG", [128, 3, 512], F32, "AT", 25024)
        TERN = at("TERN", [128, 3, 512], F16, "AT", 31168)
        QUANT = at("QUANT", [128, 2, 3, 512], F32, "AT", 34240)
        XN2 = at("XN2", [TP, NT, D], F32, "AT", 25024)
        G = at("G", [128, KT, N], F32, "AT")
        QP = at("QP", [128, KT, N], F32, "AT", 20000)
        PTMP = at("PTMP", [128, 3, 418], F32, "AT", 40000)
        OW = at("OW", [TP, 2, D], F32, "AT", 45024)
        KEXP = at("KEXP", [TP, 2, 2, D], F32, "AT", 40032)
        QF = at("QF", [128, KT, N], F32, "XK", 320)
        KF = at("KF", [128, KT, N], F32, "MT", 352)
        KP = at("KP", [TP, NT, D], F32, "XK", 320)
        V1 = at("V1", [TP, NT, KT, 130], F32, "XN")
        PB = at("PB", [128, KT, 128], F32, "BC")
        KVB = at("KVB", [128, KT, 130], F32, "BC", 2048)
        IDNS = at("IDNS", [128, 128], F32, "BC", 4128)
        WG = at("WG", [128, KT * NE], F32, "BC", 4640)
        WGS = at("WGS", [128, 2, KT, NE], F16, "BC", 4896)
        GSTATS = at("GSTATS", [128, KT, 3, 6], F32, "BC", 5152)
        GMV = at("GMV", [128, KT, 2], F32, "BC", 5440)
        GCOL = at("GCOL", [128, 4, KT], F32, "BC", 5472)
        ZERO = at("ZERO", [128, 512], F32, "STG", 1536 * 4)
        XET = at("XET", [128, 2, 2, KT, CAP], F16, "XK")
        XE = at("XE", [CT, 2, 3, D], F32, "MT")
        HTMP = at("HTMP", [128, 2, 2 * CAP], F32, "AT")
        HH = at("HH", [128, 2, 2, 2, CAP], F16, "AT", 4992)
        EO = at("EO", [CT, 2, 3, D], F32, "AT", 9984)
        GATHER = at("GATHER", [TP, 4, D], F32, "AT", 22272)
        ROUTE = at("ROUTE", [TP, 12, NT, NE], F32, "AT", 30464)
        CARRY = at("CARRY", [TP, NT + 1, 2 * NE], F32, "AT", 38144)
        MASK = at("MASK", [TP, NT, 2, NE], F16, "AT", 39584)
        TOK = at("TOK", [TP, 12, NT], F32, "AT", 40224)
        SIDX = at("SIDX", [TP, 2, NT], I32, "AT", 40736)
        GIDX = at("GIDX", [TP, 2, NT], I32, "AT", 40832)
        EBASE = at("EBASE", [TP, 2, NE], F32, "AT", 40928)
        DUMP = at("DUMP", [TP, 2, NT], F32, "AT", 41088)
        slots_in = nc.dram_tensor("slots_in", [SLOTS + 2 * N, D], F32).ap()
        slots_out = nc.dram_tensor("slots_out", [SLOTS, D], F32).ap()
        counts_low_kept = nc.dram_tensor("counts_low_kept", [TP, NT, N], F16).ap()
        used = [0]

        def small(name, shape, dt):
            size = {F32: 4, F16: 2, I32: 4}[dt]
            for n in shape[1:]:
                size *= n
            x = at(name, shape, dt, "C", used[0])
            used[0] += size + (-size) % 32
            assert used[0] <= 7168, name
            return x

        IDN = small("IDN", [128, 128], F32)
        ONES = small("ONES", [128, 128], F32)
        ONES16 = small("ONES16", [128, 128], F16)
        TRI16 = small("TRI16", [128, 128], F16)
        IOTA_S = small("IOTA_S", [128, ONE_COL], F16)
        IOTA_D = small("IOTA_D", [128, 128], F16)
        STATS = small("STATS", [TP, NT, 6], F32)
        MV = small("MV", [TP, NT, 2], F32)
        STD = small("STD", [TP, NT], F32)
        RSTD = small("RSTD", [TP, NT], F32)
        SM8 = small("SM8", [TP, 2, 3, H], F32)
        COL = small("COL", [128, 7, KT], F32)
        BK, BL, G1, B1, KMAX, KBIAS, KREC = (COL[:, n, :] for n in range(7))
        VALUES = small("VALUES", [128, SEG], F32)
        FAR = small("FAR", [1, 2], F32)
        FARI = small("FARI", [1, 1], I32)
        DEG = small("DEG", [TP, NT], F32)
        RDEG = small("RDEG", [TP, NT], F32)
        THR = small("THR", [128, NT], F32)
        CID = small("CID", [128, 2, 3], F32)
        RED = small("RED", [128, 2, 3], F32)
        LOHI = small("LOHI", [128, 2, NT], F32)
        LOHIR = small("LOHIR", [128, 2, NT], F32)
        PLAN = small("PLAN", [1, 3, NT + 1], F32)
        MULT = small("MULT", [1, 32], F32)
        PLANI = small("PLANI", [1, 3, NT + 1], I32)
        EPSC = small("EPSC", [128, 1], F32)
        EPSA = small("EPSA", [128, 1], F32)
        EPSW = small("EPSW", [128, 1], F32)
        PS = ctx.enter_context(nc.psum_tensor("PS", [128, 8, 512], F32))
        B = [PS[:, b, :] for b in range(8)]

        def sem(name):
            return ctx.enter_context(nc.semaphore(name))

        bank_full = [sem(f"bank{b}_full") for b in range(8)]
        bank_free = [sem(f"bank{b}_free") for b in range(8)]
        bk = Banks(bank_full, bank_free)
        stages = [
            ("ln0_T", {b: 2 for b in range(5)}), ("mix_k", {b: 2 for b in K_BANKS}), ("mix_kmax", {4: 1}),
            ("edges", {0: 1, 1: 1}), ("mix_kbias", {7: 1}), ("mix_q", {2: 3, 3: 3, 0: 2, 1: 2}), ("mix_qT", {4: 5, 5: 5}),
            ("mix_v", {0: 5, 1: 5}), ("mix_ctx", {6: 1, 7: 1}), ("mix_out", {2: 5, 3: 5}),
            ("counts_T", {0: 10, 1: 10, 2: 10}),
            ("deg0", {b: 1 for b in DEG_BANKS[0]}), ("agg0", {b: 2 for b in range(6)}),
            ("scale0", {6: 2, 7: 1}), ("gnn0", {6: 5, 7: 5}),
            ("ln1_T", {b: 2 for b in range(5)}), ("ffn_scale", {6: 2 * (FT - 1), 7: FT - 1}), ("ffn", {b: FT for b in range(6)}),
            ("down", {6: 5, 7: 5}), ("ln2_T", {b: 2 for b in range(5)}),
            ("deg1", {b: 1 for b in DEG_BANKS[1]}), ("agg1", {b: 2 for b in range(6)}),
            ("gnn1", {b: 2 for b in range(6)}), ("qk1", {b: 4 for b in range(6)}), ("v1", {6: 5, 7: 5}),
            ("phi_q", {b: 2 for b in range(6)}), ("phi_k", {6: 3, 7: 3, 0: 2, 1: 2}), ("kv", {0: 1, 1: 1}), ("att", {3: 5, 5: 5}),
            ("att_T", {6: 5, 7: 5}), ("proj", {0: 5, 1: 5}), ("ln3_T", {b: 2 for b in range(5)}),
            ("gate", {4: 1}), ("places", {5: 2, 6: 2}), ("slots_T", {0: NE, 1: NE, 2: NE}), ("hidden", {3: NE, 4: NE}),
            ("expert", {5: NE, 6: NE, 7: NE}),
        ]
        for s in stages:
            bk.stage(*s)
        x_loaded = [sem(f"x_loaded{n}") for n in range(2)]
        small_loaded = sem("small_loaded")
        consts_made = sem("consts_made")
        staged = [sem(f"staged{s}") for s in range(2)]
        high_split = sem("high_split")
        weight_ready = sem("weight_ready")
        stored = sem("stored")
        dve_own, act_own, pool_own = sem("dve_own"), sem("act_own"), sem("pool_own")
        std_ready, xn_ready, xk_high, xk_low, xt_high = (
            sem("std_ready"), sem("xn_ready"), sem("xk_high"), sem("xk_low"), sem("xt_high"))
        var_ready = sem("var_ready")
        q_shifted, q_exp, q_soft = sem("q_shifted"), sem("q_exp"), sem("q_soft")
        k_seen, kdiag_ready, kbias_ready, k_shifted, k_exp = (
            sem(n) for n in ("k_seen", "kdiag_ready", "kbias_ready", "k_shifted", "k_exp"))
        edges_loaded, edges_float = sem("edges_loaded"), sem("edges_float")
        lohi_local, lohi_all, plan_ready = sem("lohi_local"), sem("lohi_all"), sem("plan_ready")
        onehot_ready, onehot_free, away_ready, act_onehot_ready = (
            sem(n) for n in ("onehot_ready", "onehot_free", "away_ready", "act_onehot_ready"))
        seg_int, lohi_ready, acc_added = sem("seg_int"), sem("lohi_ready"), sem("acc_added")
        counts_high, deg_ready, diag_ready = sem("counts_high"), sem("deg_ready"), sem("diag_ready")
        mean_high, mean_ready = sem("mean_high"), sem("mean_ready")
        beta_added, gnn_var, gnn_std = sem("beta_added"), sem("gnn_var"), sem("gnn_std")

        qkv = t["L1_mix_w_qkv"]
        units = [t["L0_mix_WkT"], t["L0_mix_WqT"], t["L0_mix_WvT"], t["L0_gnn_W_selfT"], t["L0_gnn_W_neighT"],
                 t["L1_gnn_W_lT"], t["L1_gnn_W_rT"], qkv[:, 0:D], qkv[:, D:2 * D], qkv[:, 2 * D:], t["L1_mix_w_proj"]]
        NU = len(units)
        unit_slot = [0, 1, 2, 0, 1, 0, 1, 2, 0, 1, 2]
        last_use = {3: "mix_k", 4: "mix_q", 5: "down", 6: "down", 7: "down", 8: "gnn1", 9: "gnn1", 10: "qk1"}

        def stage_slot(n):
            return n % 2 if n < 5 else (n + 1) % 2

        def staged_count(n):
            return 16 * sum(stage_slot(m) == stage_slot(n) for m in range(n + 1))

        def plan(eng, T):
            lo = eng.value_load(PLANI[0:1, 0, T:T + 1], min_val=0, max_val=ER)
            n = eng.value_load(PLANI[0:1, 1, T:T + 1], min_val=1, max_val=(ER + SEG) // SEG + 1)
            before = eng.value_load(PLANI[0:1, 2, T:T + 1], min_val=0, max_val=NT * ((ER + SEG) // SEG + 1))
            return lo, n, before

        ffn_staged = [sem(f"ffn_staged{n}") for n in range(2)]
        magnitude, ternary, quantised, ffn_high, ffn_low = (
            sem(n) for n in ("magnitude", "ternary", "quantised", "ffn_high", "ffn_low"))
        far_known, counts_float = sem("far_known"), sem("counts_float")
        hidden_high, counts_spilled, counts_back, wide_own = (
            sem(n) for n in ("hidden_high", "counts_spilled", "counts_back", "wide_own"))
        gnn1_var, gnn1_std, gnn1_done, phi_min, phi_exp, kmin, kexp, att_ready, bproj_added = (
            sem(n) for n in ("gnn1_var", "gnn1_std", "gnn1_done", "phi_min", "phi_exp", "kmin", "kexp", "att_ready", "bproj_added"))
        gather_rows = sem("gather_rows")
        route_loaded, route_consts, wg_high, wg_ready, gate_exp_in, gate_exp, masks_ready, places_ready = (
            sem(n) for n in ("route_loaded", "route_consts", "wg_high", "wg_ready", "gate_exp_in", "gate_exp", "masks_ready", "places_ready"))
        zero_made, zero_stored, scattered, slots_high, relu_high, relu_low = (
            sem(n) for n in ("zero_made", "zero_stored", "scattered", "slots_high", "relu_high", "relu_low"))
        slots_loaded = [sem(f"slots_loaded{n}") for n in range(2)]
        outs_stored = [sem(f"outs_stored{n}") for n in range(2)]
        gathered = [sem(f"gathered{n}") for n in range(4)]
        half_added, y_ready = sem("half_added"), sem("y_ready")

        prescaled, expert_prescaled = sem("prescaled"), sem("expert_prescaled")
        hidden_done = sem("hidden_done")

        def expert_staged(e, par):
            slot = (par + NU + 1) % 2
            return 16 * sum(stage_slot(m) == slot for m in range(NU)) + 32 * (e // 2 + 1)

        def scale_use(n, a):
            stage, n = ("scale0", 0) if peeled(n, 1) else ("ffn_scale", n - 1)
            return (stage, 7, n) if a == 1 else (stage, 6, n * 2 + a // 2)

        def counts_low(dve, v, T):
            for b in range(3):
                n = min(4, NT - 4 * b)
                dve.wait_ge(counts_high, 3 * T + b + 1)
                cols = slice(T * TP, (T + 1) * TP)
                v.tensor_tensor(AT[:, 1, 4 * b:4 * b + n, cols], B[b][:TP, 0:n * TP].rearrange("p (s d) -> p s d", s=n),
                                  AT[:, 0, 4 * b:4 * b + n, cols], ALU.subtract).then_inc(bank_free[b], 1)

        block = ctx.enter_context(nc.Block())

        @block.sync
        def _(sp):
            for n in range(2):
                sp.dma_start(X[:, 5 * n:5 * n + 5, :], t["x"].rearrange("(t p) d -> p t d", p=TP)[:, 5 * n:5 * n + 5, :])\
                  .then_inc(x_loaded[n], 16)
            def load_weight(n):
                sl = stage_slot(n)
                sp.dma_start(STG[sl][:, :].rearrange("p (k o) -> p k o", k=KT), units[n].rearrange("(k p) o -> p k o", p=128))\
                  .then_inc(staged[sl], 16)

            load_weight(0)
            for dst, name in ((BQ, "L0_mix_bq"), (BV, "L0_mix_bv"), (BIAS, "L0_gnn_bias"), (GAMMA, "L0_gnn_gamma"),
                              (BETA, "L0_gnn_beta"), (BPROJ, "L1_mix_b_proj")):
                sp.dma_start(dst, t[name].partition_broadcast(TP)).then_inc(small_loaded, 16)
            for dst, name in ((BK, "L0_mix_bkC"), (BL, "L1_gnn_b_lC"), (G1, "L1_gnn_gammaC"), (B1, "L1_gnn_betaC")):
                sp.dma_start(dst, t[name]).then_inc(small_loaded, 16)
            load_weight(1)
            sp.wait_ge(edges_loaded, 1)
            for a, name in enumerate(("src", "dst")):
                e = t[name]
                sp.dma_start(IDX[:, a, 0:2, :], e[0:256 * EC].rearrange("(g p e) -> p g e", p=128, e=EC)).then_inc(edges_loaded, 16)
                sp.dma_start(IDX[0:ER - 256, a, 2, :], e[256 * EC:ER * EC].rearrange("(p e) -> p e", e=EC)).then_inc(edges_loaded, 16)
                sp.dma_start(IDX[ER - 256:ER - 255, a, 2, 0:E - ER * EC], e[ER * EC:E].rearrange("(p e) -> p e", p=1))\
                    .then_inc(edges_loaded, 16)

            for n in (2, 3, 4):
                sp.wait_ge(weight_ready, n - 1)
                load_weight(n)
            wide = [t[x].rearrange("(k p) f -> p k f", p=128) for x in ("L0_ffn_w_gateT", "L0_ffn_w_upT")]
            for n in range(FT):
                if n == 2:
                    bk.after_evacuation(sp, "counts_T")
                    sp.dma_start(counts_low_kept, AT[:, 1, :, :]).then_inc(counts_spilled, 16)
                if n < 2:
                    sp.wait_ge(weight_ready, 4 + n)
                else:
                    sp.wait_ge(ternary, n - 1)
                st = STG[(n + 1) % 2]
                for a in range(2):
                    sp.dma_start(st[:, a * 512:(a + 1) * 512].rearrange("p (k f) -> p k f", k=KT), wide[a][:, :, n * 128:(n + 1) * 128])\
                      .then_inc(ffn_staged[n % 2], 16)
                sp.dma_start(st[:, 1024:1536], t["L0_ffn_w_downT"][n * 128:(n + 1) * 128, :]).then_inc(ffn_staged[n % 2], 16)
                if n == 3:
                    sp.wait_ge(zero_made, 1)
                    sp.dma_start(slots_in[0:SLOTS, :].rearrange("(p r) d -> p r d", p=128),
                                 ZERO[:, :].unsqueeze(1).to_broadcast([128, SLOTS // 128, D])).then_inc(zero_stored, 16)
            sp.wait_ge(zero_stored, 16)
            for n in (5, 6):
                sp.wait_ge(ternary, FT - 1 + n - 5)
                load_weight(n)
            bk.after_products(sp, "ffn")
            sp.dma_start(WG[:, :].rearrange("p (k e) -> p k e", k=KT), t["L1_ffn_w_gating"].rearrange("(k p) e -> p k e", p=128))\
                .then_inc(route_loaded, 16)
            sp.wait_ge(wide_own, 1)
            for h in range(H):
                p = slice(64 * (h % 2), 64 * (h % 2) + 64)
                sp.dma_start(PB[p, h // 2, p], t["L1_mix_proj_mat"][h, :, :]).then_inc(route_loaded, 16)
            bk.after_products(sp, "ln2_T")
            sp.wait_ge(xk_low, 2 * NT)
            far = sp.value_load(FARI[0:1, 0:1], min_val=0, max_val=1)
            with sp.If(far == 1):
                sp.dma_start(AT[:, 1, :, :], counts_low_kept).then_inc(counts_back, 16)
            for n in range(7, NU):
                sp.wait_ge(weight_ready, n - 1)
                load_weight(n)

            def load_expert(e, par):
                st = STG[(par + NU + 1) % 2]
                sp.wait_ge(weight_ready, e + (NU - 1))
                sp.dma_start(st[:, 0:1024].rearrange("p (k h) -> p k h", k=KT), t["L1_ffn_w1"][ds(e, 1), :, :].rearrange("a (k p) h -> p (a k) h", p=128))\
                  .then_inc(staged[(par + NU + 1) % 2], 16)
                sp.dma_start(st[:, 1024:2048].rearrange("p (k d) -> p k d", k=2), t["L1_ffn_w2"][ds(e, 1), :, :].rearrange("a (k p) d -> p (a k) d", p=128))\
                  .then_inc(staged[(par + NU + 1) % 2], 16)

            def load_slots(e, par):
                if not peeled(e, 2):
                    bk.filled(sp, "slots_T", 2, e - 2)
                sp.dma_start(XE[:, par, :, :], slots_in[ds(e * CAP, CAP), :].rearrange("(c p) d -> p c d", p=CT))\
                    .then_inc(slots_loaded[par], 16)

            def store_slots(e, par):
                bk.emptied(sp, "expert", 7, e)
                sp.dma_start(slots_out[ds(e * CAP, CAP), :].rearrange("(c p) d -> p c d", p=CT), EO[:, par, :, :])\
                    .then_inc(outs_stored[par], 16)

            for e in range(3):
                load_expert(e, e % 2)
            sp.wait_ge(scattered, 16 * 2 * NT)
            for par in range(2):
                load_slots(par, par)
            load_slots(2, 0)
            load_expert(3, 1)
            with sp.Fori(0, NE // 2 - 2) as i:
                for par in range(2):
                    load_slots(i * 2 + (par + 3), 1 - par)
                    load_expert(i * 2 + (par + 4), par)
                    store_slots(i * 2 + par, par)
            load_slots(NE - 1, 1)
            for e in range(NE - 4, NE):
                store_slots(e, e % 2)
            for i in range(NT):
                sp.wait_ge(y_ready, i + 1)
                sp.dma_start(out[i * TP:(i + 1) * TP, :], X[:, i, :]).then_inc(stored, 16)
            sp.wait_ge(stored, 16 * NT)

        @block.gpsimd
        def _(pool):
            g = nc.gpsimd
            own = Own(pool, pool_own)
            g.memset(IDX[:, :, 2, :], -1).then_inc(edges_loaded, 1)
            own.step(g.memset(IDN[:, :], 0.0))
            g.affine_select(out=IDN[:, :], in_=IDN[:, :], compare_op=ALU.not_equal, fill=1.0, base=0,
                            pattern=[[-1, 128]], channel_multiplier=1).then_inc(consts_made, 1)
            g.memset(ONES[:, :], 1.0).then_inc(consts_made, 1)
            g.memset(ONES16[:, :], 1.0).then_inc(consts_made, 1)
            pool.wait_ge(consts_made, 3)
            g.affine_select(out=TRI16[:, :], in_=ONES16[:, :], compare_op=ALU.is_gt, fill=0.0, base=0,
                            pattern=[[1, 128]], channel_multiplier=-1).then_inc(consts_made, 1)
            g.iota(IOTA_S[:, :], [[1, ONE_COL]], base=0, channel_multiplier=0, allow_small_or_imprecise_dtypes=True)\
             .then_inc(consts_made, 1)
            g.iota(IOTA_D[:, :], [[1, 128]], base=0, channel_multiplier=0, allow_small_or_imprecise_dtypes=True)\
             .then_inc(consts_made, 1)
            own.step(g.memset(EPSC[:, :], EPS))
            g.memset(EPSA[:, :], EPS / A_SCALE ** 2).then_inc(consts_made, 1)
            g.memset(EPSW[:, :], EPS * W_SCALE).then_inc(consts_made, 1)
            g.iota(MULT[:, :], [[SEG, 32]], base=0, channel_multiplier=0, allow_small_or_imprecise_dtypes=True).then_inc(consts_made, 1)
            g.iota(THR[:, :], [[TP, NT]], base=0, channel_multiplier=0, allow_small_or_imprecise_dtypes=True).then_inc(consts_made, 1)
            g.iota(CID[:, 0, :], [[-128, 3]], base=512, channel_multiplier=-1, allow_small_or_imprecise_dtypes=True)\
                .then_inc(consts_made, 1)
            g.iota(CID[:, 1, :], [[128, 3]], base=1, channel_multiplier=1, allow_small_or_imprecise_dtypes=True).then_inc(consts_made, 1)

            def prescale(n):
                st = STG[stage_slot(n)]
                pool.wait_ge(staged[stage_slot(n)], staged_count(n))
                g.tensor_scalar(st[:, :], st[:, :], W_SCALE, 1.0, ALU.mult, ALU.mult).then_inc(prescaled, 1)

            def split_low(n):
                prescale(n)
                pool.wait_ge(high_split, n + 1)
                w = W[unit_slot[n]]
                g.tensor_tensor(w[:, 1, :], STG[stage_slot(n)][:, :], w[:, 0, :], ALU.subtract)\
                 .then_inc(weight_ready, 1)

            def keep_low(done, XN):
                with pool.Fori(0, NT) as i:
                    pool.wait_ge(xk_high, i + (done + 1))
                    g.tensor_tensor(XK[:, 1, ds(i, 1), :], XN[:, ds(i, 1), :], XK[:, 0, ds(i, 1), :], ALU.subtract).then_inc(xk_low, 1)

            split_low(0)
            keep_low(0, XN)
            split_low(1)
            pool.wait_ge(kbias_ready, 1)
            with pool.Fori(0, NT) as i:
                g.tensor_tensor(EK[:, ds(i, 1), :], EK[:, ds(i, 1), :], KTOP[:, :].unsqueeze(1), ALU.add).then_inc(k_shifted, 1)
            for n in (2, 3, 4):
                split_low(n)
            pool.wait_ge(lohi_local, 1)
            g.partition_all_reduce(LOHIR[:, :, :].rearrange("p a t -> p (a t)"), LOHI[:, :, :].rearrange("p a t -> p (a t)"), 128,
                                   bass.bass_isa.ReduceOp.max).then_inc(lohi_all, 1)
            bk.after_evacuation(pool, "mix_out")
            with pool.Fori(0, NT) as i:
                g.tensor_tensor(X[:, ds(i, 1), :], X[:, ds(i, 1), :], BETA.unsqueeze(1), ALU.add).then_inc(beta_added, 1)
            pool.wait_ge(plan_ready, 1)
            pool.sem_inc(acc_added, 2)
            for T in range(NT):
                _, n, before = plan(pool, T)
                acc = ACCI[T % 2]
                if T >= 2:
                    bk.filled(pool, "counts_T", 2, T - 2)
                own.step(g.memset(acc[:, :, :], 0))
                with pool.Fori(0, n) as i:
                    pool.wait_ge(lohi_ready, before + i + 4)
                    pool.wait_ge(acc_added, before + i + 2)
                    g.tensor_tensor(acc[:, :, :], acc[:, :, :], LH[:, :, :], ALU.add).then_inc(acc_added, 1)
                pool.wait_ge(acc_added, before + n + 2)
                ones = acc[:, :, ONE_COL:ONE_COL + 1]
                own.step(g.tensor_tensor(ones[:, 0, :], ones[:, 0, :], ones[:, 1, :], ALU.add))
                g.tensor_copy(DEG[:, T:T + 1], ones[:, 0, :]).then_inc(deg_ready, 1)
                pool.wait_ge(deg_ready, T + 1)
                g.tensor_copy(ACC[T % 2][:, :, :], acc[:, :, :]).then_inc(counts_float, 1)

            g.memset(ZERO[:, :], 0.0).then_inc(zero_made, 1)

            def quantise(n, par):
                pool.wait_ge(ternary, n + 1)
                g.tensor_tensor(QUANT[:, par, :, :], TERN[:, :, :], QUANT[:, par, :, :], ALU.mult)\
                 .then_inc(quantised, 1)

            def quantised_low(n, par):
                pool.wait_ge(ffn_high, n * 2 + 2)
                own.mark(g.tensor_tensor(GU[:, par, :, 1, :], QUANT[:, par, 0:2, :], GU[:, par, :, 0, :], ALU.subtract))
                g.tensor_tensor(WD[:, 1, ds(n, 1), :], QUANT[:, par, 2:3, :], WD[:, 0, ds(n, 1), :], ALU.subtract).then_inc(ffn_low, 1)

            quantise(0, 0)
            quantise(1, 1)
            quantised_low(0, 0)
            with own.loop(4, 2) as i:
                for u in range(2):
                    quantised_low(i * 2 + (u + 1), 1 - u)
                    quantise(i * 2 + (u + 2), u)
            quantised_low(9, 1)
            quantise(10, 0)
            quantised_low(10, 0)

            bk.after_products(pool, "ffn")
            own.step(g.memset(IDNS[:, :], 0.0))
            own.mark(g.affine_select(out=IDNS[:, :], in_=IDNS[:, :], compare_op=ALU.not_equal, fill=A_SCALE * W_SCALE, base=0,
                                     pattern=[[-1, 128]], channel_multiplier=1))
            own.step(g.memset(KVB[:, :, :], 0.0))
            g.memset(PB[:, :, :], 0.0).then_inc(wide_own, 1)
            keep_low(NT, XN2)
            pool.wait_ge(xn_ready, 3 * NT)
            with pool.Fori(0, NT) as i:
                g.tensor_tensor(X[:, ds(i, 1), :], X[:, ds(i, 1), :], BPROJ.unsqueeze(1), ALU.add).then_inc(bproj_added, 1)
            for n in range(5, NU):
                split_low(n)
            bk.after_products(pool, "proj")
            g.iota(EBASE[:, 0, :], [[CAP, NE]], base=0, channel_multiplier=0, allow_small_or_imprecise_dtypes=True)\
                .then_inc(route_consts, 1)
            g.iota(EBASE[:, 1, :], [[-1, NE]], base=NE, channel_multiplier=0, allow_small_or_imprecise_dtypes=True)\
                .then_inc(route_consts, 1)
            g.iota(DUMP[:, :, :], [[1, 2], [2 * TP, NT]], base=SLOTS, channel_multiplier=2, allow_small_or_imprecise_dtypes=True)\
                .then_inc(route_consts, 1)

            def expert_low(e):
                pool.wait_ge(high_split, e + (NU + 1))
                g.tensor_tensor(W[e % 3][:, 1, :], STG[(e + NU + 1) % 2][:, :], W[e % 3][:, 0, :], ALU.subtract)\
                 .then_inc(weight_ready, 1)

            expert_low(0)
            expert_low(1)
            pool.wait_ge(zero_stored, 16)
            for c in range(2):
                pool.wait_ge(places_ready, c + 1)
                for i in range(NT):
                    g.indirect_dma_start(out=slots_in, out_offset=bass.IndirectOffsetOnAxis(ap=SIDX[:, c, i:i + 1], axis=0),
                                         in_=XN[:, i, :], in_offset=None).then_inc(scattered, 16)
            for e in range(2, NE):
                expert_low(e)
            pool.wait_ge(gather_rows, 2)
            for u in range(2):
                pool.wait_ge(outs_stored[u], 16 * (NE // 2))
            for n in range(2 * NT):
                if n >= 4:
                    pool.wait_ge(half_added if n % 2 == 0 else y_ready, (n - 4) // 2 + 1)
                g.indirect_dma_start(out=GATHER[:, n % 4, :], out_offset=None, in_=slots_out,
                                     in_offset=bass.IndirectOffsetOnAxis(ap=GIDX[:, n % 2, n // 2:n // 2 + 1], axis=0))\
                 .then_inc(gathered[n % 4], 16)

        @block.scalar
        def _(act):
            s = nc.scalar
            own = Own(act, act_own)

            def split_high(n):
                act.wait_ge(prescaled, n + 1)
                if n in last_use:
                    bk.after_products(act, last_use[n])
                s.activation(W[unit_slot[n]][:, 0, :], STG[stage_slot(n)][:, :], ACT.Copy).then_inc(high_split, 1)

            def std_of(n, half, ready):
                rows = slice(half * NT // 2, (half + 1) * NT // 2)
                s.activation(STD[:, rows], MV[:, rows, 1], ACT.Sqrt, bias=EPSA[:TP, :], scale=A_SCALE ** -2).then_inc(ready, 1)

            def keep_high(n, XN=XN):
                with act.Fori(0, NT // 2) as i:
                    act.wait_ge(xn_ready, i + n)
                    s.activation(XK[:, 0, ds(i + (n - 1) % NT, 1), :], XN[:, ds(i + (n - 1) % NT, 1), :], ACT.Copy).then_inc(xk_high, 1)

            def transposed_high(stage):
                with act.Fori(0, 2) as i:
                    for u in range(NT // 2):
                        bk.filled(act, stage, u, i)
                        s.activation(XT[:, 0, :, ds(i * (N // 2) + u * TP, TP)],
                                     B[u][:, 0:KT * TP].rearrange("p (k n) -> p k n", k=KT), ACT.Copy).then_inc(xt_high, 1)

            def stds(n):
                for half in range(2):
                    act.wait_ge(var_ready, 2 * n + half + 1)
                    std_of(n, half, std_ready)

            act.wait_ge(consts_made, 12)
            act.wait_ge(var_ready, 1)
            std_of(0, 0, std_ready)
            act.wait_ge(var_ready, 2)
            std_of(0, 1, std_ready)
            split_high(0)
            transposed_high("ln0_T")
            keep_high(1)
            keep_high(NT // 2 + 1)
            split_high(1)

            with act.Fori(0, 2) as i:
                for u, b in enumerate(K_BANKS):
                    act.wait_ge(k_seen, i * 5 + (u + 2))
                    s.activation(EK[:, ds(i * 5 + u, 1), :], B[b][:TP, :].unsqueeze(1), ACT.Copy, scale=UNSCALE).then_inc(bank_free[b], 1)
            act.wait_ge(edges_loaded, 97)
            s.activation(IDXF[:, :, :, :], IDX[:, :, :, :], ACT.Copy).then_inc(edges_float, 1)
            bk.filled(act, "mix_kbias", 7, 0)
            s.activation(KTOP[:, :], B[7][:TP, :], ACT.Copy).then_inc(kbias_ready, 1)
            act.wait_ge(kbias_ready, 1)
            act.sem_inc(bank_free[7], 1)
            bk.after_evacuation(act, "mix_k")

            def q_exps(i):
                for u in range(2):
                    act.wait_ge(q_shifted, i * 2 + (u + 1))
                    s.activation(QW[:, i % 2, u, :], QW[:, i % 2, u, :], ACT.Exp).then_inc(q_exp, 1)

            act.wait_ge(xk_low, NT)
            q_exps(0)
            for i in range(NT // 2):
                if i + 1 < NT // 2:
                    q_exps(i + 1)
                for u in range(2):
                    bk.filled(act, "mix_qT", 4 + u, i)
                    s.activation(QT[:, :, (2 * i + u) * TP:(2 * i + u + 1) * TP], B[4 + u][:, 0:KT * TP].rearrange("p (k n) -> p k n", k=KT), ACT.Copy)\
                     .then_inc(bank_free[4 + u], 1)
                if i == 0:
                    split_high(2)
            with act.Fori(0, NT) as i:
                act.wait_ge(k_shifted, i + 1)
                s.activation(EK[:, ds(i, 1), :], EK[:, ds(i, 1), :], ACT.Exp).then_inc(k_exp, 1)
            split_high(3)
            split_high(4)

            def counts_high_part(T):
                for b in range(3):
                    n = min(4, NT - 4 * b)
                    bk.filled(act, "counts_T", b, T)
                    s.activation(AT[:, 0, 4 * b:4 * b + n, T * TP:(T + 1) * TP], B[b][:TP, 0:n * TP].rearrange("p (s d) -> p s d", s=n),
                                 ACT.Copy).then_inc(counts_high, 1)

            def as_integers(f):
                act.wait_ge(onehot_free, f * SEG + RING)
                act.wait_ge(lohi_ready, f + 1)
                s.activation(I2[:, ds((f + 1) % 2, 1), :, :].rearrange("p a h c -> p (a h) c"),
                             PS[:TP, ds((f + 1) % 2 * 2 + 4, 2), 0:HW], ACT.Copy).then_inc(seg_int, 1)

            act.wait_ge(plan_ready, 1)
            act.sem_inc(act_onehot_ready, 1)
            bk.after_evacuation(act, "mix_out")
            for T in range(NT):
                lo, n, before = plan(act, T)
                with act.Fori(0, n) as i:
                    first = nc.s_assert_within(lo + i * SEG, 0, NCH - SEG,
                                               skip_runtime_bounds_check_because="the plan's last segment starts before the last chunk")
                    for j in range(SHARE - 1, SEG, SHARE):
                        act.wait_ge(onehot_free, (before + i) * SEG + (j + 1))
                        act.wait_ge(act_onehot_ready, (before + i) * (SEG // SHARE) + (j // SHARE + 1))
                        if j == SHARE - 1:
                            s.activation(VALUES[:, j:SEG], SRCV[:, ds(first + j, SEG - j)], ACT.Copy)
                        s.activation(AWAY[:, :], IOTA_S[:, :], ACT.Abs, bias=SRCB[:, ds(first + j, 1)], scale=SRCV[:, ds(first + j, 1)])\
                         .then_inc(away_ready, 1)
                        act.wait_ge(away_ready, (before + i) * (SEG // SHARE) + (j // SHARE + 1))
                        s.activation(ONEHOT_S[:, j % RING, 0:ONE_COL], AWAY[:, :], ACT.Relu, bias=VALUES[:, j:j + 1], scale=-1.0)\
                         .then_inc(act_onehot_ready, 1)
                        if j == SHARE - 1:
                            as_integers(before + i)
                if T:
                    counts_high_part(T - 1)
            as_integers(before + n)
            counts_high_part(NT - 1)

            def means_high(stage):
                with act.Fori(0, KT // 2) as i:
                    for u in range(2):
                        for c, (lo, n) in enumerate(CHUNKS):
                            bk.emptied(act, stage, 3 * u + c, i)
                            s.activation(MT[:, 0, ds(i * 2 + u, 1), lo:lo + n], MTMP[:, u, c:c + 1, 0:n], ACT.Copy)\
                             .then_inc(mean_high, 1)

            means_high("agg0")
            def magnitudes(n, par):
                if n:
                    act.wait_ge(ternary, n)
                act.wait_ge(ffn_staged[par], (n // 2 + 1) * 48)
                s.activation(MAG[:, :, :].rearrange("p a c -> p (a c)"), STG[(par + 1) % 2][:, 0:1536], ACT.Abs).then_inc(magnitude, 1)

            def scale_rows(n, par):
                for a in range(3):
                    b = (6, 7, 6)[a]
                    bk.filled(act, *scale_use(n, a))
                    if a == 0 and n >= 2:
                        act.wait_ge(ffn_low, n - 1)
                    s.activation(QUANT[:, par, a, :], B[b][:, :], ACT.Identity, bias=EPSW[:, :], scale=W_SCALE / 128)\
                     .then_inc(bank_free[b], 1)

            def quantised_high(n, par):
                act.wait_ge(quantised, n + 1)
                s.activation(GU[:, par, :, 0, :], QUANT[:, par, 0:2, :], ACT.Copy).then_inc(ffn_high, 1)
                s.activation(WD[:, 0, ds(n, 1), :], QUANT[:, par, 2:3, :], ACT.Copy).then_inc(ffn_high, 1)

            def gates(j):
                for c, (lo, n) in enumerate(CHUNKS):
                    bk.filled(act, "ffn", c, j)
                    if j:
                        act.wait_ge(hidden_done, j * 3 + (c + 1 - 3))
                    s.activation(GATED[:, c, 0:n], B[c][:, 0:n], ACT.Silu, scale=UNSCALE).then_inc(bank_free[c], 1)
                for c, (lo, n) in enumerate(CHUNKS):
                    bk.emptied(act, "ffn", 3 + c, j)
                    s.activation(HT[:, 0, ds(j, 1), lo:lo + n], GATED[:, c:c + 1, 0:n], ACT.Copy).then_inc(hidden_high, 1)

            act.wait_ge(counts_spilled, 16)
            bk.after_products(act, "agg0")
            magnitudes(0, 0)
            scale_rows(0, 0)
            magnitudes(1, 1)
            act.wait_ge(quantised, 1)
            s.activation(GU[:, 0, :, 0, :], QUANT[:, 0, 0:2, :], ACT.Copy).then_inc(ffn_high, 1)
            for half in range(2):
                act.wait_ge(gnn_var, half + 1)
                std_of(0, half, gnn_std)
                act.wait_ge(var_ready, 2 + half + 1)
                std_of(1, half, std_ready)
            bk.after_products(act, "gnn0")
            s.activation(WD[:, 0, 0:1, :], QUANT[:, 0, 2:3, :], ACT.Copy).then_inc(ffn_high, 1)
            scale_rows(1, 1)
            transposed_high("ln1_T")
            quantised_high(1, 1)
            magnitudes(2, 0)
            for j in range(FT):
                if j + 2 < FT:
                    scale_rows(j + 2, j % 2)
                if j + 3 < FT:
                    magnitudes(j + 3, (j + 1) % 2)
                gates(j)
                if j + 2 < FT:
                    quantised_high(j + 2, j % 2)

            stds(2)
            bk.after_products(act, "down")
            keep_high(2 * NT + 1, XN2)
            keep_high(2 * NT + NT // 2 + 1, XN2)
            transposed_high("ln2_T")
            split_high(5)
            split_high(6)
            means_high("agg1")
            split_high(7)
            for m in range(KT):
                for c, (lo, n) in enumerate(CHUNKS):
                    b = 3 * (m % 2) + c
                    bk.filled(act, "gnn1", b, m // 2)
                    s.activation(G[:, m, lo:lo + n], B[b][:, 0:n], ACT.Relu, bias=BL[:, m:m + 1], scale=UNSCALE).then_inc(bank_free[b], 1)
            split_high(8)
            split_high(9)
            act.wait_ge(gnn1_var, 1)
            s.activation(GCOL[:, 0, :], GMV[:, :, 1], ACT.Sqrt, bias=EPSC[:, :]).then_inc(gnn1_std, 1)
            for m in range(2 * KT):
                for c, (lo, n) in enumerate(CHUNKS):
                    b = 3 * (m % 2) + c
                    bk.filled(act, "qk1", b, m // 2)
                    s.activation((QF if m < KT else KF)[:, m % KT, lo:lo + n], B[b][:, 0:n], ACT.Copy, scale=UNSCALE)\
                     .then_inc(bank_free[b], 1)
            split_high(10)
            for m in range(KT):
                for c, (lo, n) in enumerate(CHUNKS):
                    act.wait_ge(phi_min, 3 * m + c + 1)
                    s.activation(PTMP[:, c, 0:n], PTMP[:, c, 0:n], ACT.Exp).then_inc(phi_exp, 1)
            for i in range(NT):
                act.wait_ge(kmin, i + 1)
                s.activation(KEXP[:, i // 2 % 2, i % 2, :], KEXP[:, i // 2 % 2, i % 2, :], ACT.Exp).then_inc(kexp, 1)

            def parts_T(stage, banks):
                with act.Fori(0, NT // 2) as i:
                    for u in range(2):
                        bk.filled(act, stage, banks[u], i)
                        s.activation(XT[:, 0, :, ds(i * (2 * TP) + u * TP, TP)],
                                     B[banks[u]][:, 0:KT * TP].rearrange("p (k n) -> p k n", k=KT), ACT.Copy,
                                     scale=A_SCALE).then_inc(xt_high, 1)

            parts_T("att_T", (6, 7))
            act.wait_ge(route_loaded, 16)
            s.activation(WGS[:, 0, :, :].rearrange("p k e -> p (k e)"), WG[:, :], ACT.Copy, scale=W_SCALE).then_inc(wg_high, 1)

            def expert_high(e):
                act.wait_ge(expert_prescaled, e + 1)
                if e < 3:
                    bk.after_products(act, "v1" if e < 2 else "proj")
                else:
                    bk.filled(act, "expert", 7, e - 3)
                s.activation(W[e % 3][:, 0, :], STG[(e + NU + 1) % 2][:, :], ACT.Copy).then_inc(high_split, 1)

            expert_high(0)
            expert_high(1)
            stds(3)
            transposed_high("ln3_T")
            act.wait_ge(gate_exp_in, 1)
            s.activation(ROUTE[:, 0, :, :], ROUTE[:, 0, :, :], ACT.Exp).then_inc(gate_exp, 1)
            expert_high(2)

            def slots_high_parts(e, par):
                for b in range(3):
                    bk.filled(act, "slots_T", b, e)
                    s.activation(XET[:, par, 0, :, b * CT:(b + 1) * CT], B[b][:, 0:KT * CT].rearrange("p (k n) -> p k n", k=KT),
                                 ACT.Copy).then_inc(slots_high, 1)

            def relus(e, par):
                for m in range(2):
                    bk.filled(act, "hidden", 3 + m, e)
                    s.activation(HTMP[:, par, m * CAP:(m + 1) * CAP], B[3 + m][:, 0:CAP], ACT.Relu, scale=UNSCALE * A_SCALE)\
                     .then_inc(bank_free[3 + m], 1)
                for m in range(2):
                    bk.emptied(act, "hidden", 3 + m, e)
                s.activation(HH[:, par, 0, :, :].rearrange("p m c -> p (m c)"), HTMP[:, par, :], ACT.Copy).then_inc(relu_high, 1)

            def first_out(e, par):
                bk.filled(act, "expert", 5, e)
                if e >= 2:
                    act.wait_ge(outs_stored[par], 16 * (e // 2))
                s.activation(EO[:, par, 0, :], B[5][:CT, :], ACT.Copy, scale=UNSCALE).then_inc(bank_free[5], 1)

            slots_high_parts(0, 0)
            relus(0, 0)
            slots_high_parts(1, 1)
            for e in range(NE):
                if e + 1 < NE:
                    relus(e + 1, (e + 1) % 2)
                if e + 2 < NE:
                    slots_high_parts(e + 2, e % 2)
                first_out(e, e % 2)
                if e + 3 < NE:
                    expert_high(e + 3)

        @block.tensor
        def _(pe):
            te = nc.tensor
            for b in range(8):
                pe.sem_inc(bank_free[b], 1)
            pe.wait_ge(consts_made, 12)

            def sum_products(dst, pairs):
                for n, (a, b) in enumerate(pairs):
                    last = te.matmul(dst, a, b, start=(n == 0), stop=(n == len(pairs) - 1))
                return last

            def normed_T(stage, done, XN=XN, tiles=range(NT)):
                for i in tiles:
                    pe.wait_ge(xn_ready, done + i + 1)
                    b = i % (NT // 2)
                    bk.acquire(pe, stage, b, i // (NT // 2))
                    for k in range(KT):
                        last = te.transpose(B[b][:, k * TP:(k + 1) * TP], XN[:, i, k * 128:(k + 1) * 128],
                                            IDN[:TP, :TP])
                    last.then_inc(bank_full[b], 1)

            def by_token(stage, banks, terms):
                per = len(banks)
                with pe.Fori(0, NT // per) as i:
                    for u in range(per):
                        bk.acquire(pe, stage, banks[u], i)
                        sum_products(B[banks[u]][:TP, :], [
                            (a[:, pa, k, ds(i * (per * TP) + u * TP, TP)], w[:, pw, k, :])
                            for a, w, kt in terms for k in range(kt) for pa, pw in PASSES
                        ]).then_inc(bank_full[banks[u]], 1)

            def by_feature(stage, banks, m, terms, use):
                for c, (lo, n) in enumerate(CHUNKS):
                    bk.acquire(pe, stage, banks[c], use)
                    sum_products(B[banks[c]][:, 0:n], [
                        (w[:, pw, k, m * 128:(m + 1) * 128], a[:, pa, k, lo:lo + n])
                        for a, w in terms for k in range(KT) for pw, pa in PASSES
                    ]).then_inc(bank_full[banks[c]], 1)

            normed_T("ln0_T", 0)
            bk.after_evacuation(pe, "ln0_T")
            pe.wait_ge(weight_ready, 1)
            by_token("mix_k", K_BANKS, [(XT, rows(0), KT)])
            pe.wait_ge(k_seen, NT + 1)
            bk.acquire(pe, "mix_kmax", 4, 0)
            for k in range(KT):
                last = te.transpose(B[4][:, k * TP:(k + 1) * TP], KTOP[:, k * 128:(k + 1) * 128], IDN[:TP, :TP])
            last.then_inc(bank_full[4], 1)
            pe.wait_ge(edges_float, 1)
            for a in range(2):
                bk.acquire(pe, "edges", a, 0)
                for gg in range(3):
                    last = te.transpose(B[a][:, gg * EC:(gg + 1) * EC], IDXF[:, a, gg, :], IDN[:, :])
                last.then_inc(bank_full[a], 1)
            pe.wait_ge(kdiag_ready, 1)
            bk.acquire(pe, "mix_kbias", 7, 0)
            te.matmul(B[7][:TP, :], ONES[:, :TP], KDIAG[:, :, :].rearrange("p k c -> p (k c)"), start=True, stop=True)\
                .then_inc(bank_full[7], 1)

            def q_pair(i):
                for u in range(2):
                    b = Q_BANKS[i % 2][u]
                    bk.acquire(pe, "mix_q", b, i // 2)
                    sum_products(B[b][:TP, :], [
                        (XT[:, pa, k, (2 * i + u) * TP:(2 * i + u + 1) * TP], rows(1)[:, pw, k, :])
                        for k in range(KT) for pa, pw in PASSES
                    ]).then_inc(bank_full[b], 1)

            pe.wait_ge(weight_ready, 2)
            q_pair(0)
            q_pair(1)
            for i in range(NT // 2):
                if i + 2 < NT // 2:
                    q_pair(i + 2)
                for u in range(2):
                    pe.wait_ge(q_soft, 2 * i + u + 1)
                    bk.acquire(pe, "mix_qT", 4 + u, i)
                    for k in range(KT):
                        last = te.transpose(B[4 + u][:, k * TP:(k + 1) * TP], QW[:, i % 2, u, k * 128:(k + 1) * 128], IDN[:TP, :TP])
                    last.then_inc(bank_full[4 + u], 1)
            pe.wait_ge(weight_ready, 3)
            by_token("mix_v", (0, 1), [(XT, rows(2), KT)])
            bk.after_evacuation(pe, "mix_v")
            pe.wait_ge(k_exp, NT)
            for b in (6, 7):
                bk.acquire(pe, "mix_ctx", b, 0)
                for m in (2 * (b - 6), 2 * (b - 6) + 1):
                    last = sum_products(B[b][:, m % 2 * 256:m % 2 * 256 + 130], [
                        (EK[:, i, m * 128:(m + 1) * 128], V[:, i, m, :]) for i in range(NT)])
                last.then_inc(bank_full[b], 1)
            bk.after_evacuation(pe, "mix_qT")
            bk.after_evacuation(pe, "mix_ctx")
            for i in range(NT):
                bk.acquire(pe, "mix_out", 2 + i % 2, i // 2)
                for m in range(KT):
                    last = te.matmul(B[2 + i % 2][:TP, m * 128:(m + 1) * 128], QT[:, m, i * TP:(i + 1) * TP],
                                     CTX[:, m, :], start=True, stop=True)
                last.then_inc(bank_full[2 + i % 2], 1)

            def counts_transposes(T):
                pe.wait_ge(counts_float, T + 1)
                for b in range(3):
                    bk.acquire(pe, "counts_T", b, T)
                    for j in range(min(4, NT - 4 * b)):
                        sb = 4 * b + j
                        last = te.transpose(B[b][:TP, j * TP:(j + 1) * TP], ACC[T % 2][:, sb // 5, sb % 5 * TP:(sb % 5 + 1) * TP],
                                            IDN[:TP, :TP])
                    last.then_inc(bank_full[b], 1)

            pe.wait_ge(plan_ready, 1)
            pe.sem_inc(onehot_free, RING)
            pe.sem_inc(seg_int, 1)
            bk.after_evacuation(pe, "mix_out")
            for T in range(NT):
                _, n, before = plan(pe, T)
                with pe.Fori(0, n) as i:
                    pe.wait_ge(seg_int, before + i + 1)
                    for j in range(SEG):
                        if j % SHARE == SHARE - 1:
                            pe.wait_ge(act_onehot_ready, (before + i) * (SEG // SHARE) + (j // SHARE + 2))
                        else:
                            pe.wait_ge(onehot_ready, (before + i) * PER_SEG + (j - j // SHARE + j // BATCH + 2))
                        for h in range(2):
                            last = te.matmul(PS[:, ds((before + i) % 2 * 2 + (4 + h), 1), 0:HW].rearrange("p a c -> p (a c)"),
                                             ONEHOT_D[:, j // BATCH, j % BATCH, :], ONEHOT_S[:, j % RING, h * HW:(h + 1) * HW],
                                             start=(j == 0), stop=(j == SEG - 1))
                        last.then_inc(onehot_free, 1)
                if T:
                    counts_transposes(T - 1)

            def degrees(stage, done):
                pe.wait_ge(diag_ready, done + 1)
                for b, (lo, n) in zip(DEG_BANKS[done], CHUNKS):
                    bk.acquire(pe, stage, b, 0)
                    te.matmul(B[b][:, 0:n], ONES[:TP, :], DIAG[:, :, :].rearrange("p a b -> p (a b)")[:, lo:lo + n], start=True,
                              stop=True).then_inc(bank_full[b], 1)

            def neighbours(stage):
                pe.wait_ge(far_known, 1)
                far = pe.value_load(FARI[0:1, 0:1], min_val=0, max_val=1)
                with pe.Fori(0, KT // 2) as i:
                    for u in range(2):
                        for c, (lo, n) in enumerate(CHUNKS):
                            bk.acquire(pe, stage, 3 * u + c, i)

                            def products(pa, pb, first, last):
                                for sb in range(NT):
                                    ins = te.matmul(B[3 * u + c][:, 0:n], XK[:, pa, sb, ds(i * 256 + 128 * u, 128)], AT[:, pb, sb, lo:lo + n],
                                                    start=first and sb == 0, stop=last and sb == NT - 1, skip_group_check=True)
                                return ins

                            products(0, 0, True, False)
                            with pe.If(far == 1):
                                if stage == "agg1":
                                    pe.wait_ge(counts_back, 16)
                                products(0, 1, False, False)
                            products(1, 0, False, True).then_inc(bank_full[3 * u + c], 1)

            degrees("deg0", 0)
            counts_transposes(NT - 1)
            bk.after_evacuation(pe, "counts_T")
            neighbours("agg0")
            pe.wait_ge(weight_ready, 5)
            pe.wait_ge(mean_ready, 3 * KT)
            def scale_sum(n, a):
                b = (6, 7, 6)[a]
                pe.wait_ge(magnitude, n + 1)
                bk.acquire(pe, *scale_use(n, a))
                te.matmul(B[b][:, :], ONES[:, :], MAG[:, a, :], start=True, stop=True).then_inc(bank_full[b], 1)

            def gate_up(j, par, ahead):
                pe.wait_ge(ffn_low, j + 1)
                first = peeled(j, 1)
                if ahead and not first:
                    scale_sum(j + 2, 0)
                    scale_sum(j + 2, 1)
                for a in range(2):
                    for c, (lo, n) in enumerate(CHUNKS):
                        b = 3 * a + c
                        bk.acquire(pe, "ffn", b, j)
                        sum_products(B[b][:, 0:n], [
                            (GU[:, par, a, pw, k * 128:(k + 1) * 128], XT[:, pa, k, lo:lo + n]) for k in range(KT) for pw, pa in PASSES
                        ]).then_inc(bank_full[b], 1)
                        if ahead and (first and a or not first and (a, c) == (0, 0)):
                            scale_sum(j + 2, c if first else 2)

            for a in range(3):
                scale_sum(0, a)
            by_token("gnn0", (6, 7), [(XT, rows(0), KT), (MT, rows(1), KT)])
            for a in range(3):
                scale_sum(1, a)
            normed_T("ln1_T", NT)
            bk.after_evacuation(pe, "ln1_T")
            gate_up(0, 0, True)
            gate_up(1, 1, True)
            with pe.Fori(0, 3) as i:
                for u in range(2):
                    gate_up(i * 2 + (u + 2), u, True)
            gate_up(8, 0, True)
            gate_up(9, 1, False)
            gate_up(10, 0, False)
            pe.wait_ge(hidden_done, 3 * FT)
            by_token("down", (6, 7), [(HT, WD, FT)])

            normed_T("ln2_T", 2 * NT, XN2, range(NT // 2))
            degrees("deg1", 1)
            normed_T("ln2_T", 2 * NT, XN2, range(NT // 2, NT))
            pe.wait_ge(xk_low, 2 * NT)
            neighbours("agg1")
            pe.wait_ge(weight_ready, 7)
            pe.wait_ge(mean_ready, 6 * KT)
            bk.after_evacuation(pe, "ln2_T")
            for m in range(KT):
                by_feature("gnn1", (0, 1, 2) if m % 2 == 0 else (3, 4, 5), m, [(MT, rows(0)), (XT, rows(1))], m // 2)
            for m in range(2 * KT):
                if m % KT == 0:
                    pe.wait_ge(weight_ready, 8 + m // KT)
                by_feature("qk1", (0, 1, 2) if m % 2 == 0 else (3, 4, 5), m % KT, [(XT, rows(2 if m < KT else 0))], m // 2)
            pe.wait_ge(weight_ready, 10)
            by_token("v1", (6, 7), [(XT, rows(1), KT)])
            pe.wait_ge(route_loaded, 16 * 9)
            bk.after_evacuation(pe, "qk1")
            for m in range(KT):
                for c, (lo, n) in enumerate(CHUNKS):
                    b = 3 * (m % 2) + c
                    bk.acquire(pe, "phi_q", b, m // 2)
                    te.matmul(B[b][:, 0:n], PB[:, m, :], QF[:, m, lo:lo + n], start=True, stop=True).then_inc(bank_full[b], 1)
            for i in range(NT):
                b = PHI_BANKS[i // 2 % 2][i % 2]
                bk.acquire(pe, "phi_k", b, i // 4)
                for m in range(KT):
                    last = te.matmul(B[b][:TP, m * 128:(m + 1) * 128], KF[:, m, i * TP:(i + 1) * TP], PB[:, m, :],
                                     start=True, stop=True)
                last.then_inc(bank_full[b], 1)
            bk.after_evacuation(pe, "v1")
            bk.after_evacuation(pe, "phi_k")
            for b in range(2):
                bk.acquire(pe, "kv", b, 0)
                for m in (2 * b, 2 * b + 1):
                    last = sum_products(B[b][:, m % 2 * 256:m % 2 * 256 + 130], [
                        (KP[:, i, m * 128:(m + 1) * 128], V1[:, i, m, :]) for i in range(NT)])
                last.then_inc(bank_full[b], 1)
            bk.after_evacuation(pe, "kv")
            bk.after_evacuation(pe, "phi_q")

            def att_transposes(i):
                pe.wait_ge(att_ready, i + 1)
                bk.acquire(pe, "att_T", 6 + i % 2, i // 2)
                for k in range(KT):
                    last = te.transpose(B[6 + i % 2][:, k * TP:(k + 1) * TP], OW[:, i % 2, k * 128:(k + 1) * 128], IDN[:TP, :TP])
                last.then_inc(bank_full[6 + i % 2], 1)

            for i in range(NT):
                b = 3 + 2 * (i % 2)
                bk.acquire(pe, "att", b, i // 2)
                for m in range(KT):
                    last = te.matmul(B[b - 1 + m // 2][:TP, m % 2 * 256:m % 2 * 256 + 130], QP[:, m, i * TP:(i + 1) * TP], KVB[:, m, :], start=True, stop=True)
                last.then_inc(bank_full[b], 1)
                if i:
                    att_transposes(i - 1)
            att_transposes(NT - 1)
            pe.wait_ge(weight_ready, NU)
            pe.wait_ge(gnn1_done, KT)
            bk.after_evacuation(pe, "att_T")
            for i in range(NT):
                b = i % 2
                cols = slice(i * TP, (i + 1) * TP)
                bk.acquire(pe, "proj", b, i // 2)
                for k in range(KT):
                    te.matmul(B[b][:TP, k * 128:(k + 1) * 128], G[:, k, cols], IDNS[:, :], start=(k == 0), stop=False,
                              skip_group_check=True)
                terms = [(k, pa, pw) for k in range(KT) for pa, pw in PASSES]
                for n, (k, pa, pw) in enumerate(terms):
                    last = te.matmul(B[b][:TP, :], XT[:, pa, k, cols], rows(2)[:, pw, k, :], start=False, stop=(n == len(terms) - 1),
                                     skip_group_check=True)
                last.then_inc(bank_full[b], 1)

            normed_T("ln3_T", 3 * NT)
            pe.wait_ge(wg_ready, 1)
            bk.after_evacuation(pe, "ln3_T")
            bk.acquire(pe, "gate", 4, 0)
            for i in range(NT):
                last = sum_products(B[4][:TP, i * NE:(i + 1) * NE], [
                    (XT[:, pa, k, i * TP:(i + 1) * TP], WGS[:, pw, k, :]) for k in range(KT) for pa, pw in PASSES])
            last.then_inc(bank_full[4], 1)
            for c in range(2):
                pe.wait_ge(masks_ready, c + 1)
                for b, lhs in ((6, ONES16), (5, TRI16)):
                    bk.acquire(pe, "places", b, c)
                    te.matmul(B[b][:TP, 0:NT * NE], lhs[:TP, :TP], MASK[:, :, c, :], start=True, stop=True).then_inc(bank_full[b], 1)

            def slots_transposes(e, par):
                pe.wait_ge(slots_loaded[par], (e // 2 + 1) * 16)
                for b in range(3):
                    bk.acquire(pe, "slots_T", b, e)
                    for k in range(KT):
                        last = te.transpose(B[b][:, k * CT:(k + 1) * CT], XE[:, par, b, k * 128:(k + 1) * 128], IDN[:CT, :CT])
                    last.then_inc(bank_full[b], 1)

            def hidden(e, par):
                pe.wait_ge(weight_ready, e + (NU + 1))
                for b in range(3):
                    bk.emptied(pe, "slots_T", b, e)
                w1 = W[e % 3][:, :, 0:1024].rearrange("p a (k h) -> p a k h", k=KT)
                for m in range(2):
                    bk.acquire(pe, "hidden", 3 + m, e)
                    sum_products(B[3 + m][:, 0:CAP], [
                        (w1[:, pw, k, m * 128:(m + 1) * 128], XET[:, par, pa, k, :]) for k in range(KT) for pw, pa in PASSES
                    ]).then_inc(bank_full[3 + m], 1)

            def expert_out(e, par):
                pe.wait_ge(relu_low, e + 1)
                w2 = W[e % 3][:, :, 1024:2048].rearrange("p a (k d) -> p a k d", k=2)
                for c in range(3):
                    bk.acquire(pe, "expert", 5 + c, e)
                    sum_products(B[5 + c][:CT, :], [
                        (HH[:, par, pa, k, c * CT:(c + 1) * CT], w2[:, pw, k, :]) for k in range(2) for pa, pw in PASSES
                    ]).then_inc(bank_full[5 + c], 1)

            slots_transposes(0, 0)
            hidden(0, 0)
            slots_transposes(1, 1)
            for e in range(NE):
                if e + 1 < NE:
                    hidden(e + 1, (e + 1) % 2)
                if e + 2 < NE:
                    slots_transposes(e + 2, e % 2)
                expert_out(e, e % 2)

        @block.vector
        def _(dve):
            v = nc.vector
            own = Own(dve, dve_own)

            def heads(x):
                return x.rearrange("p (h d) -> p h d", h=H)

            def stats(i, x):
                return v.bn_stats(STATS[:, i, :], x[:, i, :])

            def mean_var(half, ready):
                for i in range(half * NT // 2, (half + 1) * NT // 2):
                    last = v.bn_aggr(MV[:, i, :], STATS[:, i, :])
                    if i % (NT // 2) < NT // 2 - 1:
                        m = own.mark(last)
                last.then_inc(ready, 1)
                own.after(m)

            def norm(stage, n, evacuate=None, XN=XN):
                for half in range(2):
                    tiles = range(half * NT // 2, (half + 1) * NT // 2)
                    if evacuate:
                        added = evacuate(tiles[0])
                    for i in tiles:
                        if n == 0 and i % 5 == 0:
                            dve.wait_ge(x_loaded[half], 16)
                        if evacuate:
                            before = added
                            if i + 1 in tiles:
                                added = evacuate(i + 1)
                            before()
                        m = own.mark(stats(i, X))
                    own.after(m)
                    mean_var(half, var_ready)
                    dve.wait_ge(std_ready, 2 * n + half + 1)
                    own.step(v.reciprocal(RSTD[:, tiles[0]:tiles[-1] + 1], STD[:, tiles[0]:tiles[-1] + 1]))
                    with dve.Fori(0, NT // 2) as i:
                        tile = ds(i + tiles[0], 1)
                        v.tensor_scalar(XN[:, tile, :], X[:, tile, :], MV[:, tile, 0:1].rearrange("p a b -> p (a b)"), RSTD[:, tile],
                                        ALU.subtract, ALU.mult).then_inc(xn_ready, 1)
                if n != 2:
                    transposed_low(stage, n)

            def transposed_low(stage, n):
                with dve.Fori(0, 2) as i:
                    for u in range(NT // 2):
                        dve.wait_ge(xt_high, i * (NT // 2) + (NT * (n + (n == 3)) + u + 1))
                        cols = ds(i * (N // 2) + u * TP, TP)
                        v.scalar_tensor_tensor(XT[:, 1, :, cols], B[u][:, 0:KT * TP].rearrange("p (k n) -> p k n", k=KT),
                                               1.0, XT[:, 0, :, cols], ALU.mult, ALU.subtract).then_inc(bank_free[u], 1)

            def add_products(stage, b0):
                def evacuate(i):
                    b = b0 + i % 2
                    bk.filled(dve, stage, b, i // 2)
                    v.scalar_tensor_tensor(X[:, i, :], B[b][:TP, :], UNSCALE, X[:, i, :], ALU.mult, ALU.add).then_inc(bank_free[b], 1)
                    return lambda: bk.emptied(dve, stage, b, i // 2)
                return evacuate

            v.memset(KTOP[:, :], -3e38).then_inc(k_seen, 1)
            norm("ln0_T", 0)
            dve.wait_ge(small_loaded, 160)
            with dve.Fori(0, 2) as i:
                for u, b in enumerate(K_BANKS):
                    bk.filled(dve, "mix_k", b, i)
                    dve.wait_ge(k_seen, i * 5 + (u + 1))
                    v.tensor_tensor(KTOP[:, :], B[b][:TP, :], KTOP[:, :], ALU.max).then_inc(k_seen, 1)
            bk.filled(dve, "mix_kmax", 4, 0)
            own.step(v.tensor_reduce(KMAX, B[4][:, 0:KT * TP].rearrange("p (k n) -> p k n", k=KT), AX.X, ALU.max))
            v.scalar_tensor_tensor(KMAX, KMAX, UNSCALE, BK, ALU.mult, ALU.add).then_inc(bank_free[4], 1)
            bk.after_evacuation(dve, "mix_kmax")
            own.step(v.tensor_tensor(KBIAS, BK, KMAX, ALU.subtract))
            v.tensor_tensor(KDIAG[:, :, :], IDN[:, :].unsqueeze(1).to_broadcast([128, KT, 128]),
                            KBIAS.unsqueeze(2).to_broadcast([128, KT, 128]), ALU.mult).then_inc(kdiag_ready, 1)
            bk.filled(dve, "edges", 1, 0)
            v.tensor_copy(DST[:, :], B[1][:, 0:NCH]).then_inc(bank_free[1], 1)
            bk.filled(dve, "edges", 0, 0)
            own.mark(v.tensor_copy(SRC[:, :], B[0][:, 0:NCH]))
            v.tensor_scalar(SRCV[:, :], B[0][:, 0:NCH], float(HS), BASE - 1.0, ALU.is_ge, ALU.mult).then_inc(bank_free[0], 1)
            bk.after_evacuation(dve, "edges")
            own.step(v.tensor_scalar(SRCV[:, :], SRCV[:, :], 1.0, None, ALU.add))
            tmp = TMP[:, :, :].rearrange("p g e -> p (g e)")
            own.step(v.tensor_scalar(tmp, SRC[:, :], float(HS), float(HS), ALU.is_ge, ALU.mult))
            own.step(v.tensor_tensor(SRC[:, :], SRC[:, :], tmp, ALU.subtract))
            own.step(v.scalar_tensor_tensor(SRCB[:, :], SRC[:, :], -1.0, SRCV[:, :], ALU.mult, ALU.mult))

            def q_shift(i):
                qw = QW[:, i % 2, :, :]
                for u in range(2):
                    b = Q_BANKS[i % 2][u]
                    bk.filled(dve, "mix_q", b, i // 2)
                    if i >= 2:
                        bk.filled(dve, "mix_qT", 4 + u, i - 2)
                    v.scalar_tensor_tensor(qw[:, u, :], B[b][:TP, :], UNSCALE, BQ, ALU.mult, ALU.add).then_inc(bank_free[b], 1)
                for u in range(2):
                    bk.emptied(dve, "mix_q", Q_BANKS[i % 2][u], i // 2)
                    m = own.mark(v.tensor_reduce(SM8[:, u, 0, :], heads(qw[:, u, :]), AX.X, ALU.max))
                own.after(m)
                for u in range(2):
                    v.tensor_tensor(heads(qw[:, u, :]), heads(qw[:, u, :]), SM8[:, u, 0, :].unsqueeze(2).to_broadcast([TP, H, DH]),
                                    ALU.subtract).then_inc(q_shifted, 1)

            q_shift(0)
            for i in range(NT // 2):
                if i + 1 < NT // 2:
                    q_shift(i + 1)
                qw = QW[:, i % 2, :, :]
                for u in range(2):
                    dve.wait_ge(q_exp, i * 2 + (u + 1))
                    m = own.mark(v.tensor_reduce(SM8[:, u, 1, :], heads(qw[:, u, :]), AX.X, ALU.add))
                own.after(m)
                for u in range(2):
                    m = own.mark(v.reciprocal(SM8[:, u, 2, :], SM8[:, u, 1, :]))
                own.after(m)
                for u in range(2):
                    v.scalar_tensor_tensor(heads(qw[:, u, :]), heads(qw[:, u, :]), DH ** -0.5,
                                           SM8[:, u, 2, :].unsqueeze(2).to_broadcast([TP, H, DH]), ALU.mult, ALU.mult)\
                     .then_inc(q_soft, 1)
            own.mark(v.tensor_reduce(RED[:, 0, :], IDXF[:, 1, :, :], AX.X, ALU.max))
            own.step(v.tensor_scalar(TMP[:, :, :], IDXF[:, 1, :, :], 0.0, 2.0 * N, ALU.is_lt, ALU.mult))
            own.step(v.tensor_tensor(TMP[:, :, :], TMP[:, :, :], IDXF[:, 1, :, :], ALU.add))
            own.step(v.tensor_reduce(RED[:, 1, :], TMP[:, :, :], AX.X, ALU.min))
            thr = THR[:, :].unsqueeze(2).to_broadcast([128, NT, 3])

            def per_tile(x):
                return x.unsqueeze(1).to_broadcast([128, NT, 3])

            own.mark(v.scalar_tensor_tensor(RANGE[:, 0, 0, :, :], per_tile(RED[:, 0, :]), 0.5, thr, ALU.add, ALU.is_gt))
            own.step(v.scalar_tensor_tensor(RANGE[:, 0, 1, :, :], per_tile(RED[:, 1, :]), TP - 0.5, thr, ALU.subtract, ALU.is_lt))
            own.step(v.tensor_tensor(RANGE[:, 0, 2, :, :], RANGE[:, 0, 0, :, :], RANGE[:, 0, 1, :, :], ALU.mult))
            for a in range(2):
                m = own.mark(v.tensor_tensor(RANGE[:, 1, a, :, :], RANGE[:, 0, 2, :, :], per_tile(CID[:, a, :]), ALU.mult))
            own.after(m)
            v.tensor_reduce(LOHI[:, :, :], RANGE[:, 1, 0:2, :, :], AX.X, ALU.max).then_inc(lohi_local, 1)
            bk.after_products(dve, "mix_qT")
            own.step(v.memset(V[:, :, :, 128:130], 1.0))
            with dve.Fori(0, NT // 2) as i:
                for u in range(2):
                    bk.filled(dve, "mix_v", u, i)
                    v.scalar_tensor_tensor(V[:, ds(i * 2 + u, 1), :, 0:128].rearrange("p a k c -> p (a k) c"), B[u][:TP, :].rearrange("p (k c) -> p k c", k=KT),
                                           UNSCALE, BV.rearrange("p (k c) -> p k c", k=KT), ALU.mult, ALU.add).then_inc(bank_free[u], 1)
            dve.wait_ge(lohi_all, 1)
            own.mark(v.memset(PLAN[:, :, :], 0.0))
            own.step(v.tensor_scalar(LOHI[0:1, 0, :], LOHIR[0:1, 0, :], -1.0, 512.0, ALU.mult, ALU.add))
            own.step(v.tensor_scalar(PLAN[0:1, 0, 0:NT], LOHI[0:1, 0, :], float(ER), None, ALU.min))
            own.step(v.tensor_scalar(LOHI[0:1, 0, :], PLAN[0:1, 0, 0:NT], 1.0, None, ALU.add))
            own.step(v.tensor_tensor(LOHI[0:1, 1, :], LOHIR[0:1, 1, :], LOHI[0:1, 0, :], ALU.max))
            own.step(v.tensor_tensor(LOHI[0:1, 1, :], LOHI[0:1, 1, :], PLAN[0:1, 0, 0:NT], ALU.subtract))
            own.step(v.tensor_tensor(STEPS[:, :, :], LOHI[0:1, 1, :].unsqueeze(2).to_broadcast([1, NT, 32]),
                                     MULT[:, :].unsqueeze(1).to_broadcast([1, NT, 32]), ALU.is_gt))
            own.step(v.tensor_reduce(PLAN[0:1, 1, 0:NT], STEPS[:, :, :], AX.X, ALU.add))
            for T in range(NT):
                own.step(v.tensor_tensor(PLAN[0:1, 2, T + 1:T + 2], PLAN[0:1, 2, T:T + 1], PLAN[0:1, 1, T:T + 1], ALU.add))
            v.tensor_copy(PLANI[:, :, :], PLAN[:, :, :]).then_inc(plan_ready, 1)
            dve.wait_ge(plan_ready, 1)
            dve.sem_inc(lohi_ready, 2)

            own.step(v.memset(CTX[:, :, :], 0.0))
            bk.after_products(dve, "mix_ctx")
            contexts = PS[:, 6:8, :].rearrange("p b (a c) -> p (b a) c", a=2)
            own.step(v.reciprocal(KREC.unsqueeze(2), contexts[:, :, 128:129]))
            for hh in range(2):
                p = slice(64 * hh, 64 * hh + 64)
                v.tensor_tensor(CTX[p, :, p], contexts[p, :, p], KREC[p, :].unsqueeze(2).to_broadcast([64, KT, 64]), ALU.mult)\
                 .then_inc(bank_free[6 + hh], 1)
            with dve.Fori(0, NT // 2) as i:
                for u in range(2):
                    bk.filled(dve, "mix_out", 2 + u, i)
                    v.tensor_tensor(X[:, ds(i * 2 + u, 1), :], B[2 + u][:TP, :].rearrange("p (a d) -> p a d", a=1), X[:, ds(i * 2 + u, 1), :], ALU.add)\
                     .then_inc(bank_free[2 + u], 1)
            own.mark(v.memset(ONEHOT_S[:, :, ONE_COL:ONE_COL + 1], 1.0))
            own.step(v.memset(ONEHOT_S[:, :, ONE_COL + 1:2 * HW], 0.0))

            def unpack(f):
                dve.wait_ge(seg_int, f + 2)
                dve.wait_ge(acc_added, f + 1)
                both = I2[:, ds((f + 1) % 2, 1), :, :].rearrange("p a h c -> p (a h c)")
                v.tensor_scalar(LH[:, 0, :], both, int(BASE) - 1, None, ALU.bitwise_and)
                v.tensor_scalar(LH[:, 1, :], both, 12, None, ALU.logical_shift_right).then_inc(lohi_ready, 1)

            for T in range(NT):
                lo, n, before = plan(dve, T)
                own.step(v.tensor_scalar(DREL[:, T % 2, :], DST[:, :], -float(TP * T), None, ALU.add))
                with dve.Fori(0, n) as i:
                    first = nc.s_assert_within(lo + i * SEG, 0, NCH - SEG,
                                               skip_runtime_bounds_check_because="the plan's last segment starts before the last chunk")
                    for j in range(SEG):
                        if j % SHARE == SHARE - 1:
                            continue
                        dve.wait_ge(onehot_free, (before + i) * SEG + (j + 1))
                        if j % BATCH == 0:
                            v.tensor_tensor(ONEHOT_D[:, j // BATCH, :, :], IOTA_D[:, :].unsqueeze(1).to_broadcast([128, BATCH, 128]),
                                            DREL[:, T % 2, ds(first + j, BATCH)].unsqueeze(2).to_broadcast([128, BATCH, 128]), ALU.is_equal)\
                             .then_inc(onehot_ready, 1)
                        v.tensor_scalar(ONEHOT_S[:, j % RING, 0:ONE_COL], IOTA_S[:, :], SRC[:, ds(first + j, 1)],
                                        SRCV[:, ds(first + j, 1)], ALU.is_equal, ALU.mult).then_inc(onehot_ready, 1)
                        if j == SEG - 2:
                            unpack(before + i)
                if T >= 2:
                    counts_low(dve, v, T - 2)
            unpack(before + n)

            def degrees(stage, done):
                dve.wait_ge(deg_ready, NT)
                if done == 0:
                    own.step(v.tensor_scalar(DEG[:, :], DEG[:, :], 1.0, None, ALU.max))
                    own.step(v.reciprocal(RDEG[:, :], DEG[:, :]))
                v.tensor_tensor(DIAG[:, :, :], IDN[:TP, :TP].unsqueeze(1).to_broadcast([TP, NT, TP]),
                                RDEG[:, :].unsqueeze(2).to_broadcast([TP, NT, TP]), ALU.mult).then_inc(diag_ready, 1)
                if done == 0:
                    counts_low(dve, v, NT - 2)
                else:
                    transposed_low("ln2_T", 2)
                for b, (lo, n) in zip(DEG_BANKS[done], CHUNKS):
                    bk.filled(dve, stage, b, 0)
                    v.tensor_copy(DG[:, lo:lo + n], B[b][:, 0:n]).then_inc(bank_free[b], 1)
                bk.after_evacuation(dve, stage)
                if done == 0:
                    own.step(v.tensor_reduce(FAR[:, 0:1], DG[0:1, :], AX.X, ALU.min))
                    own.step(v.tensor_scalar(FAR[:, 1:2], FAR[:, 0:1], 1 / (EXACT + 0.5), None, ALU.is_lt))
                    v.tensor_copy(FARI[:, :], FAR[:, 1:2]).then_inc(far_known, 1)
                    counts_low(dve, v, NT - 1)

            def means(stage, done):
                with dve.Fori(0, KT // 2) as i:
                    for u in range(2):
                        for c, (lo, n) in enumerate(CHUNKS):
                            bk.filled(dve, stage, 3 * u + c, i)
                            v.tensor_tensor(MTMP[:, u, c, 0:n], B[3 * u + c][:, 0:n], DG[:, lo:lo + n], ALU.mult)\
                                .then_inc(bank_free[3 * u + c], 1)
                        for c, (lo, n) in enumerate(CHUNKS):
                            dve.wait_ge(mean_high, i * 6 + (3 * u + c + 1 + 3 * KT * done))
                            v.tensor_tensor(MT[:, 1, ds(i * 2 + u, 1), lo:lo + n], MTMP[:, u, c:c + 1, 0:n],
                                            MT[:, 0, ds(i * 2 + u, 1), lo:lo + n], ALU.subtract).then_inc(mean_ready, 1)

            degrees("deg0", 0)
            means("agg0", 0)
            def ternaries(n, par):
                w = STG[(par + 1) % 2][:, 0:1536].rearrange("p (a c) -> p a c", a=3)
                for a in (2, 1):
                    bk.emptied(dve, *scale_use(n, a))
                if not peeled(n, 1):
                    dve.wait_ge(quantised, n)
                own.mark(v.scalar_tensor_tensor(MAG[:, :, :], QUANT[:, par, :, :], 0.5 / W_SCALE, w, ALU.mult, ALU.is_lt))
                own.step(v.scalar_tensor_tensor(TERN[:, :, :], QUANT[:, par, :, :], -0.5 / W_SCALE, w, ALU.mult, ALU.is_gt))
                v.tensor_tensor(TERN[:, :, :], MAG[:, :, :], TERN[:, :, :], ALU.subtract).then_inc(ternary, 1)

            ternaries(0, 0)
            dve.wait_ge(beta_added, NT)
            for half in range(2):
                tiles = range(half * NT // 2, (half + 1) * NT // 2)
                for i in (*tiles, tiles[-1] + 1):
                    if i in tiles:
                        b = 6 + i % 2
                        bk.filled(dve, "gnn0", b, i // 2)
                        v.scalar_tensor_tensor(XN[:, i, :], B[b][:TP, :], UNSCALE, BIAS, ALU.mult, ALU.add).then_inc(bank_free[b], 1)
                    if i > tiles[0]:
                        bk.emptied(dve, "gnn0", 6 + (i - 1) % 2, (i - 1) // 2)
                        own.step(stats(i - 1, XN))
                        aggregated = v.bn_aggr(MV[:, i - 1, :], STATS[:, i - 1, :])
                        if i in tiles:
                            own.step(aggregated)
                        else:
                            aggregated.then_inc(gnn_var, 1)
                            dve.wait_ge(gnn_var, half + 1)
                        m = own.mark(v.scalar_tensor_tensor(XN[:, i - 1, :], XN[:, i - 1, :], MV[:, i - 1, 0:1], GAMMA, ALU.subtract, ALU.mult))
                dve.wait_ge(gnn_std, half + 1)
                own.step(v.reciprocal(RSTD[:, tiles[0]:tiles[-1] + 1], STD[:, tiles[0]:tiles[-1] + 1]))
                own.step(v.tensor_scalar(RSTD[:, tiles[0]:tiles[-1] + 1], RSTD[:, tiles[0]:tiles[-1] + 1], 1 / A_SCALE, None, ALU.mult))
                own.after(m)
                for i in tiles:
                    m = own.mark(v.scalar_tensor_tensor(X[:, i, :], XN[:, i, :], RSTD[:, i:i + 1], X[:, i, :], ALU.mult, ALU.add))
                own.after(m)
                for i in tiles:
                    m = own.mark(stats(i, X))
                own.after(m)
                mean_var(half, var_ready)
                dve.wait_ge(std_ready, 2 + half + 1)
                own.step(v.reciprocal(RSTD[:, tiles[0]:tiles[-1] + 1], STD[:, tiles[0]:tiles[-1] + 1]))
                for i in tiles:
                    v.tensor_scalar(XN[:, i, :], X[:, i, :], MV[:, i, 0:1], RSTD[:, i:i + 1], ALU.subtract, ALU.mult).then_inc(xn_ready, 1)
            transposed_low("ln1_T", 1)

            def hiddens(j):
                for c, (lo, n) in enumerate(CHUNKS):
                    bk.filled(dve, "ffn", 3 + c, j)
                    bk.emptied(dve, "ffn", c, j)
                    v.scalar_tensor_tensor(GATED[:, c, 0:n], B[3 + c][:, 0:n], UNSCALE * A_SCALE, GATED[:, c, 0:n], ALU.mult, ALU.mult)\
                     .then_inc(bank_free[3 + c], 1)
                for c, (lo, n) in enumerate(CHUNKS):
                    dve.wait_ge(hidden_high, j * 3 + (c + 1))
                    v.tensor_tensor(HT[:, 1, ds(j, 1), lo:lo + n], GATED[:, c:c + 1, 0:n], HT[:, 0, ds(j, 1), lo:lo + n], ALU.subtract)\
                     .then_inc(hidden_done, 1)

            ternaries(1, 1)
            with own.loop(4, 4) as i:
                for u in range(2):
                    ternaries(i * 2 + (u + 2), u)
                    hiddens(i * 2 + u)
            ternaries(10, 0)
            for j in (8, 9, 10):
                hiddens(j)
            norm("ln2_T", 2, add_products("down", 6), XN2)
            degrees("deg1", 1)
            dve.wait_ge(xk_low, 2 * NT)
            means("agg1", 1)

            for m in range(KT):
                for c, (lo, n) in enumerate(CHUNKS):
                    bk.emptied(dve, "gnn1", 3 * (m % 2) + c, m // 2)
                    mm = own.mark(v.bn_stats(GSTATS[:, m, c, :], G[:, m, lo:lo + n]))
            own.after(mm)
            for m in range(KT):
                ins = v.bn_aggr(GMV[:, m, :], GSTATS[:, m, :, :])
                if m < KT - 1:
                    mm = own.mark(ins)
                else:
                    ins.then_inc(gnn1_var, 1)
            dve.wait_ge(gnn1_var, 1)
            dve.wait_ge(gnn1_std, 1)
            own.step(v.reciprocal(GCOL[:, 1, :], GCOL[:, 0, :]))
            own.step(v.tensor_tensor(GCOL[:, 2, :], GCOL[:, 1, :], G1, ALU.mult))
            own.step(v.tensor_tensor(GCOL[:, 3, :], GMV[:, :, 0], GCOL[:, 2, :], ALU.mult))
            own.step(v.tensor_tensor(GCOL[:, 3, :], B1, GCOL[:, 3, :], ALU.subtract))
            for m in range(KT):
                v.tensor_scalar(G[:, m, :], G[:, m, :], GCOL[:, 2, m:m + 1], GCOL[:, 3, m:m + 1], ALU.mult, ALU.add).then_inc(gnn1_done, 1)
            own.step(v.memset(V1[:, :, :, 128:130], 1.0))
            with dve.Fori(0, NT // 2) as i:
                for u in range(2):
                    bk.filled(dve, "v1", 6 + u, i)
                    v.tensor_scalar(V1[:, ds(i * 2 + u, 1), :, 0:128].rearrange("p a k c -> p (a k) c"), B[6 + u][:TP, :].rearrange("p (k c) -> p k c", k=KT),
                                    UNSCALE, None, ALU.mult).then_inc(bank_free[6 + u], 1)
            for m in range(KT):
                for c, (lo, n) in enumerate(CHUNKS):
                    b = 3 * (m % 2) + c
                    bk.filled(dve, "phi_q", b, m // 2)
                    if m:
                        bk.emptied(dve, "phi_q", 3 * ((m - 1) % 2) + c, (m - 1) // 2)
                    v.tensor_scalar(PTMP[:, c, 0:n], B[b][:, 0:n], 0.0, None, ALU.min).then_inc(phi_min, 1)
                for c, (lo, n) in enumerate(CHUNKS):
                    b = 3 * (m % 2) + c
                    dve.wait_ge(phi_exp, 3 * m + c + 1)
                    v.scalar_tensor_tensor(QP[:, m, lo:lo + n], B[b][:, 0:n], 0.0, PTMP[:, c, 0:n], ALU.max, ALU.add)\
                        .then_inc(bank_free[b], 1)
            bk.after_products(dve, "phi_q")

            def phi_k_mins(i):
                for u in range(2):
                    b = PHI_BANKS[i % 2][u]
                    bk.filled(dve, "phi_k", b, i // 2)
                    if i >= 2:
                        bk.emptied(dve, "phi_k", b, i // 2 - 1)
                    v.tensor_scalar(KEXP[:, i % 2, u, :], B[b][:TP, :], 0.0, None, ALU.min).then_inc(kmin, 1)

            bk.after_evacuation(dve, "phi_q")
            phi_k_mins(0)
            for i in range(NT // 2):
                if i + 1 < NT // 2:
                    phi_k_mins(i + 1)
                for u in range(2):
                    b = PHI_BANKS[i % 2][u]
                    dve.wait_ge(kexp, i * 2 + (u + 1))
                    v.scalar_tensor_tensor(KP[:, i * 2 + u, :], B[b][:TP, :], 0.0, KEXP[:, i % 2, u, :], ALU.max, ALU.add)\
                        .then_inc(bank_free[b], 1)
            dve.wait_ge(wide_own, 1)
            bk.after_products(dve, "kv")
            products = PS[:, 0:2, :].rearrange("p b (a c) -> p (b a) c", a=2)
            for hh in range(2):
                p = slice(64 * hh, 64 * hh + 64)
                own.mark(v.tensor_copy(KVB[p, :, 128 + hh:129 + hh], products[p, :, 128:129]))
                v.tensor_copy(KVB[p, :, p], products[p, :, p]).then_inc(bank_free[hh], 1)
            bk.after_evacuation(dve, "phi_k")

            def expert_prescale(e, par):
                st = STG[(par + NU + 1) % 2]
                dve.wait_ge(staged[(par + NU + 1) % 2], expert_staged(e, par))
                v.tensor_scalar(st[:, :], st[:, :], W_SCALE, None, ALU.mult).then_inc(expert_prescaled, 1)

            def att_low(i):
                b, cols = 6 + i % 2, slice(i * TP, (i + 1) * TP)
                dve.wait_ge(xt_high, 3 * NT + i + 1)
                v.scalar_tensor_tensor(XT[:, 1, :, cols], B[b][:, 0:KT * TP].rearrange("p (k n) -> p k n", k=KT), A_SCALE,
                                       XT[:, 0, :, cols], ALU.mult, ALU.subtract).then_inc(bank_free[b], 1)

            for i in range(NT):
                if i >= 2:
                    att_low(i - 2)
                b = 3 + 2 * (i % 2)
                bk.filled(dve, "att", b, i // 2)
                both = PS[:TP, b - 1:b + 1, :].rearrange("p b (a c) -> p (b a) c", a=2)
                own.step(v.reciprocal(SM8[:, i % 2, 2, :].rearrange("p (m h) -> p m h", m=KT), both[:, :, 128:130]))
                if i >= 2:
                    bk.filled(dve, "att_T", 6 + i % 2, i // 2 - 1)
                v.tensor_tensor(OW[:, i % 2, :].rearrange("p (m h d) -> p m h d", m=KT, h=2), both[:, :, 0:128].rearrange("p m (h d) -> p m h d", h=2),
                                SM8[:, i % 2, 2, :].rearrange("p (m h) -> p m h", m=KT).unsqueeze(3).to_broadcast([TP, KT, 2, DH]),
                                ALU.mult).then_inc(att_ready, 1)
                dve.wait_ge(att_ready, i + 1)
                dve.sem_inc(bank_free[b], 1)
            att_low(NT - 2)
            att_low(NT - 1)
            expert_prescale(0, 0)
            expert_prescale(1, 1)
            dve.wait_ge(wg_high, 1)
            v.scalar_tensor_tensor(WGS[:, 1, :, :].rearrange("p k e -> p (k e)"), WG[:, :], W_SCALE, WGS[:, 0, :, :].rearrange("p k e -> p (k e)"),
                                   ALU.mult, ALU.subtract).then_inc(wg_ready, 1)
            dve.wait_ge(bproj_added, NT)
            norm("ln3_T", 3, add_products("proj", 0))

            R = [ROUTE[:, n, :, :] for n in range(12)]
            K = [TOK[:, n, :] for n in range(12)]

            def by_expert(x):
                return x.unsqueeze(2).to_broadcast([TP, NT, NE])

            def by_tokens(x):
                return x.unsqueeze(1).to_broadcast([TP, NT, NE])

            bk.filled(dve, "gate", 4, 0)
            v.tensor_scalar(R[0], B[4][:TP, 0:NT * NE].rearrange("p (t e) -> p t e", t=NT), UNSCALE, None, ALU.mult)\
                .then_inc(bank_free[4], 1)
            bk.after_evacuation(dve, "gate")
            own.step(v.tensor_reduce(K[0], R[0], AX.X, ALU.max))
            v.tensor_tensor(R[0], R[0], by_expert(K[0]), ALU.subtract).then_inc(gate_exp_in, 1)
            dve.wait_ge(gate_exp, 1)
            own.step(v.tensor_reduce(K[0], R[0], AX.X, ALU.add))
            own.step(v.reciprocal(K[1], K[0]))
            own.step(v.tensor_tensor(R[0], R[0], by_expert(K[1]), ALU.mult))
            dve.wait_ge(route_consts, 3)
            own.mark(v.memset(CARRY[:, 0, :], 0.0))
            for c in range(2):
                own.step(v.tensor_reduce(K[2 + c], R[c], AX.X, ALU.max))
                own.step(v.tensor_tensor(R[2], R[c], by_expert(K[2 + c]), ALU.is_equal))
                own.step(v.tensor_tensor(R[2], R[2], by_tokens(EBASE[:, 1, :]), ALU.mult))
                own.step(v.tensor_reduce(K[4], R[2], AX.X, ALU.max))
                own.step(v.tensor_tensor(R[3 + c], R[2], by_expert(K[4]), ALU.is_equal))
                v.tensor_copy(MASK[:, :, c, :], R[3 + c]).then_inc(masks_ready, 1)
                own.step(v.tensor_tensor(R[8], R[3 + c], by_tokens(EBASE[:, 0, :]), ALU.mult))
                own.step(v.tensor_reduce(K[6], R[8], AX.X, ALU.add))
                if c == 0:
                    own.step(v.tensor_tensor(R[2], R[0], R[3], ALU.mult))
                    own.step(v.tensor_tensor(R[1], R[0], R[2], ALU.subtract))
                mine = slice(c * NE, (c + 1) * NE)
                bk.filled(dve, "places", 6, c)
                own.step(v.tensor_copy(CARRY[:, 1, mine], B[6][:TP, 0:NE]))
                for i in range(1, NT):
                    ins = v.tensor_tensor(CARRY[:, i + 1, mine], B[6][:TP, i * NE:(i + 1) * NE], CARRY[:, i, mine], ALU.add)
                    if i < NT - 1:
                        own.step(ins)
                    else:
                        ins.then_inc(bank_free[6], 1)
                bk.emptied(dve, "places", 6, c)
                if c == 0:
                    own.mark(v.tensor_scalar(CARRY[:, NT, mine], CARRY[:, NT, mine], float(CAP), None, ALU.min))
                bk.filled(dve, "places", 5, c)
                within = B[5][:TP, 0:NT * NE].rearrange("p (t e) -> p t e", t=NT)
                v.tensor_tensor(R[5 + c], within, CARRY[:, 0:NT, mine], ALU.add).then_inc(bank_free[5], 1)
                bk.emptied(dve, "places", 5, c)
                if c == 1:
                    own.step(v.tensor_tensor(R[6], R[6], by_tokens(CARRY[:, NT, 0:NE]), ALU.add))
                own.step(v.tensor_tensor(R[7], R[5 + c], R[3 + c], ALU.mult))
                own.step(v.tensor_reduce(K[5], R[7], AX.X, ALU.add))
                own.mark(v.tensor_tensor(K[6], K[6], K[5], ALU.add))
                own.step(v.tensor_scalar(K[10 + c], K[5], float(CAP), None, ALU.is_lt))
                own.step(v.tensor_tensor(K[9], K[6], DUMP[:, c, :], ALU.subtract))
                own.step(v.tensor_tensor(K[9], K[9], K[10 + c], ALU.mult))
                own.step(v.tensor_tensor(K[9], K[9], DUMP[:, c, :], ALU.add))
                v.tensor_copy(SIDX[:, c, :], K[9]).then_inc(places_ready, 1)
                own.step(v.tensor_tensor(K[8], K[6], K[10 + c], ALU.mult))
                v.tensor_copy(GIDX[:, c, :], K[8]).then_inc(gather_rows, 1)
            own.step(v.tensor_tensor(K[4], K[2], K[3], ALU.add))
            own.step(v.tensor_scalar(K[4], K[4], 1e-9, None, ALU.add))
            own.step(v.reciprocal(K[4], K[4]))
            for c in range(2):
                own.step(v.tensor_tensor(K[2 + c], K[2 + c], K[4], ALU.mult))
                own.step(v.tensor_tensor(K[2 + c], K[2 + c], K[10 + c], ALU.mult))

            def slots_low(e, par):
                for b in range(3):
                    dve.wait_ge(slots_high, e * 3 + (b + 1))
                    cols = slice(b * CT, (b + 1) * CT)
                    v.scalar_tensor_tensor(XET[:, par, 1, :, cols], B[b][:, 0:KT * CT].rearrange("p (k n) -> p k n", k=KT), 1.0,
                                           XET[:, par, 0, :, cols], ALU.mult, ALU.subtract).then_inc(bank_free[b], 1)

            def relu_lows(e, par):
                dve.wait_ge(relu_high, e + 1)
                v.tensor_tensor(HH[:, par, 1, :, :].rearrange("p m c -> p (m c)"), HTMP[:, par, :], HH[:, par, 0, :, :].rearrange("p m c -> p (m c)"),
                                ALU.subtract).then_inc(relu_low, 1)

            def outs(e, par):
                if e >= 2:
                    dve.wait_ge(outs_stored[par], 16 * (e // 2))
                for c in (1, 2):
                    bk.filled(dve, "expert", 5 + c, e)
                    if c == 2:
                        bk.emptied(dve, "expert", 5, e)
                    v.tensor_scalar(EO[:, par, c, :], B[5 + c][:CT, :], UNSCALE, None, ALU.mult).then_inc(bank_free[5 + c], 1)

            expert_prescale(2, 0)
            slots_low(0, 0)
            relu_lows(0, 0)
            slots_low(1, 1)
            for e in range(NE):
                if e + 1 < NE:
                    relu_lows(e + 1, (e + 1) % 2)
                if e + 2 < NE:
                    slots_low(e + 2, e % 2)
                outs(e, e % 2)
                if e + 3 < NE:
                    expert_prescale(e + 3, (e + 1) % 2)
            for i in range(NT):
                for c in range(2):
                    n = 2 * i + c
                    dve.wait_ge(gathered[n % 4], 16 * (n // 4 + 1))
                    if c:
                        dve.wait_ge(half_added, i + 1)
                    v.scalar_tensor_tensor(X[:, i, :], GATHER[:, n % 4, :], K[2 + c][:, i:i + 1], X[:, i, :], ALU.mult, ALU.add)\
                     .then_inc(y_ready if c else half_added, 1)


def arrange(inputs):
    import numpy as np

    put = {}
    for name, a in inputs.items():
        a = np.asarray(a)
        if name in ("L0_mix_Wq", "L0_mix_Wk", "L0_mix_Wv", "L0_gnn_W_self", "L0_gnn_W_neigh", "L0_ffn_w_gate",
                    "L0_ffn_w_up", "L0_ffn_w_down", "L1_gnn_W_l", "L1_gnn_W_r"):
            put[name + "T"] = np.ascontiguousarray(a.T)
        elif name in ("L0_mix_bk", "L1_gnn_b_l", "L1_gnn_gamma", "L1_gnn_beta"):
            put[name + "C"] = np.ascontiguousarray(a.reshape(KT, 128).T)
        else:
            put[name] = np.ascontiguousarray(a)
    return put


def kernel(**inputs):
    import concourse.bacc as bacc
    from concourse import mybir as mb
    from concourse.bass_utils import run_bass_kernel_spmd

    nc = bacc.Bacc("TRN2", target_bir_lowering=False, num_devices=1)
    arrays = {f"in_{k}_dram": a for k, a in arrange(inputs).items()}
    t = {k[3:-5]: nc.dram_tensor(k, a.shape, mb.dt.from_np(a.dtype), kind="ExternalInput").ap() for k, a in arrays.items()}
    out = nc.dram_tensor("out_dram", (N, D), F32, kind="ExternalOutput").ap()
    gps_two_layers(nc, t, out)
    return run_bass_kernel_spmd(nc, [arrays], core_ids=[0]).results[0]["out_dram"]
```
